# Optimizing a Trainium2 kernel written in Bass

```python
import numpy as np
import jax
import jax.numpy as jnp

def _softmax(x, axis=-1):
    return jax.nn.softmax(x, axis=axis)

def _gelu(x):
    return jax.nn.gelu(x, approximate=True)

def _silu(x):
    return jax.nn.silu(x)

def _sigmoid(x):
    return jax.nn.sigmoid(x)

def _layernorm(x, axis=-1, eps=1e-05):
    m = jnp.mean(x, axis=axis, keepdims=True)
    v = jnp.var(x, axis=axis, keepdims=True)
    return (x - m) / jnp.sqrt(v + eps)

def _scatter_add(tgt, idx, src, axis=0):
    return tgt.at[idx].add(src)

def _segment_sum(src, seg, n):
    return jax.ops.segment_sum(src, seg, n)
kernel_name = 'mk_sandwich_d1_jaxref_r8_119b2f'

def setup_inputs(seed: int=0):
    np.random.seed(seed)
    _w = jnp.asarray

    def _L0_attn_setup():
        import jax, jax.numpy as jnp
        import numpy as np
        B, L, D = (2, 256, 128)
        H, HD = (16, 64)
        LD = 32
        key = jax.random.key(seed)
        ks = jax.random.split(key, 6)
        s = lambda fan_in: 1.0 / np.sqrt(fan_in)
        x_bld = jax.random.normal(ks[0], (B, L, D), dtype=jnp.float32)
        Wq = jax.random.normal(ks[1], (D, H, HD), dtype=jnp.float32) * s(D)
        Wkv_down = jax.random.normal(ks[2], (D, LD), dtype=jnp.float32) * s(D)
        Wk_up = jax.random.normal(ks[3], (LD, H, HD), dtype=jnp.float32) * s(LD)
        Wv_up = jax.random.normal(ks[4], (LD, H, HD), dtype=jnp.float32) * s(LD)
        Wout = jax.random.normal(ks[5], (H, HD, D), dtype=jnp.float32) * s(H * HD)
        return {'x_bld': x_bld, 'Wq': Wq, 'Wkv_down': Wkv_down, 'Wk_up': Wk_up, 'Wv_up': Wv_up, 'Wout': Wout}
    _L0_attn_in = _L0_attn_setup()

    def _L0_ffn_setup():
        import jax, jax.numpy as jnp
        import numpy as np
        import math
        B, T, D, H, E, TOPK, CAPF = (4, 256, 128, 16, 8, 2, 2.0)
        HD = D // H

        def layernorm(x, g, b, eps=1e-05):
            m = jnp.mean(x, -1, keepdims=True)
            v = jnp.mean(jnp.square(x - m), -1, keepdims=True)
            return (x - m) * jax.lax.rsqrt(v + eps) * g + b

        def block_forward(x, ln1_g, ln1_b, Wqkv, Wproj, ln2_g, ln2_b, Wgate, W1, b1, W2, b2):
            Bb, Tt, d = x.shape
            hd = HD
            half = hd // 2
            h = layernorm(x, ln1_g, ln1_b)
            qkv = (h @ Wqkv).reshape(Bb, Tt, H, 3 * hd)
            q, k, v = (qkv[..., :hd], qkv[..., hd:2 * hd], qkv[..., 2 * hd:])
            inv_freq = 1.0 / 10000.0 ** (jnp.arange(0, hd, 2, dtype=jnp.float32) / hd)
            ang = jnp.arange(Tt, dtype=jnp.float32)[:, None] * inv_freq
            sin = jnp.sin(ang)[None, :, None, :].astype(x.dtype)
            cos = jnp.cos(ang)[None, :, None, :].astype(x.dtype)

            def rope(t):
                t1, t2 = (t[..., :half], t[..., half:])
                return jnp.concatenate([t1 * cos - t2 * sin, t1 * sin + t2 * cos], -1)
            q, k = (rope(q), rope(k))
            scores = jnp.einsum('bqhd,bkhd->bhqk', q, k) / math.sqrt(hd)
            causal = jnp.tril(jnp.ones((Tt, Tt), dtype=bool))
            scores = jnp.where(causal, scores, jnp.asarray(-1000000000.0, scores.dtype))
            probs = jax.nn.softmax(scores, axis=-1)
            attn = jnp.einsum('bhqk,bkhd->bqhd', probs, v).reshape(Bb, Tt, d) @ Wproj
            x = x + attn
            h2 = layernorm(x, ln2_g, ln2_b)
            flat = h2.reshape(-1, d)
            N = flat.shape[0]
            capacity = int(math.ceil(CAPF * N / E))
            gates = jax.nn.softmax((flat @ Wgate).astype(jnp.float32), -1).astype(flat.dtype)
            _, top_inds = jax.lax.top_k(gates, TOPK)
            mask = jnp.zeros((N, E), dtype=bool).at[jnp.arange(N)[:, None], top_inds].set(True)
            pos = jnp.cumsum(mask.astype(jnp.int32), axis=0) * mask - 1
            keep = (pos < capacity) & mask
            t_flat = jnp.repeat(jnp.arange(N), TOPK)
            e_flat = top_inds.reshape(-1)
            p = pos[t_flat, e_flat]
            kp = keep[t_flat, e_flat]
            p_eff = jnp.where(kp, p, capacity)
            exp_in = jnp.zeros((E, capacity, d), flat.dtype).at[e_flat, p_eff].set(flat[t_flat], mode='drop')
            hmid = jax.nn.gelu(jnp.einsum('ecd,edf->ecf', exp_in, W1) + b1[:, None, :], approximate=False)
            exp_out = jnp.einsum('ecf,efd->ecd', hmid, W2) + b2[:, None, :]
            gate = gates[t_flat, e_flat] * kp.astype(flat.dtype)
            p_g = jnp.minimum(p_eff, capacity - 1)
            moe = jnp.zeros((N, d), flat.dtype).at[t_flat].add(exp_out[e_flat, p_g] * gate[:, None])
            return x + moe.reshape(Bb, Tt, d)
        key = jax.random.key(seed)
        ks = jax.random.split(key, 8)
        s = 0.02
        return {'x': jax.random.normal(ks[0], (B, T, D), jnp.float32), 'ln1_g': jnp.ones((D,), jnp.float32), 'ln1_b': jnp.zeros((D,), jnp.float32), 'Wqkv': jax.random.normal(ks[1], (D, 3 * D), jnp.float32) * s, 'Wproj': jax.random.normal(ks[2], (D, D), jnp.float32) * s, 'ln2_g': jnp.ones((D,), jnp.float32), 'ln2_b': jnp.zeros((D,), jnp.float32), 'Wgate': jax.random.normal(ks[3], (D, E), jnp.float32) * s, 'W1': jax.random.normal(ks[4], (E, D, 4 * D), jnp.float32) * s, 'b1': jnp.zeros((E, 4 * D), jnp.float32), 'W2': jax.random.normal(ks[5], (E, 4 * D, D), jnp.float32) * s, 'b2': jnp.zeros((E, D), jnp.float32)}
    _L0_ffn_in = _L0_ffn_setup()
    _d = {'L0_attn_x_bld': _L0_attn_in['x_bld'], 'L0_attn_Wq': _L0_attn_in['Wq'], 'L0_attn_Wkv_down': _L0_attn_in['Wkv_down'], 'L0_attn_Wk_up': _L0_attn_in['Wk_up'], 'L0_attn_Wv_up': _L0_attn_in['Wv_up'], 'L0_attn_Wout': _L0_attn_in['Wout'], 'L0_ffn_ln1_g': _L0_ffn_in['ln1_g'], 'L0_ffn_ln1_b': _L0_ffn_in['ln1_b'], 'L0_ffn_Wqkv': _L0_ffn_in['Wqkv'], 'L0_ffn_Wproj': _L0_ffn_in['Wproj'], 'L0_ffn_ln2_g': _L0_ffn_in['ln2_g'], 'L0_ffn_ln2_b': _L0_ffn_in['ln2_b'], 'L0_ffn_Wgate': _L0_ffn_in['Wgate'], 'L0_ffn_W1': _L0_ffn_in['W1'], 'L0_ffn_b1': _L0_ffn_in['b1'], 'L0_ffn_W2': _L0_ffn_in['W2'], 'L0_ffn_b2': _L0_ffn_in['b2']}
    _x0 = _d['L0_attn_x_bld']
    _d['L0_attn_x_bld'] = jax.random.normal(jax.random.fold_in(jax.random.key(seed), 1), (4, 1024, 128), dtype=_x0.dtype)
    del _x0
    return _d

def reference(L0_attn_x_bld, L0_attn_Wq, L0_attn_Wkv_down, L0_attn_Wk_up, L0_attn_Wv_up, L0_attn_Wout, L0_ffn_ln1_g, L0_ffn_ln1_b, L0_ffn_Wqkv, L0_ffn_Wproj, L0_ffn_ln2_g, L0_ffn_ln2_b, L0_ffn_Wgate, L0_ffn_W1, L0_ffn_b1, L0_ffn_W2, L0_ffn_b2):

    def _L0_attn_ref(x_bld, Wq, Wkv_down, Wk_up, Wv_up, Wout):
        import jax, jax.numpy as jnp
        import numpy as np
        B, L, D = (2, 256, 128)
        H, HD = (16, 64)
        LD = 32
        q_blhd = jnp.einsum('bld,dhk->blhk', x_bld, Wq)
        latent_bll = jnp.einsum('bld,dc->blc', x_bld, Wkv_down)
        k_blhd = jnp.einsum('blc,chk->blhk', latent_bll, Wk_up)
        v_blhd = jnp.einsum('blc,chk->blhk', latent_bll, Wv_up)
        attn = jnp.einsum('bqhd,bkhd->bhqk', q_blhd, k_blhd) / jnp.sqrt(jnp.asarray(HD, dtype=x_bld.dtype))
        l = x_bld.shape[1]
        mask = (jnp.arange(l)[None, :] <= jnp.arange(l)[:, None])[None, None]
        neg_inf = jnp.finfo(attn.dtype).min
        attn = jax.nn.softmax(jnp.where(mask, attn, neg_inf), axis=-1)
        y_blhd = jnp.einsum('bhqk,bkhd->bqhd', attn, v_blhd)
        return jnp.einsum('bqhd,hdo->bqo', y_blhd, Wout)

    def _L0_ffn_ref(x, ln1_g, ln1_b, Wqkv, Wproj, ln2_g, ln2_b, Wgate, W1, b1, W2, b2):
        import jax, jax.numpy as jnp
        import numpy as np
        import math
        B, T, D, H, E, TOPK, CAPF = (4, 256, 128, 16, 8, 2, 2.0)
        HD = D // H

        def layernorm(x, g, b, eps=1e-05):
            m = jnp.mean(x, -1, keepdims=True)
            v = jnp.mean(jnp.square(x - m), -1, keepdims=True)
            return (x - m) * jax.lax.rsqrt(v + eps) * g + b

        def block_forward(x, ln1_g, ln1_b, Wqkv, Wproj, ln2_g, ln2_b, Wgate, W1, b1, W2, b2):
            Bb, Tt, d = x.shape
            hd = HD
            half = hd // 2
            h = layernorm(x, ln1_g, ln1_b)
            qkv = (h @ Wqkv).reshape(Bb, Tt, H, 3 * hd)
            q, k, v = (qkv[..., :hd], qkv[..., hd:2 * hd], qkv[..., 2 * hd:])
            inv_freq = 1.0 / 10000.0 ** (jnp.arange(0, hd, 2, dtype=jnp.float32) / hd)
            ang = jnp.arange(Tt, dtype=jnp.float32)[:, None] * inv_freq
            sin = jnp.sin(ang)[None, :, None, :].astype(x.dtype)
            cos = jnp.cos(ang)[None, :, None, :].astype(x.dtype)

            def rope(t):
                t1, t2 = (t[..., :half], t[..., half:])
                return jnp.concatenate([t1 * cos - t2 * sin, t1 * sin + t2 * cos], -1)
            q, k = (rope(q), rope(k))
            scores = jnp.einsum('bqhd,bkhd->bhqk', q, k) / math.sqrt(hd)
            causal = jnp.tril(jnp.ones((Tt, Tt), dtype=bool))
            scores = jnp.where(causal, scores, jnp.asarray(-1000000000.0, scores.dtype))
            probs = jax.nn.softmax(scores, axis=-1)
            attn = jnp.einsum('bhqk,bkhd->bqhd', probs, v).reshape(Bb, Tt, d) @ Wproj
            x = x + attn
            h2 = layernorm(x, ln2_g, ln2_b)
            flat = h2.reshape(-1, d)
            N = flat.shape[0]
            capacity = int(math.ceil(CAPF * N / E))
            gates = jax.nn.softmax((flat @ Wgate).astype(jnp.float32), -1).astype(flat.dtype)
            _, top_inds = jax.lax.top_k(gates, TOPK)
            mask = jnp.zeros((N, E), dtype=bool).at[jnp.arange(N)[:, None], top_inds].set(True)
            pos = jnp.cumsum(mask.astype(jnp.int32), axis=0) * mask - 1
            keep = (pos < capacity) & mask
            t_flat = jnp.repeat(jnp.arange(N), TOPK)
            e_flat = top_inds.reshape(-1)
            p = pos[t_flat, e_flat]
            kp = keep[t_flat, e_flat]
            p_eff = jnp.where(kp, p, capacity)
            exp_in = jnp.zeros((E, capacity, d), flat.dtype).at[e_flat, p_eff].set(flat[t_flat], mode='drop')
            hmid = jax.nn.gelu(jnp.einsum('ecd,edf->ecf', exp_in, W1) + b1[:, None, :], approximate=False)
            exp_out = jnp.einsum('ecf,efd->ecd', hmid, W2) + b2[:, None, :]
            gate = gates[t_flat, e_flat] * kp.astype(flat.dtype)
            p_g = jnp.minimum(p_eff, capacity - 1)
            moe = jnp.zeros((N, d), flat.dtype).at[t_flat].add(exp_out[e_flat, p_g] * gate[:, None])
            return x + moe.reshape(Bb, Tt, d)
        return block_forward(x, ln1_g, ln1_b, Wqkv, Wproj, ln2_g, ln2_b, Wgate, W1, b1, W2, b2)
    x = L0_attn_x_bld
    x = x + _layernorm(_L0_attn_ref(_layernorm(x, axis=-1), L0_attn_Wq, L0_attn_Wkv_down, L0_attn_Wk_up, L0_attn_Wv_up, L0_attn_Wout), axis=-1)
    x = x + _layernorm(_L0_ffn_ref(_layernorm(x, axis=-1), L0_ffn_ln1_g, L0_ffn_ln1_b, L0_ffn_Wqkv, L0_ffn_Wproj, L0_ffn_ln2_g, L0_ffn_ln2_b, L0_ffn_Wgate, L0_ffn_W1, L0_ffn_b1, L0_ffn_W2, L0_ffn_b2), axis=-1)
    return x

_drawn_inputs = setup_inputs


def setup_inputs(seed=0):
    import zlib

    import numpy as np

    out = dict(_drawn_inputs(seed))
    spreads = {'L0_ffn_ln1_g': (1.0, 0.6),
     'L0_ffn_ln1_b': (0.0, 0.8),
     'L0_ffn_ln2_g': (1.0, 0.6),
     'L0_ffn_ln2_b': (0.0, 0.8),
     'L0_ffn_b1': (0.0, 0.8),
     'L0_ffn_b2': (0.0, 2.0)}
    factors = {'L0_ffn_Wqkv': 8.0,
     'L0_ffn_Wproj': 8.0,
     'L0_ffn_Wgate': 6.259,
     'L0_ffn_W1': 8.0,
     'L0_ffn_W2': 8.0}
    for name, (base, spread) in spreads.items():
        noise = np.random.default_rng([zlib.crc32(name.encode()), seed]).standard_normal(out[name].shape)
        drawn = base * np.exp(spread * noise) if base else spread * noise
        out[name] = jnp.asarray(drawn.astype(out[name].dtype))
    for name, factor in factors.items():
        out[name] = (out[name] * factor).astype(out[name].dtype)
    return out
```

```python
from contextlib import ExitStack

import concourse.bass as bass
from concourse import mybir

F32 = mybir.dt.float32
F32R = mybir.dt.float32r
BF16 = mybir.dt.bfloat16
U32 = mybir.dt.uint32
ALU = mybir.AluOpType
ACT = mybir.ActivationFunctionType
AX = mybir.AxisListType

P = 128
BANK = 512
BATCH, SEQ, DIM = 4, 1024, 128
TOK = BATCH * SEQ
BLOCKS = TOK // P
SB = SEQ // P
CHUNKS = SEQ // BANK
CB = BANK // P
HEADS, LATENT, KDIM = 16, 32, 64
GROUP = 4
GROUPS = HEADS // GROUP
SLOTS = BATCH * GROUPS
HD2 = DIM // HEADS
QKV = 3 * HD2
EXPERTS, HIDDEN, TOPK = 8, 512, 2
CAPACITY = 2 * TOK // EXPERTS
EPS = 1e-5
MASKED = -2.0 ** 126
STACK = 96
ROWS = STACK + 2
RING = 4
UNITS = 12 * GROUP
M_ITEMS = 24
M_PASS = 4 * (M_ITEMS + 2) + 2


class Tally:

    def __init__(self, sem, start=0, per=0):
        self.sem, self.start, self.per = sem, start, per
        self.base, self.n = start, 0

    def turn(self, i):
        self.base, self.n = self.start + i * self.per, 0

    def next(self, k=1):
        self.n += k
        return self.base + self.n


def key_blocks(c):
    return [(kb, max(0, kb - CB * c) * P) for kb in range(CB * (c + 1))]


def max_items():
    short = [((h, h + 1), qb) for qb in range(CB) for h in (0, 2)]
    long = [((h,), qb) for qb in range(CB, SB) for h in range(GROUP)]
    return short + long


def pass_steps(layer, last):
    quads = [(c, kb, off) for c in range(CHUNKS) for kb, off in key_blocks(c)]
    steps, after = [], []

    def finish(g, c):
        if layer.sums:
            return [(g, "inverse", (c, m), None) for m in range(CB)] + [(g, "scale", c, None)]
        return [(g, "turn", c, None)]

    for g in range(GROUPS):
        next_max = not (last and g == GROUPS - 1)
        items, done = max_items() if next_max else [], 0
        places = 2 * (len(quads) - 1) - 1
        for n, quad in enumerate(quads):
            for h in range(GROUP):
                steps.append((g, "score", (quad, h), n))
                if h % 2:
                    place = 2 * n + h // 2 + 1
                    want = min(len(items), -(-place * len(items) // places))
                    for item in items[done:want]:
                        steps.append((g, "max", item, None))
                        steps += [after.pop(0)] if after else []
                    done = want
                    if not next_max and after:
                        steps.append(after.pop(0))
                    if next_max and place == places + 1:
                        steps.append((g, "max rows", None, None))
                        if layer.queries and not (last and g >= 1):
                            steps.append((g, "queries", None, None))
                if h == 2 and n:
                    steps.append((g, "values", quads[n - 1], n - 1))
                if h == 3 and n:
                    if layer.sums:
                        steps.append((g, "sums", quads[n - 1], n - 1))
                    if quads[n - 1][0] != quad[0]:
                        steps.append((g, "drain", quads[n - 1][0], None))
                        after = after + finish(g, quads[n - 1][0])
        steps.append((g, "values", quads[-1], len(quads) - 1))
        if layer.sums:
            steps.append((g, "sums", quads[-1], len(quads) - 1))
        steps.append((g, "drain", CHUNKS - 1, None))
        steps += after
        after = finish(g, CHUNKS - 1)
    steps += after
    if layer.queries:
        steps += [(g, "project", half, None) for half in range(2)]
    return steps


TILED = ("queries", "max", "max rows", "turn", "project")


class Layer:

    def __init__(self, name, scale, sums, v_width, q_dmas, sem):
        self.scale, self.sums, self.turns, self.v_width, self.q_dmas = scale, sums, not sums, v_width, q_dmas
        self.queries = sums
        self.ahead = 3 if self.queries else 2
        self.pass_tiles = sum(kind in TILED for _, kind, _, _ in pass_steps(self, False))
        self.last_tiles = sum(kind in TILED for _, kind, _, _ in pass_steps(self, True))
        self.first_tiles = M_ITEMS + 1 + (3 if sums else 0)
        self.tile_ready = sem(f"{name}_tile_ready")
        self.tile_done = sem(f"{name}_tile_done")
        self.scores_ready = sem(f"{name}_scores_ready")
        self.probs_ready = sem(f"{name}_probs_ready")
        self.quad_done = sem(f"{name}_quad_done")
        self.inverse_ready = sem(f"{name}_inverse_ready")
        self.inverted = sem(f"{name}_inverted")
        self.chunk_free = sem(f"{name}_chunk_free")
        self.high_ready = sem(f"{name}_high_ready")
        self.masked = sem(f"{name}_masked")
        self.max_turn = sem(f"{name}_max_turn")
        self.mask_turn = sem(f"{name}_mask_turn")
        self.parts_ready = sem(f"{name}_parts_ready")
        self.stack_in = [sem(f"{name}_stack_in{r}") for r in range(RING)]
        self.max_in = [sem(f"{name}_max_in{r}") for r in range(RING)]


def build(nc, t, dump=None):
    with ExitStack() as ctx:
        tensors = {}

        def sb(name, shape, dt=F32, scope=ctx):
            tensors[name] = scope.enter_context(nc.sbuf_tensor(name, shape, dt))
            return tensors[name]

        def sem(name):
            return ctx.enter_context(nc.semaphore(name))

        tile_ps = ctx.enter_context(nc.psum_tensor("tile_ps", [P, 2, 2 * BANK], F32))
        score_ps = ctx.enter_context(nc.psum_tensor("score_ps", [P, 2, BANK], F32))
        value_ps = ctx.enter_context(nc.psum_tensor("value_ps", [P, BANK], F32))
        sum_ps = ctx.enter_context(nc.psum_tensor("sum_ps", [P, BANK], F32))

        ident = sb("ident", [P, P])
        late_key = sb("late_key", [P, SEQ], BF16)
        upper = sb("upper", [P, P])
        ones = sb("ones", [P, P])
        affine1 = sb("affine1", [P, 2, DIM])

        x = sb("x", [P, BLOCKS, DIM])
        xn = sb("xn", [P, BLOCKS, DIM])
        stats = sb("stats", [P, BLOCKS, 6])
        mean_var = sb("mean_var", [P, BLOCKS, 2])
        var_eps = sb("var_eps", [P, BLOCKS])
        root = sb("root", [P, BLOCKS])
        rstd = sb("rstd", [P, BLOCKS])
        newton = sb("newton", [P, BLOCKS])

        both = ctx.enter_context(ExitStack())
        q_stack = sb("q_stack", [P, RING, GROUP, SEQ], F32R, both)
        probs = sb("probs", [P, 8, BANK], F32, both)
        sum_inv = sb("sum_inv", [P, BANK], F32, both)
        turn_inv = sb("turn_inv", [P, CB, GROUP, 1], F32, both)
        max_of = sb("max_of", [P, GROUP, SB], F32, both)
        max_parts = sb("max_parts", [P, 4, GROUP * SB], F32R, both)
        max_rows = sb("max_rows", [P, P], F32R, both)

        with ExitStack() as first:
            xn_t = sb("xn_t", [P, TOK], F32, first)
            k_stack1 = sb("k_stack1", [P, RING, SEQ], F32R, first)
            v_blocks1 = sb("v_blocks1", [P, RING, SB, LATENT], F32, first)
            latent = sb("latent", [P, TOK], F32R, first)
            latent_rows = sb("latent_rows", [P, BLOCKS, LATENT], F32, first)
            q_high = sb("q_high", [P, SEQ], F32R, first)
            q_low = sb("q_low", [P, SEQ], F32R, first)
            attended = sb("attended", [P, GROUPS, SEQ], F32, first)
            down3 = sb("down3", [P, 3, LATENT], F32, first)
            absorbed_q = sb("absorbed_q", [P, HEADS * LATENT], F32, first)
            absorbed_o = sb("absorbed_o", [P, GROUPS, DIM], F32, first)
        w_in = attended
        wq_raw, wout_raw = w_in[:, 0, :], w_in[:, 1, :].rearrange("p (g o) -> p g o", g=8)
        wk_raw, wv_raw = w_in[0:LATENT, 2, :], w_in[0:LATENT, 3, :]
        wq_t = probs[:, 0:2, :].rearrange("p a (g d) -> p (a g) d", g=4)
        wkv_t = probs[:, 2, :].rearrange("p (w g c) -> p w g c", w=2, g=8)

        second = ctx.enter_context(ExitStack())
        v_tokens = sb("v_tokens", [P, BLOCKS, HEADS, HD2 + 1], F32, second)
        v_blocks2 = sb("v_blocks2", [P, RING, SB, GROUP, HD2 + 1], F32, second)
        with ExitStack() as between:
            h_t = sb("h_t", [P, 2, SEQ], F32, between)
            wqkv = sb("wqkv", [P, 3 * DIM], F32, between)
            rope = sb("rope", [P, 2, SB, HD2 // 2], F32, between)
            qk_raw = sb("qk_raw", [P, SB, 2 * DIM], F32, between)
            qk = sb("qk", [P, SB, 2 * DIM], F32, between)
            rope_part = sb("rope_part", [P, 2, SB, 2 * DIM // 2], F32, between)
            qk_high = sb("qk_high", [P, 2, SEQ], F32R, between)
            qk_low = sb("qk_low", [P, 2, SEQ], F32R, between)
        k_stack2 = sb("k_stack2", [P, RING, GROUP, SEQ], F32R, second)
        second.close()
        both.close()

        last_part = ctx.enter_context(ExitStack())
        affine2 = sb("affine2", [P, 2, DIM], F32, last_part)
        wproj = sb("wproj", [P, DIM], F32, last_part)
        wgate = sb("wgate", [P, EXPERTS], F32, last_part)
        turned = sb("turned", [P, 2, SEQ], F32, last_part)
        h2_t = sb("h2_t", [P, 2, SEQ], F32, last_part)
        ROUTE = [P, BLOCKS, EXPERTS]
        gates = sb("gates", ROUTE, F32, last_part)
        chosen = [sb(f"chosen{k}", ROUTE, F32, last_part) for k in range(TOPK)]
        route = [sb(f"route{k}", ROUTE, F32, last_part) for k in range(3)]
        taken = sb("taken", [P, EXPERTS, BLOCKS], F32, last_part)
        rank = sb("rank", ROUTE, F32, last_part)
        first_slot = sb("first_slot", ROUTE, F32, last_part)
        row_value = sb("row_value", [P, BLOCKS], F32, last_part)
        slot_of = sb("slot_of", [P, TOPK, BLOCKS], F32, last_part)
        kept = sb("kept", [P, TOPK, BLOCKS], F32, last_part)
        gate_of = sb("gate_of", [P, TOPK, BLOCKS], F32, last_part)
        put_at = sb("put_at", [P, TOPK, BLOCKS], U32, last_part)
        get_at = sb("get_at", [P, TOPK, BLOCKS], U32, last_part)
        zeros = sb("zeros", [P, SB * DIM], F32, last_part)
        w1 = sb("w1", [P, 2, HIDDEN], F32, last_part)
        w2 = sb("w2", [P, 2, HIDDEN // P, DIM], F32, last_part)
        b1_rows = sb("b1_rows", [EXPERTS * HIDDEN // P, P], F32, last_part)
        b1 = sb("b1", [P, EXPERTS, HIDDEN // P], F32, last_part)
        b2 = sb("b2", [P, 2, DIM], F32, last_part)
        expert_in = sb("expert_in", [P, 2, SB, DIM], F32, last_part)
        expert_in_t = sb("expert_in_t", [P, 2, CAPACITY], F32, last_part)
        hidden = sb("hidden", [P, 2, HIDDEN // P, BANK], F32, last_part)
        expert_out = sb("expert_out", [P, 2, SB, DIM], F32, last_part)
        fetched = sb("fetched", [P, TOPK, BLOCKS, DIM], F32, last_part)
        x1_back = sb("x1_back", [P, BLOCKS, DIM], F32, last_part)

        x1_dram = nc.dram_tensor("x1_scratch", [BATCH, SEQ, DIM], F32).ap()
        q_dram = nc.dram_tensor("q_scratch", [BATCH, 2, HEADS, HD2, SEQ], F32).ap()
        k_dram = nc.dram_tensor("k_scratch", [BATCH, 2, HEADS, HD2, SEQ], F32).ap()
        slots_in = nc.dram_tensor("slots_in", [EXPERTS * CAPACITY, DIM], F32).ap()
        slots_out = nc.dram_tensor("slots_out", [EXPERTS * CAPACITY, DIM], F32).ap()

        def tokens(dram, b):
            return dram[b].rearrange("(n p) d -> p n d", p=P)

        def blocks_of(b):
            return slice(SB * b, SB * (b + 1))

        x_in = [sem(f"x_in{b}") for b in range(BATCH)]
        w_loaded, consts, ones_rows = sem("w_loaded"), sem("consts"), sem("ones_rows")
        dve_step = sem("dve_step")
        var_ready, root_ready, normed = sem("var_ready"), sem("root_ready"), sem("normed")
        pre_ready, pre_done, high_written = sem("pre_ready"), sem("pre_done"), sem("high_written")
        stored = sem("stored")
        a1 = Layer("a1", KDIM ** -0.5, True, LATENT, 3 * GROUP + 2, sem)
        a2 = Layer("a2", HD2 ** -0.5, False, HD2 + 1, 9, sem)
        a1.k_stack, a1.v_blocks = k_stack1, v_blocks1
        a2.k_stack, a2.v_blocks = k_stack2, v_blocks2
        PRE_TILES = 13
        QUADS = 12
        A1_TILES, A2_TILES = (a.first_tiles + (BATCH - 1) * a.pass_tiles + a.last_tiles for a in (a1, a2))

        x1_ready, x1_stored, h_ready = sem("x1_ready"), sem("x1_stored"), sem("h_ready")
        mid_loaded = sem("mid_loaded")
        mid_ready, mid_act, mid_dve = sem("mid_ready"), sem("mid_act"), sem("mid_dve")
        qk_drained, qk_turned, qk_rounded = sem("qk_drained"), sem("qk_turned"), sem("qk_rounded")
        qk_stored = sem("qk_stored")
        cleared = sem("cleared")
        v_ones, stack_cleared = sem("v_ones"), sem("stack_cleared")
        late_loaded = sem("late_loaded")
        post_ready, post_act, post_dve = sem("post_ready"), sem("post_act"), sem("post_dve")
        h2_ready, logits_ready = sem("h2_ready"), sem("logits_ready")
        exp_in, exp_out, mask_ready, count_ready = sem("exp_in"), sem("exp_out"), sem("mask_ready"), sem("count_ready")
        zeroed_src, zeroed, routed, scattered = sem("zeroed_src"), sem("zeroed"), sem("routed"), sem("scattered")
        w_in2 = [sem(f"expert_w{k}") for k in range(2)]
        e_in = [sem(f"expert_in{k}") for k in range(2)]
        e_turned, e_turned_done = sem("expert_turned"), sem("expert_turned_done")
        hid_ready, hid_done, out_ready = sem("hidden_ready"), sem("hidden_done"), sem("out_ready")
        out_done, out_stored = sem("out_done"), [sem(f"out_stored{k}") for k in range(2)]
        b1_turned = sem("b1_turned")
        gathered, x1_loaded, final_ready = sem("gathered"), sem("x1_loaded"), sem("final_ready")

        block = ctx.enter_context(nc.Block())

        def passes(eng, do):
            with eng.Fori(0, BATCH - 1) as i:
                do(i, False)
            do(BATCH - 1, True)

        @block.gpsimd
        def _(pool):
            pool.memset(ident[:], 0.0).then_inc(consts, 1)
            pool.memset(late_key[:], 0.0).then_inc(consts, 1)
            pool.memset(upper[:], 1.0).then_inc(consts, 1)
            pool.memset(ones[:], 1.0).then_inc(consts, 1)
            pool.wait_ge(consts, 4)
            pool.affine_select(out=ident[:], in_=ident[:], compare_op=ALU.not_equal, fill=1.0, base=0,
                               pattern=[[-1, P]], channel_multiplier=1).then_inc(consts, 1)
            diagonal = late_key[:, SEQ - P:]
            pool.affine_select(out=diagonal, in_=diagonal, compare_op=ALU.is_ge, fill=MASKED, base=0,
                               pattern=[[-1, P]], channel_multiplier=1).then_inc(consts, 1)
            pool.affine_select(out=upper[:], in_=upper[:], compare_op=ALU.is_ge, fill=0.0,
                               base=0, pattern=[[1, P]], channel_multiplier=-1).then_inc(consts, 1)
            pool.wait_ge(consts, 7)
            pool.memset(latent[STACK:P, :].bitcast(F32), 1.0).then_inc(ones_rows, 1)

            def mask(a):
                probs_ready = Tally(a.probs_ready, 2, UNITS * GROUPS)
                turns = Tally(a.masked, 0, SB * GROUPS)

                def slots(i, last):
                    probs_ready.turn(i)
                    for g, kind, what, quad in pass_steps(a, last):
                        if kind != "score" or what[1] < GROUP - 1:
                            continue
                        (c, kb, off), _ = what
                        exps = probs_ready.next(GROUP)
                        if kb >= CB * c:
                            pool.wait_ge(a.probs_ready, exps)
                            pool.sem_inc(a.mask_turn, 1)
                            part = probs[:, GROUP * (quad % 2):GROUP * (quad % 2 + 1), off:off + P]
                            pool.affine_select(out=part, in_=part, compare_op=ALU.is_ge, fill=0.0, base=0,
                                               pattern=[[0, GROUP], [1, P]], channel_multiplier=-1).then_inc(a.masked, 1)

                passes(pool, slots)

            mask(a1)
            pool.wait_ge(a1.tile_done, 2 + A1_TILES)
            for rows in (slice(LATENT, 2 * LATENT), slice(2 * LATENT, P)):
                pool.memset(q_stack[rows].rearrange("p r h q -> p (r h q)").bitcast(F32), 0.0).then_inc(stack_cleared, 1)
            pool.wait_ge(qk_stored, 16 * 4 * BATCH)
            pool.wait_ge(stack_cleared, 2)
            for r in (2, 3):
                pool.memset(k_stack2[:, r].rearrange("p h q -> p (h q)").bitcast(F32), 1.0).then_inc(stack_cleared, 1)
            mask(a2)
            pool.wait_ge(zeroed, 16 * EXPERTS)
            pool.wait_ge(routed, 1)
            for n in range(BLOCKS):
                for k in range(TOPK):
                    pool.indirect_dma_start(
                        out=slots_in, out_offset=bass.IndirectOffsetOnAxis(ap=put_at[:, k, n:n + 1], axis=0),
                        in_=x[:, n, :], in_offset=None, bounds_check=EXPERTS * CAPACITY - 1,
                        oob_is_err=False).then_inc(scattered, 16)
            for k in range(2):
                pool.wait_ge(out_stored[k], 16 * EXPERTS // 2)
            for n in range(BLOCKS):
                for k in range(TOPK):
                    pool.indirect_dma_start(
                        out=fetched[:, k, n, :], out_offset=None, in_=slots_out,
                        in_offset=bass.IndirectOffsetOnAxis(ap=get_at[:, k, n:n + 1], axis=0)).then_inc(gathered, 16)

        @block.sync
        def _(sp):
            for b in range(BATCH):
                sp.dma_start(x[:, blocks_of(b), :], tokens(t["x"], b)).then_inc(x_in[b], 16)
                if b == 0:
                    sp.dma_start(wq_raw, t["wq"].rearrange("d h k -> d (h k)")).then_inc(w_loaded, 16)
                    sp.dma_start(wk_raw, t["wk"].rearrange("c h k -> c (h k)")).then_inc(w_loaded, 16)
                    sp.dma_start(wv_raw, t["wv"].rearrange("c h k -> c (h k)")).then_inc(w_loaded, 16)
                    sp.dma_start(wout_raw, t["wout"].rearrange("(g two) k o -> (two k) g o", two=2)).then_inc(w_loaded, 16)
                    for r in range(3):
                        sp.dma_start(down3[:, r, :], t["wdown"]).then_inc(w_loaded, 16)
            for k, name in enumerate(("ln1_g", "ln1_b")):
                sp.dma_start(affine1[:, k, :], t[name].partition_broadcast(P)).then_inc(w_loaded, 16)

            def max_rows_in(a, r):
                for part in range(2):
                    n = GROUP * SB
                    sp.dma_start(q_stack[STACK + part:STACK + part + 1, r, :, :].bitcast(F32)
                                 .rearrange("p h (n q) -> p (h n) q", q=P),
                                 max_rows[n * part:n * (part + 1), :].bitcast(F32)).then_inc(a.max_in[r], 16)

            def slots_of(a, stack_in):
                tile_done = Tally(a.tile_done, 2, a.pass_tiles)
                for g in range(a.ahead):
                    if a.queries:
                        sp.wait_ge(a.tile_done, tile_done.next())
                    stack_in(g, 0)
                sp.wait_ge(a.tile_done, tile_done.next(M_ITEMS + 1))
                max_rows_in(a, 0)
                tile_done.start += a.first_tiles

                def slots(i, last):
                    tile_done.turn(i)
                    at = -1
                    for g, kind, what, _ in pass_steps(a, last):
                        done = tile_done.next() if kind in TILED else None
                        if kind == "queries":
                            sp.wait_ge(a.tile_done, done)
                            stack_in((g + 3) % GROUPS, i if g < 1 else i + 1)
                        elif not a.queries and g > at and not (last and g >= 2):
                            sp.wait_ge(a.inverse_ready, 2 * GROUPS * i + 2 * g + 1)
                            stack_in((g + 2) % GROUPS, i if g < 2 else i + 1)
                        if kind == "max rows":
                            sp.wait_ge(a.tile_done, done)
                            max_rows_in(a, (g + 1) % RING)
                        at = max(at, g)

                passes(sp, slots)

            def stack_in1(g, b):
                done = a1.stack_in[g]
                for j in range(GROUP):
                    rows = slice(LATENT * j, LATENT * (j + 1))
                    for part, src in enumerate((q_high, q_high, q_low)):
                        sp.dma_start(q_stack[LATENT * part:LATENT * (part + 1), g, j, :].bitcast(F32),
                                     src[rows, :].bitcast(F32)).then_inc(done, 16)
                sp.dma_start(k_stack1[0:ROWS, g, :].bitcast(F32),
                             latent[0:ROWS, bass.ds(b * SEQ, SEQ)].bitcast(F32)).then_inc(done, 16)
                sp.dma_start(v_blocks1[:, g, :, :], latent_rows[:, bass.ds(b * SB, SB), :]).then_inc(done, 16)

            def stack_in2(g, b):
                done = a2.stack_in[g]
                sp.wait_ge(qk_stored, 16 * 4 * BATCH)
                heads = slice(GROUP * g, GROUP * (g + 1))
                for part in range(4):
                    rows = slice(HD2 * part, HD2 * (part + 1))
                    for stack, dram, low in ((q_stack, q_dram, part // 2), (k_stack2, k_dram, part % 2)):
                        src = dram[bass.ds(b, 1), low, heads, :, :].rearrange("one h c q -> c (one h) q")
                        sp.dma_start(stack[rows, g, :, :].bitcast(F32), src).then_inc(done, 16)
                sp.dma_start(v_blocks2[:, g, :, :, :], v_tokens[:, bass.ds(b * SB, SB), heads, :]).then_inc(done, 16)

            sp.wait_ge(pre_done, PRE_TILES)
            sp.wait_ge(ones_rows, 1)
            slots_of(a1, stack_in1)

            sp.wait_ge(a1.tile_done, 2 + A1_TILES)
            sp.dma_start(wqkv[:], t["wqkv"]).then_inc(mid_loaded, 16)
            for k, name in enumerate(("rope_cos", "rope_sin")):
                sp.dma_start(rope[:, k, :, :], t[name].rearrange("(n p) j -> p n j", p=P)).then_inc(mid_loaded, 16)
            for b in range(BATCH):
                sp.wait_ge(x1_ready, SB * (b + 1))
                sp.dma_start(tokens(x1_dram, b), x[:, blocks_of(b), :]).then_inc(x1_stored, 16)
                for w, dram in enumerate((q_dram, k_dram)):
                    sp.wait_ge(mid_dve, 2 * b + w + 1)
                    for low, src in enumerate((qk_high, qk_low)):
                        sp.dma_start(dram[b, low].rearrange("h c q -> (h c) q"),
                                     src[:, w, :].bitcast(F32)).then_inc(qk_stored, 16)
            sp.wait_ge(qk_stored, 16 * 4 * BATCH)
            sp.wait_ge(stack_cleared, 6)
            sp.wait_ge(v_ones, 1)
            slots_of(a2, stack_in2)

            sp.wait_ge(a2.tile_done, 2 + A2_TILES)
            sp.dma_start(wproj[:], t["wproj"]).then_inc(late_loaded, 16)
            sp.dma_start(wgate[:], t["wgate"]).then_inc(late_loaded, 16)
            for k, name in enumerate(("ln2_g", "ln2_b")):
                sp.dma_start(affine2[:, k, :], t[name].partition_broadcast(P)).then_inc(late_loaded, 16)
            sp.dma_start(b1_rows[:], t["b1"].rearrange("e (f p) -> (e f) p", p=P)).then_inc(late_loaded, 16)
            sp.wait_ge(zeroed_src, 1)
            for e in range(EXPERTS):
                sp.dma_start(slots_in[CAPACITY * e:CAPACITY * (e + 1), :].rearrange("(p n) d -> p (n d)", p=P),
                             zeros[:]).then_inc(zeroed, 16)

            def weights_in(e, k):
                sp.dma_start(w1[:, k, :], t["w1"][e]).then_inc(w_in2[k], 16)
                sp.dma_start(w2[:, k, :, :], t["w2"][e].rearrange("(f p) d -> p f d", p=P)).then_inc(w_in2[k], 16)
                sp.dma_start(b2[:, k, :], t["b2"][e].partition_broadcast(P)).then_inc(w_in2[k], 16)

            def expert_rows_in(e, k):
                sp.dma_start(expert_in[:, k, :, :],
                             slots_in[CAPACITY * e:CAPACITY * (e + 1), :].rearrange("(n p) d -> p n d", p=P)
                             ).then_inc(e_in[k], 16)

            weights_in(0, 0)
            weights_in(1, 1)
            sp.wait_ge(scattered, 16 * TOPK * BLOCKS)
            expert_rows_in(0, 0)
            expert_rows_in(1, 1)
            for b in range(BATCH):
                sp.dma_start(x1_back[:, blocks_of(b), :], tokens(x1_dram, b)).then_inc(x1_loaded, 16)
            for e in range(EXPERTS):
                k = e % 2
                sp.wait_ge(out_done, e + 1)
                sp.dma_start(slots_out[CAPACITY * e:CAPACITY * (e + 1), :].rearrange("(n p) d -> p n d", p=P),
                             expert_out[:, k, :, :]).then_inc(out_stored[k], 16)
                if e + 2 < EXPERTS:
                    weights_in(e + 2, k)
                    expert_rows_in(e + 2, k)
            for b in range(BATCH):
                sp.wait_ge(final_ready, SB * (b + 1))
                sp.dma_start(tokens(t["out"], b), x[:, blocks_of(b), :]).then_inc(stored, 16)
            for n, (name, make) in enumerate((dump or {}).items()):
                sp.dma_start(t[name], make(tensors)).then_inc(stored, 16)
            sp.wait_ge(stored, 16 * (BATCH + len(dump or {})))

        @block.scalar
        def _(act):
            roots = 0

            def square_root(b):
                nonlocal roots
                roots += 1
                act.wait_ge(var_ready, roots)
                act.activation(root[:, blocks_of(b)], var_eps[:, blocks_of(b)], ACT.Sqrt).then_inc(root_ready, 1)

            def copy(out, src):
                return act.activation(out, src, ACT.Copy)

            for b in range(BATCH):
                square_root(b)
            n = 0

            def drain(out, src):
                nonlocal n
                act.wait_ge(pre_ready, n + 1)
                copy(out, src).then_inc(pre_done, 1)
                n += 1

            drain(wq_t.rearrange("p g d -> p (g d)"), tile_ps[:, 0, :])
            drain(wkv_t.rearrange("p w g c -> p (w g c)"), tile_ps[:, 1, 0:2 * 8 * LATENT])
            drain(absorbed_q[:].rearrange("p (g two c) -> p two g c", two=2, c=LATENT),
                  tile_ps[:, 0, :].rearrange("p (two k) -> p two k", two=2)[:, :, 0:8 * LATENT]
                  .rearrange("p two (g c) -> p two g c", c=LATENT))
            act.wait_ge(pre_ready, n + 1)
            for j in range(GROUP):
                rows, col = slice(LATENT * j, LATENT * (j + 1)), BANK * (j % 2)
                last = copy(absorbed_o[rows, :, :], tile_ps[rows, 1, col:col + BANK].rearrange("p (g o) -> p g o", o=DIM))
            last.then_inc(pre_done, 1)
            n += 1
            for b in range(BATCH):
                drain(xn_t[:, SEQ * b:SEQ * (b + 1)], tile_ps[:, n % 2, :])
            for b in range(BATCH):
                act.wait_ge(pre_ready, n + 1)
                copy(latent[0:STACK, SEQ * b:SEQ * (b + 1)], tile_ps[0:STACK, n % 2, :]).then_inc(high_written, 1)
                n += 1
            drain(latent_rows[:].rearrange("p n c -> p (n c)"), tile_ps[:, n % 2, :])
            assert n == PRE_TILES

            def exponentials(a):
                act.sem_inc(a.probs_ready, 2)
                act.sem_inc(a.chunk_free, 1)
                scores_ready = Tally(a.scores_ready, 0, UNITS * GROUPS)
                quad_used = Tally(a.quad_done, 0, QUADS * GROUPS)
                quad_done = Tally(a.quad_done, 2, QUADS * GROUPS)
                inverse_ready = Tally(a.inverse_ready, 2, 2 * GROUPS)

                def slots(i, last):
                    for tally in (scores_ready, quad_used, quad_done, inverse_ready):
                        tally.turn(i)
                    for g, kind, what, quad in pass_steps(a, last):
                        if kind == "score":
                            (c, kb, off), h = what
                            u = GROUP * quad + h
                            if h == 0:
                                act.wait_ge(a.quad_done, quad_used.next())
                            act.wait_ge(a.scores_ready, scores_ready.next())
                            act.activation(probs[:, u % 8, off:], score_ps[:, u % 2, off:], ACT.Exp,
                                           scale=a.scale).then_inc(a.probs_ready, 1)
                        elif kind == "drain":
                            act.wait_ge(a.quad_done, quad_done.next(len(key_blocks(what))))
                            act.wait_ge(a.inverse_ready, inverse_ready.next())
                            if a.sums:
                                copy(attended[:, g, BANK * what:BANK * (what + 1)], value_ps[:])
                                copy(sum_inv[:], sum_ps[:]).then_inc(a.chunk_free, 1)
                            else:
                                copy(sum_inv[:], value_ps[:]).then_inc(a.chunk_free, 1)

                passes(act, slots)

            exponentials(a1)

            for b in range(BATCH):
                for _ in range(3):
                    square_root(b)
                act.wait_ge(mid_ready, 7 * b + 1)
                copy(h_t[:, b % 2, :], tile_ps[:, (7 * b) % 2, :]).then_inc(mid_act, 1)
                act.wait_ge(v_ones, 1)
                if b:
                    act.wait_ge(qk_turned, b)
                for m in range(4):
                    act.wait_ge(mid_ready, 7 * b + 2 + m)
                    tile = tile_ps[:, (7 * b + 1 + m) % 2, :].rearrange("p (n c) -> p n c", n=2)
                    copy(qk_raw[:, 2 * m:2 * m + 2, :], tile[:, :, 0:2 * DIM]).then_inc(qk_drained, 1)
                    for two in range(2):
                        last = copy(v_tokens[:, SB * b + 2 * m + two, :, 0:HD2],
                                    tile[:, two, 2 * DIM:3 * DIM].rearrange("p (h c) -> p h c", c=HD2))
                    last.then_inc(mid_act, 1)
                if b:
                    act.wait_ge(qk_stored, 16 * 4 * b)
                for w in range(2):
                    act.wait_ge(mid_ready, 7 * b + 6 + w)
                    copy(qk_high[:, w, :], tile_ps[:, (7 * b + 5 + w) % 2, :]).then_inc(qk_rounded, 1)

            exponentials(a2)

            for b in range(BATCH):
                act.wait_ge(post_ready, 3 * b + 1)
                copy(turned[:, b % 2, :], tile_ps[:, (3 * b) % 2, :]).then_inc(post_act, 1)
                square_root(b)
                act.wait_ge(post_ready, 3 * b + 3)
                copy(h2_t[:, b % 2, :], tile_ps[:, (3 * b + 2) % 2, :]).then_inc(post_act, 1)
            act.wait_ge(exp_in, 1)
            act.activation(gates[:], route[0][:], ACT.Exp).then_inc(exp_out, 1)
            act.wait_ge(b1_turned, 1)
            for e in range(EXPERTS):
                act.wait_ge(w_in2[e % 2], 48 * (e // 2 + 1))
                for c in range(2):
                    for f in range(HIDDEN // P):
                        unit = 8 * e + 4 * c + f
                        act.wait_ge(hid_ready, unit + 1)
                        if f == 0 and 2 * e + c >= 2:
                            act.wait_ge(out_ready, 2 * e + c - 1)
                        act.activation(hidden[:, c, f, :], score_ps[:, unit % 2, :], ACT.Gelu,
                                       bias=b1[:, e, f:f + 1]).then_inc(hid_done, 1)
            for b in range(BATCH):
                square_root(b)

        @block.tensor
        def _(pe):
            pe.wait_ge(consts, 7)
            pe.wait_ge(w_loaded, 16 * 9)
            for g in range(8):
                last = pe.transpose(tile_ps[:, 0, P * g:P * (g + 1)], wq_raw[:, P * g:P * (g + 1)], ident[:])
            last.then_inc(pre_ready, 1)
            for w, raw in enumerate((wk_raw, wv_raw)):
                for g in range(8):
                    at = (8 * w + g) * LATENT
                    last = pe.transpose(tile_ps[:, 1, at:at + LATENT], raw[:, P * g:P * (g + 1)], ident[0:LATENT, 0:LATENT])
            last.then_inc(pre_ready, 1)
            pe.wait_ge(pre_done, 2)
            for h in range(HEADS):
                k = slice(KDIM * (h % 2), KDIM * (h % 2 + 1))
                col = BANK * (h % 2) + LATENT * (h // 2)
                last = pe.matmul(tile_ps[:, 0, col:col + LATENT], wq_t[k, h // 2, :], wkv_t[k, 0, h // 2, :],
                                 start=True, stop=True)
            last.then_inc(pre_ready, 1)
            for h in range(HEADS):
                k = slice(KDIM * (h % 2), KDIM * (h % 2 + 1))
                j, g = h % GROUP, h // GROUP
                col = BANK * (h % 2) + P * g
                last = pe.matmul(tile_ps[LATENT * j:LATENT * (j + 1), 1, col:col + P],
                                 wkv_t[k, 1, h // 2, :], wout_raw[k, h // 2, :], start=True, stop=True)
            last.then_inc(pre_ready, 1)
            n = 4
            for b in range(BATCH):
                pe.wait_ge(normed, SB * (b + 1))
                pe.wait_ge(pre_done, n - 1)
                for m in range(SB):
                    last = pe.transpose(tile_ps[:, n % 2, P * m:P * (m + 1)], xn[:, SB * b + m, :], ident[:])
                last.then_inc(pre_ready, 1)
                n += 1
            for b in range(BATCH):
                pe.wait_ge(pre_done, n - 1)
                for c in range(CHUNKS):
                    at = SEQ * b + BANK * c
                    last = pe.matmul(tile_ps[0:STACK, n % 2, BANK * c:BANK * (c + 1)],
                                     down3[:].rearrange("p r c -> p (r c)"), xn_t[:, at:at + BANK], start=True, stop=True)
                last.then_inc(pre_ready, 1)
                n += 1
            pe.wait_ge(pre_done, n - 1)
            for m in range(BLOCKS):
                last = pe.matmul(tile_ps[:, n % 2, LATENT * m:LATENT * (m + 1)], xn_t[:, P * m:P * (m + 1)],
                                 down3[:, 0, :], start=True, stop=True)
            last.then_inc(pre_ready, 1)
            pe.wait_ge(pre_done, n + 1)

            def attention(a):
                pe.sem_inc(a.quad_done, 2)
                tile_done = Tally(a.tile_done, 0, a.pass_tiles)
                probs_ready = Tally(a.probs_ready, 0, UNITS * GROUPS)
                chunk_free = Tally(a.chunk_free, 0, 2 * GROUPS)
                masked = Tally(a.masked, 0, SB * GROUPS)
                tiles = 0

                def next_tile():
                    nonlocal tiles
                    pe.wait_ge(a.tile_done, tile_done.next())
                    tiles += 1
                    return tile_ps[:, (tiles - 1) % 2, :]

                def keys_of(r, h):
                    return a.k_stack[0:ROWS, r, :] if a.queries else a.k_stack[0:ROWS, r, h, :]

                def queries(g, b):
                    tile = next_tile()
                    for c in range(CHUNKS):
                        last = pe.matmul(tile[:, BANK * c:BANK * (c + 1)], absorbed_q[:, P * g:P * (g + 1)],
                                         xn_t[:, bass.ds(b * SEQ + BANK * c, BANK)], start=True, stop=True)
                    last.then_inc(a.tile_ready, 1)

                def max_scores(r, heads, qb):
                    tile = next_tile()
                    keys = (qb + 1) * P
                    for at, h in enumerate(heads):
                        for k0 in range(0, keys, BANK):
                            wide = max(2 * P, min(BANK, keys - k0))
                            col = BANK * at + k0
                            last = pe.matmul(tile[:, col:col + wide], q_stack[0:STACK, r, h, P * qb:P * (qb + 1)],
                                             keys_of(r, h)[0:STACK, k0:k0 + wide], start=True, stop=True)
                    last.then_inc(a.tile_ready, 1)

                def max_to_rows(parts):
                    pe.wait_ge(a.parts_ready, parts)
                    tile = next_tile()
                    pe.transpose(tile[:, 0:P], max_parts[:].rearrange("p a b -> p (a b)").bitcast(F32),
                                 ident[:]).then_inc(a.tile_ready, 1)

                def score(r, c, kb, off, h, unit):
                    pe.wait_ge(a.probs_ready, probs_ready.next())
                    start = min(off, BANK - 2 * P)
                    last = pe.matmul(score_ps[:, unit % 2, start:], keys_of(r, h)[:, P * kb:P * (kb + 1)],
                                     q_stack[0:ROWS, r, h, BANK * c + start:BANK * (c + 1)],
                                     start=True, stop=True)
                    last.then_inc(a.scores_ready, 1)

                def values(r, c, kb, off, quad, ready):
                    if kb == 0:
                        pe.wait_ge(a.chunk_free, chunk_free.next())
                    if kb >= CB * c:
                        pe.wait_ge(a.masked, masked.next())
                    else:
                        pe.wait_ge(a.probs_ready, ready)
                    for h in range(GROUP):
                        v = a.v_blocks[:, r, kb, :] if a.queries else a.v_blocks[:, r, kb, h, :]
                        last = pe.matmul(value_ps[LATENT * h:LATENT * h + a.v_width, off:], v,
                                         probs[:, (GROUP * quad + h) % 8, off:],
                                         start=kb == 0, stop=True, skip_group_check=True)
                    return last

                def sums(kb, off, quad):
                    for h in range(GROUP):
                        last = pe.matmul(sum_ps[LATENT * h:LATENT * (h + 1), off:], ones[:, 0:LATENT],
                                         probs[:, (GROUP * quad + h) % 8, off:],
                                         start=kb == 0, stop=True, skip_group_check=True)
                    return last

                def turn(drained):
                    pe.wait_ge(a.chunk_free, drained)
                    tile = next_tile()
                    for m in range(CB):
                        last = pe.transpose(tile[:, P * m:P * (m + 1)], sum_inv[:, P * m:P * (m + 1)], ident[:])
                    last.then_inc(a.tile_ready, 1)

                def project(half, scaled):
                    pe.wait_ge(a.inverse_ready, 2 * scaled + 3)
                    tile = next_tile()
                    for m in range(CB):
                        q = P * (CB * half + m)
                        for g in range(GROUPS):
                            mm = pe.matmul(tile[:, P * m:P * (m + 1)], attended[:, g, q:q + P],
                                           absorbed_o[:, g, :], start=g == 0, stop=g == GROUPS - 1)
                    mm.then_inc(a.tile_ready, 1)

                if a.queries:
                    for g in range(a.ahead):
                        queries(g, 0)
                pe.wait_ge(a.stack_in[0], 16 * a.q_dmas)
                for heads, qb in max_items():
                    max_scores(0, heads, qb)
                max_to_rows(1)
                tile_done.start += a.first_tiles

                def slots(i, last):
                    for tally in (tile_done, probs_ready, chunk_free, masked):
                        tally.turn(i)
                    at = -1
                    for g, kind, what, quad in pass_steps(a, last):
                        if kind == "queries":
                            queries((g + 3) % GROUPS, i if g < 1 else i + 1)
                            continue
                        if g > at:
                            if not (last and g == 3):
                                pe.wait_ge(a.stack_in[(g + 1) % RING], 16 * a.q_dmas * (i + (1 if g < 3 else 2)))
                            pe.wait_ge(a.max_in[g], 32 * (i + 1))
                            at = g
                        if kind == "score":
                            score(g, *what[0], what[1], GROUP * quad + what[1])
                        elif kind == "max":
                            max_scores((g + 1) % RING, *what)
                        elif kind == "max rows":
                            max_to_rows(GROUPS * i + g + 2)
                        elif kind == "values":
                            mm = values(g, *what, quad, UNITS * (GROUPS * i + g) + 2 + GROUP * (quad + 1))
                            if not a.sums:
                                mm.then_inc(a.quad_done, 1)
                        elif kind == "sums":
                            sums(*what[1:], quad).then_inc(a.quad_done, 1)
                        elif kind == "turn":
                            turn(2 * (GROUPS * i + g) + what + 2)
                        elif kind == "project":
                            project(what, GROUPS * i + GROUPS)

                passes(pe, slots)

            attention(a1)

            pe.wait_ge(mid_loaded, 48)
            pe.wait_ge(a1.tile_done, 2 + A1_TILES)

            def mid_tile(b, k):
                if 7 * b + k >= 2:
                    pb, pk = divmod(7 * b + k - 2, 7)
                    if pk < 5:
                        pe.wait_ge(mid_act, 5 * pb + pk + 1)
                    else:
                        pe.wait_ge(mid_dve, 2 * pb + pk - 4)
                return tile_ps[:, (7 * b + k) % 2, :]

            for b in range(BATCH):
                pe.wait_ge(h_ready, b + 1)
                tile = mid_tile(b, 0)
                for m in range(SB):
                    last = pe.transpose(tile[:, P * m:P * (m + 1)], x[:, SB * b + m, :], ident[:])
                last.then_inc(mid_ready, 1)
                pe.wait_ge(mid_act, 5 * b + 1)
                by_kind = wqkv[:].rearrange("p (h s c) -> p s h c", s=3, c=HD2)
                for k in range(4):
                    tile = mid_tile(b, 1 + k)
                    for two in range(2):
                        m = 2 * k + two
                        last = pe.matmul(tile[:, BANK * two:BANK * two + 3 * DIM], h_t[:, b % 2, P * m:P * (m + 1)],
                                         by_kind, start=True, stop=True)
                    last.then_inc(mid_ready, 1)
                pe.wait_ge(qk_turned, b + 1)
                for w in range(2):
                    tile = mid_tile(b, 5 + w)
                    for m in range(SB):
                        last = pe.transpose(tile[:, P * m:P * (m + 1)], qk[:, m, DIM * w:DIM * (w + 1)], ident[:])
                    last.then_inc(mid_ready, 1)

            pe.wait_ge(mid_dve, 2 * BATCH)
            pe.wait_ge(cleared, 1)
            attention(a2)

            pe.wait_ge(late_loaded, 80)
            pe.wait_ge(a2.tile_done, 2 + A2_TILES)

            def post_tile(b, k):
                if 3 * b + k >= 2:
                    pb, pk = divmod(3 * b + k - 2, 3)
                    if pk == 1:
                        pe.wait_ge(post_dve, pb + 1)
                    else:
                        pe.wait_ge(post_act, 2 * pb + pk // 2 + 1)
                return tile_ps[:, (3 * b + k) % 2, :]

            for b in range(BATCH):
                tile = post_tile(b, 0)
                for m in range(SB):
                    last = pe.transpose(tile[:, P * m:P * (m + 1)], x[:, SB * b + m, :], ident[:])
                last.then_inc(post_ready, 1)
                pe.wait_ge(post_act, 2 * b + 1)
                tile = post_tile(b, 1)
                for m in range(SB):
                    last = pe.matmul(tile[:, P * m:P * (m + 1)], turned[:, b % 2, P * m:P * (m + 1)], wproj[:],
                                     start=True, stop=True)
                last.then_inc(post_ready, 1)
                pe.wait_ge(h2_ready, b + 1)
                tile = post_tile(b, 2)
                for m in range(SB):
                    last = pe.transpose(tile[:, P * m:P * (m + 1)], x[:, SB * b + m, :], ident[:])
                last.then_inc(post_ready, 1)
                pe.wait_ge(post_act, 2 * b + 2)
                for m in range(SB):
                    at = EXPERTS * (SB * b + m)
                    last = pe.matmul(value_ps[:, at:at + EXPERTS], h2_t[:, b % 2, P * m:P * (m + 1)], wgate[:],
                                     start=True, stop=True)
            last.then_inc(logits_ready, 1)
            pe.wait_ge(mask_ready, 1)
            flat = route[0][:].rearrange("p n e -> p (n e)")
            pe.matmul(value_ps[:, 0:BLOCKS * EXPERTS], upper[:], flat, start=True, stop=True).then_inc(count_ready, 1)
            pe.matmul(sum_ps[:, 0:BLOCKS * EXPERTS], ones[:], flat, start=True, stop=True).then_inc(count_ready, 1)

            pe.transpose(score_ps[:, 0, 0:EXPERTS * HIDDEN // P], b1_rows[:], ident[0:EXPERTS * HIDDEN // P, 0:EXPERTS * HIDDEN // P]
                         ).then_inc(count_ready, 1)
            pe.wait_ge(b1_turned, 1)

            def expert_turn(e):
                pe.wait_ge(e_in[e % 2], 16 * (e // 2 + 1))
                if e:
                    pe.wait_ge(e_turned_done, e)
                for m in range(SB):
                    last = pe.transpose(tile_ps[:, 0, P * m:P * (m + 1)], expert_in[:, e % 2, m, :], ident[:])
                last.then_inc(e_turned, 1)

            def expert_hidden(e, c):
                for f in range(HIDDEN // P):
                    unit = 8 * e + 4 * c + f
                    if unit >= 2:
                        pe.wait_ge(hid_done, unit - 1)
                    pe.matmul(score_ps[:, unit % 2, :], w1[:, e % 2, P * f:P * (f + 1)],
                              expert_in_t[:, e % 2, BANK * c:BANK * (c + 1)], start=True, stop=True).then_inc(hid_ready, 1)

            def expert_output(e, c):
                pe.wait_ge(hid_done, 8 * e + 4 * (c + 1))
                if c == 0 and e:
                    pe.wait_ge(out_done, e)
                for m in range(CB):
                    for f in range(HIDDEN // P):
                        last = pe.matmul(tile_ps[:, 1, BANK * c + P * m:BANK * c + P * (m + 1)],
                                         hidden[:, c, f, P * m:P * (m + 1)], w2[:, e % 2, f, :],
                                         start=f == 0, stop=f == HIDDEN // P - 1)
                last.then_inc(out_ready, 1)

            expert_turn(0)
            for e in range(EXPERTS):
                pe.wait_ge(w_in2[e % 2], 48 * (e // 2 + 1))
                pe.wait_ge(e_turned_done, e + 1)
                expert_hidden(e, 0)
                expert_hidden(e, 1)
                expert_output(e, 0)
                if e + 1 < EXPERTS:
                    expert_turn(e + 1)
                expert_output(e, 1)

        @block.vector
        def _(dve):
            chain = 0
            norms = 0

            def link(ins):
                nonlocal chain
                chain += 1
                ins.then_inc(dve_step, 1)
                dve.wait_ge(dve_step, chain)

            def norm_stats(src, b):
                nonlocal norms
                norms += 1
                part = blocks_of(b)
                for n in range(SB * b, SB * (b + 1)):
                    ins = dve.bn_stats(stats[:, n, :], src[:, n, :])
                link(ins)
                for n in range(SB * b, SB * (b + 1)):
                    ins = dve.bn_aggr(mean_var[:, n, :], stats[:, n, :])
                link(ins)
                dve.tensor_scalar(var_eps[:, part], mean_var[:, part, 1], EPS, None, ALU.add).then_inc(var_ready, 1)
                dve.wait_ge(root_ready, norms)
                link(dve.reciprocal(rstd[:, part], root[:, part]))
                link(dve.tensor_tensor(newton[:, part], rstd[:, part], rstd[:, part], ALU.mult))
                dve.wait_ge(var_ready, norms)
                link(dve.tensor_tensor(newton[:, part], newton[:, part], var_eps[:, part], ALU.mult))
                link(dve.tensor_scalar(newton[:, part], newton[:, part], -0.5, 1.5, ALU.mult, ALU.add))
                link(dve.tensor_tensor(rstd[:, part], rstd[:, part], newton[:, part], ALU.mult))

            def norm_apply(out, src, b, signal=None):
                for n in range(SB * b, SB * (b + 1)):
                    ins = dve.tensor_scalar(out[:, n, :], src[:, n, :], mean_var[:, n, 0:1], rstd[:, n:n + 1],
                                            ALU.subtract, ALU.mult)
                    if signal is not None:
                        ins.then_inc(signal, 1)
                if signal is None:
                    link(ins)

            def gain_and_bias(buf, b, vectors, signal):
                part = buf[:, blocks_of(b), :]
                for which, op in enumerate((ALU.mult, ALU.add)):
                    vector = vectors[:, which, :].unsqueeze(1).broadcast_to([P, SB, DIM])
                    ins = dve.tensor_tensor(part, part, vector, op)
                    if op == ALU.mult:
                        link(ins)
                    else:
                        ins.then_inc(signal, 1)

            link(dve.memset(max_parts[:].rearrange("p a b -> p (a b)").bitcast(F32), 0.0))
            dve.wait_ge(w_loaded, 16 * 9)
            dve.wait_ge(consts, 7)
            for b in range(BATCH):
                dve.wait_ge(x_in[b], 16)
                norm_stats(x, b)
                norm_apply(xn, x, b, normed)
            for b in range(BATCH):
                dve.wait_ge(high_written, b + 1)
                rows = slice(LATENT, 2 * LATENT)
                dve.tensor_tensor(latent[rows, SEQ * b:SEQ * (b + 1)], tile_ps[rows, (8 + b) % 2, :],
                                  latent[rows, SEQ * b:SEQ * (b + 1)].bitcast(F32), ALU.subtract).then_inc(pre_done, 1)

            def attention(a):
                dve.sem_inc(a.tile_done, 2)
                dve.sem_inc(a.inverse_ready, 3)
                tile_ready = Tally(a.tile_ready, 0, a.pass_tiles)
                tile_done = Tally(a.tile_done, 2, a.pass_tiles)
                high_ready = Tally(a.high_ready, 0, (2 if a.queries else 1) * GROUPS)
                inverted = Tally(a.inverted, 0, 2 * GROUPS)
                chunk_free = Tally(a.chunk_free, 1, 2 * GROUPS)
                tiles = 0

                def next_tile():
                    nonlocal tiles
                    dve.wait_ge(a.tile_ready, tile_ready.next())
                    tile_done.next()
                    tiles += 1
                    return tile_ps[:, (tiles - 1) % 2, :]

                def queries(last_use):
                    tile = next_tile()
                    if last_use:
                        dve.wait_ge(*last_use)
                    dve.tensor_copy(q_high[:], tile).then_inc(a.high_ready, 1)
                    dve.wait_ge(a.high_ready, high_ready.next())
                    dve.tensor_tensor(q_low[:], tile, q_high[:].bitcast(F32), ALU.subtract).then_inc(a.tile_done, 1)

                def max_scores(heads, qb):
                    tile = next_tile()
                    dve.sem_inc(a.max_turn, 1)
                    keys = (qb + 1) * P
                    for at, h in enumerate(heads):
                        row = tile[:, BANK * at:BANK * at + keys]
                        ins = dve.tensor_tensor_reduce(row, row, late_key[:, SEQ - keys:], 1.0, MASKED, ALU.add, ALU.max,
                                                       max_of[:, h, qb:qb + 1])
                    ins.then_inc(a.tile_done, 1)

                def max_to_rows(last_use):
                    dve.wait_ge(a.tile_done, tile_done.base + tile_done.n)
                    flat = max_of[:].rearrange("p h n -> p (h n)")
                    dve.tensor_scalar(max_parts[:, 0, :], flat, -1.0, None, ALU.mult).then_inc(a.high_ready, 1)
                    dve.wait_ge(a.high_ready, high_ready.next())
                    dve.scalar_tensor_tensor(out=max_parts[:, 1, :], in0=flat, scalar=-1.0, in1=max_parts[:, 0, :].bitcast(F32),
                                             op0=ALU.mult, op1=ALU.subtract).then_inc(a.parts_ready, 1)
                    tile = next_tile()
                    if last_use:
                        dve.wait_ge(*last_use)
                    dve.tensor_copy(max_rows[:], tile[:, 0:P]).then_inc(a.tile_done, 1)

                def inverse(c, m):
                    part = sum_inv[:, P * m:P * (m + 1)]
                    if m == 0:
                        dve.wait_ge(a.chunk_free, chunk_free.next())
                    ins = dve.reciprocal(part, part)
                    if m == CB - 1:
                        ins.then_inc(a.inverted, 1)

                def scale(g, c):
                    dve.wait_ge(a.inverted, inverted.next())
                    part = attended[:, g, BANK * c:BANK * (c + 1)]
                    dve.tensor_tensor(part, part, sum_inv[:], ALU.mult).then_inc(a.inverse_ready, 1)

                def turn(g, c, i):
                    tile = next_tile()[:, 0:BANK].rearrange("p (m h v) -> p m h v", m=CB, h=GROUP)
                    dve.wait_ge(a.tile_done, tile_done.base + tile_done.n - 1)
                    dve.reciprocal(turn_inv[:], tile[:, :, :, HD2:HD2 + 1]).then_inc(a.inverse_ready, 1)
                    dve.wait_ge(a.inverse_ready, inverse_ready.next())
                    out = x[:, bass.ds(i * SB + CB * c, CB), P // GROUP * g:P // GROUP * (g + 1)]
                    for m in range(CB):
                        ins = dve.tensor_tensor(out[:, m, :].rearrange("p (h v) -> p h v", h=GROUP), tile[:, m, :, 0:HD2],
                                                turn_inv[:, m, :, :].broadcast_to([P, GROUP, HD2]), ALU.mult)
                    ins.then_inc(a.tile_done, 1)

                inverse_ready = Tally(a.inverse_ready, 3, 2 * GROUPS)
                if a.queries:
                    queries(None)
                    for g in range(1, a.ahead):
                        queries((a.stack_in[g - 1], 16 * a.q_dmas))
                for heads, qb in max_items():
                    max_scores(heads, qb)
                max_to_rows(None)
                tile_ready.start += a.first_tiles
                tile_done.start += a.first_tiles
                high_ready.start += 4 if a.queries else 1

                def slots(i, last):
                    for tally in (tile_ready, tile_done, high_ready, inverse_ready, inverted, chunk_free):
                        tally.turn(i)
                    for g, kind, what, quad in pass_steps(a, last):
                        if kind == "queries":
                            queries((a.stack_in[(g + 2) % RING], 16 * a.q_dmas * (i + (1 if g < 2 else 2))))
                        elif kind == "max":
                            max_scores(*what)
                        elif kind == "max rows":
                            max_to_rows((a.max_in[g], 32 * (i + 1)))
                        elif kind == "inverse":
                            inverse(*what)
                        elif kind == "scale":
                            scale(g, what)
                        elif kind == "turn":
                            turn(g, what, i)
                        elif kind == "project":
                            tile = next_tile()
                            dve.tensor_copy(xn[:, bass.ds(i * SB + CB * what, CB), :],
                                            tile[:, 0:BANK].rearrange("p (n o) -> p n o", o=DIM)).then_inc(a.tile_done, 1)

                passes(dve, slots)

            attention(a1)

            dve.wait_ge(a1.tile_done, 2 + A1_TILES)
            dve.memset(v_tokens[:], 1.0).then_inc(v_ones, 1)
            for b in range(BATCH):
                norm_stats(xn, b)
                norm_apply(xn, xn, b)
                part = blocks_of(b)
                dve.tensor_tensor(x[:, part, :], x[:, part, :], xn[:, part, :], ALU.add).then_inc(x1_ready, SB)
                dve.wait_ge(x1_ready, SB * (b + 1))
                norm_stats(x, b)
                norm_apply(xn, x, b)
                norm_stats(xn, b)
                dve.wait_ge(x1_stored, 16 * (b + 1))
                norm_apply(x, xn, b)
                gain_and_bias(x, b, affine1, h_ready)
                dve.wait_ge(mid_loaded, 48)
                dve.wait_ge(qk_drained, 4 * (b + 1))
                halves = [v[:].rearrange("p n (s two j) -> p n s two j", two=2, j=HD2 // 2) for v in (qk_raw, qk)]
                shape = [P, SB, 2 * HEADS, HD2 // 2]
                cos, sin = (rope[:, k, :, :].unsqueeze(2).broadcast_to(shape) for k in range(2))
                part_a, part_b = (rope_part[:, k, :, :].rearrange("p n (s j) -> p n s j", j=HD2 // 2) for k in range(2))
                t1, t2 = halves[0][:, :, :, 0, :], halves[0][:, :, :, 1, :]
                if b:
                    dve.wait_ge(mid_ready, 7 * b)
                dve.tensor_tensor(part_a, t1, cos, ALU.mult)
                link(dve.tensor_tensor(part_b, t2, sin, ALU.mult))
                link(dve.tensor_tensor(halves[1][:, :, :, 0, :], part_a, part_b, ALU.subtract))
                dve.tensor_tensor(part_a, t1, sin, ALU.mult)
                link(dve.tensor_tensor(part_b, t2, cos, ALU.mult))
                dve.tensor_tensor(halves[1][:, :, :, 1, :], part_a, part_b, ALU.add).then_inc(qk_turned, 1)
                if b:
                    dve.wait_ge(qk_stored, 16 * 4 * b)
                for w in range(2):
                    dve.wait_ge(qk_rounded, 2 * b + w + 1)
                    dve.tensor_tensor(qk_low[:, w, :], tile_ps[:, (7 * b + 5 + w) % 2, :],
                                      qk_high[:, w, :].bitcast(F32), ALU.subtract).then_inc(mid_dve, 1)
            dve.wait_ge(qk_stored, 16 * 4 * BATCH)
            dve.wait_ge(stack_cleared, 2)
            for r in (0, 1):
                dve.memset(k_stack2[:, r].rearrange("p h q -> p (h q)").bitcast(F32), 1.0).then_inc(stack_cleared, 1)
            dve.memset(value_ps[:], 0.0).then_inc(cleared, 1)
            dve.wait_ge(cleared, 1)

            attention(a2)

            dve.wait_ge(a2.tile_done, 2 + A2_TILES)
            dve.memset(zeros[:], 0.0).then_inc(zeroed_src, 1)
            dve.wait_ge(late_loaded, 80)
            for e in range(EXPERTS):
                dve.memset(rank[:, :, e], float(EXPERTS - e))
                ins = dve.memset(first_slot[:, :, e], float(CAPACITY * e - 1))
            link(ins)
            for b in range(BATCH):
                part = blocks_of(b)
                dve.wait_ge(post_ready, 3 * b + 2)
                tile = tile_ps[:, (3 * b + 1) % 2, :].rearrange("p (n o) -> p n o", o=DIM)
                dve.tensor_tensor(xn[:, part, :], tile, xn[:, part, :], ALU.add).then_inc(post_dve, 1)
                dve.wait_ge(post_dve, b + 1)
                norm_stats(xn, b)
                norm_apply(x, xn, b)
                gain_and_bias(x, b, affine2, h2_ready)

            r0, r1, r2 = (r[:] for r in route)

            def wide(v):
                return v.unsqueeze(2).broadcast_to([P, BLOCKS, EXPERTS])

            dve.wait_ge(logits_ready, 1)
            logits = value_ps[:, 0:BLOCKS * EXPERTS].rearrange("p (n e) -> p n e", e=EXPERTS)
            link(dve.tensor_reduce(row_value[:], logits, AX.X, ALU.max))
            dve.tensor_tensor(r0, logits, wide(row_value[:]), ALU.subtract).then_inc(exp_in, 1)
            dve.wait_ge(exp_out, 1)
            link(dve.tensor_reduce(row_value[:], gates[:], AX.X, ALU.add))
            link(dve.reciprocal(row_value[:], row_value[:]))
            link(dve.tensor_tensor(gates[:], gates[:], wide(row_value[:]), ALU.mult))
            left = gates[:]
            for k in range(TOPK):
                link(dve.tensor_reduce(row_value[:], left, AX.X, ALU.max))
                link(dve.tensor_tensor(r2, left, wide(row_value[:]), ALU.is_equal))
                link(dve.tensor_tensor(r2, r2, rank[:], ALU.mult))
                link(dve.tensor_reduce(row_value[:], r2, AX.X, ALU.max))
                link(dve.tensor_tensor(chosen[k][:], r2, wide(row_value[:]), ALU.is_equal))
                if k == 0:
                    link(dve.tensor_tensor(r1, gates[:], chosen[0][:], ALU.mult))
                    link(dve.tensor_tensor(r1, gates[:], r1, ALU.subtract))
                    link(dve.tensor_tensor(r1, r1, chosen[0][:], ALU.subtract))
                    left = r1
            dve.tensor_tensor(r0, chosen[0][:], chosen[1][:], ALU.add).then_inc(mask_ready, 1)
            dve.wait_ge(count_ready, 2)
            totals = sum_ps[:, 0:BLOCKS * EXPERTS].rearrange("p (n e) -> p e n", e=EXPERTS)
            link(dve.tensor_copy(taken[:], totals))
            by_expert = r2.rearrange("p n e -> p e n")
            for e in range(EXPERTS):
                ins = dve.tensor_tensor_scan(by_expert[:, e, :], ones[:, 0:BLOCKS], taken[:, e, :], 0.0, ALU.mult, ALU.add)
            link(ins)
            link(dve.tensor_tensor(by_expert, by_expert, taken[:], ALU.subtract))
            counts = value_ps[:, 0:BLOCKS * EXPERTS].rearrange("p (n e) -> p n e", e=EXPERTS)
            link(dve.tensor_tensor(r1, counts, r2, ALU.add))
            link(dve.tensor_scalar(r2, r1, float(CAPACITY), None, ALU.is_le))
            link(dve.tensor_tensor(r1, r1, first_slot[:], ALU.add))
            for k in range(TOPK):
                for out, what in ((slot_of, r1), (kept, r2), (gate_of, gates[:])):
                    link(dve.tensor_tensor(r0, chosen[k][:], what, ALU.mult))
                    link(dve.tensor_reduce(out[:, k, :], r0, AX.X, ALU.add))
            link(dve.tensor_tensor(gate_of[:], gate_of[:], kept[:], ALU.mult))
            link(dve.tensor_tensor(slot_of[:], slot_of[:], kept[:], ALU.mult))
            link(dve.tensor_copy(get_at[:], slot_of[:]))
            link(dve.tensor_scalar(kept[:], kept[:], -float(EXPERTS * CAPACITY), float(EXPERTS * CAPACITY), ALU.mult, ALU.add))
            link(dve.tensor_tensor(slot_of[:], slot_of[:], kept[:], ALU.add))
            dve.tensor_copy(put_at[:], slot_of[:]).then_inc(routed, 1)

            dve.wait_ge(count_ready, 3)
            dve.tensor_copy(b1[:].rearrange("p e f -> p (e f)"), score_ps[:, 0, 0:EXPERTS * HIDDEN // P]).then_inc(b1_turned, 1)

            def expert_turned(e):
                dve.wait_ge(e_turned, e + 1)
                dve.tensor_copy(expert_in_t[:, e % 2, :], tile_ps[:, 0, :]).then_inc(e_turned_done, 1)

            expert_turned(0)
            for e in range(EXPERTS):
                if e + 1 < EXPERTS:
                    if e:
                        dve.wait_ge(hid_ready, 8 * e)
                    expert_turned(e + 1)
                dve.wait_ge(out_ready, 2 * (e + 1))
                if e >= 2:
                    dve.wait_ge(out_stored[e % 2], 16 * (e // 2))
                dve.wait_ge(w_in2[e % 2], 48 * (e // 2 + 1))
                dve.tensor_tensor(expert_out[:, e % 2, :, :], tile_ps[:, 1, :].rearrange("p (n d) -> p n d", d=DIM),
                                  b2[:, e % 2, :].unsqueeze(1).broadcast_to([P, SB, DIM]), ALU.add).then_inc(out_done, 1)
            dve.wait_ge(gathered, 16 * TOPK * BLOCKS)
            dve.wait_ge(x1_loaded, 16 * BATCH)
            for k in range(TOPK):
                for n in range(BLOCKS):
                    ins = dve.scalar_tensor_tensor(out=xn[:, n, :], in0=fetched[:, k, n, :], scalar=gate_of[:, k, n:n + 1],
                                                   in1=xn[:, n, :], op0=ALU.mult, op1=ALU.add)
                link(ins)
            for b in range(BATCH):
                norm_stats(xn, b)
                norm_apply(xn, xn, b)
                part = blocks_of(b)
                dve.tensor_tensor(x[:, part, :], x1_back[:, part, :], xn[:, part, :], ALU.add).then_inc(final_ready, SB)


def rope_tables():
    import numpy as np

    freq = (1.0 / np.float32(10000.0) ** (np.arange(0, HD2, 2, dtype=np.float32) / np.float32(HD2))).astype(np.float32)
    angle = np.arange(SEQ, dtype=np.float32)[:, None] * freq
    return np.cos(angle).astype(np.float32), np.sin(angle).astype(np.float32)


_INS = {
    "x": "L0_attn_x_bld", "wq": "L0_attn_Wq", "wdown": "L0_attn_Wkv_down", "wk": "L0_attn_Wk_up",
    "wv": "L0_attn_Wv_up", "wout": "L0_attn_Wout", "ln1_g": "L0_ffn_ln1_g", "ln1_b": "L0_ffn_ln1_b",
    "wqkv": "L0_ffn_Wqkv", "wproj": "L0_ffn_Wproj", "ln2_g": "L0_ffn_ln2_g", "ln2_b": "L0_ffn_ln2_b",
    "wgate": "L0_ffn_Wgate", "w1": "L0_ffn_W1", "b1": "L0_ffn_b1", "w2": "L0_ffn_W2", "b2": "L0_ffn_b2",
}


def kernel(**inputs):
    import numpy as np
    import concourse.bacc as bacc
    from concourse.bass_utils import run_bass_kernel_spmd

    nc = bacc.Bacc("TRN2", target_bir_lowering=False, num_devices=1)
    arrays = {f"in_{k}": np.ascontiguousarray(inputs[name]) for k, name in _INS.items()}
    arrays["in_rope_cos"], arrays["in_rope_sin"] = rope_tables()
    t = {k[3:]: nc.dram_tensor(k, a.shape, F32, kind="ExternalInput").ap() for k, a in arrays.items()}
    t["out"] = nc.dram_tensor("out", [BATCH, SEQ, DIM], F32, kind="ExternalOutput").ap()
    build(nc, t)
    got = run_bass_kernel_spmd(nc, [arrays], core_ids=[0])
    return got.results[0]["out"]
```

```python
from contextlib import ExitStack

import concourse.bass as bass
from concourse import mybir

F32 = mybir.dt.float32
F32R = mybir.dt.float32r
BF16 = mybir.dt.bfloat16
U32 = mybir.dt.uint32
ALU = mybir.AluOpType
ACT = mybir.ActivationFunctionType
AX = mybir.AxisListType

P = 128
BANK = 512
BATCH, SEQ, DIM = 4, 1024, 128
TOK = BATCH * SEQ
BLOCKS = TOK // P
SB = SEQ // P
CHUNKS = SEQ // BANK
CB = BANK // P
HEADS, LATENT, KDIM = 16, 32, 64
GROUP = 4
GROUPS = HEADS // GROUP
SLOTS = BATCH * GROUPS
HD2 = DIM // HEADS
QKV = 3 * HD2
EXPERTS, HIDDEN, TOPK = 8, 512, 2
CAPACITY = 2 * TOK // EXPERTS
EPS = 1e-5
MASKED = -2.0 ** 126
STACK = 96
ROWS = STACK + 2
RING = 4
UNITS = 12 * GROUP
M_ITEMS = 24
M_PASS = 4 * (M_ITEMS + 2) + 2


class Tally:

    def __init__(self, sem, start=0, per=0, short=0):
        self.sem, self.start, self.per, self.short = sem, start, per, short
        self.base, self.n = start, 0

    def turn(self, i, first=False):
        self.base, self.n = self.start if first else self.start + i * self.per - self.short, 0

    def here(self):
        return self.base + self.n

    def loop_from_1(self, per):
        self.start, self.per = self.base + self.n - per, per

    def next(self, k=1):
        self.n += k
        return self.base + self.n


def key_blocks(c):
    return [(kb, max(0, kb - CB * c) * P) for kb in range(CB * (c + 1))]


def max_items():
    short = [((h, h + 1), qb) for qb in range(CB) for h in (0, 2)]
    long = [((h,), qb) for qb in range(CB, SB) for h in range(GROUP)]
    return short + long


NORM_STEPS = 3 * 5 + 1
NORM_LINKS = 3 * (1 + 1 + 5 + 1) + 1


def norm_steps():
    steps = [("norm", (piece, r)) for r in range(3) for piece in ("stats", "moments", "root", "newton", "apply")]
    return steps + [("norm", ("gain", 2))]


def post_steps():
    steps = [("post", (name, half)) for name, half in (("turn x", 0), ("project", 0), ("project", 1))]
    steps += [("norm", (piece, 0)) for piece in ("stats", "moments", "root", "newton", "apply", "gain")]
    steps += [("post", (name, 0)) for name in ("turn h", "logits", "exp", "choose", "choose more", "count", "place")]
    for k in range(TOPK):
        steps += [("post", ("ids", k))] + [("post", ("scatter", (k, m))) for m in range(SB)]
    return steps


POST_TILED = ("turn x", "project", "turn h", "logits", "count")
POST_LINKS = (8 + 1) + 1 + (3 + 5 + 3) + 5 + 3 + (6 * TOPK + 4) + 1


def pass_steps(layer, first, last):
    quads = [(c, kb, off) for c in range(CHUNKS) for kb, off in key_blocks(c)]
    steps, after = [], []
    side = [(0, *step, None) for step in (norm_steps() if layer.queries else post_steps())] if not first else []
    every = 3 if layer.queries else 2
    turn = 0

    def finish(g, c):
        if layer.sums:
            return [(g, "inverse", (c, m), None) for m in range(CB)] + [(g, "scale", c, None)]
        return [(g, "turn", c, None)]

    for g in range(GROUPS):
        next_max = not (last and g == GROUPS - 1)
        items, done = max_items() if next_max else [], 0
        places = 2 * (len(quads) - 1) - 1
        for n, quad in enumerate(quads):
            for h in range(GROUP):
                steps.append((g, "score", (quad, h), n))
                if h % 2:
                    place = 2 * n + h // 2 + 1
                    want = min(len(items), -(-place * len(items) // places))
                    for item in items[done:want]:
                        steps.append((g, "max", item, None))
                        turn += 1
                        if after:
                            steps.append(after.pop(0))
                        elif side and turn % every == 0:
                            steps.append(side.pop(0))
                    done = want
                    if not next_max and after + side:
                        steps.append((after or side).pop(0))
                    if next_max and place == places + 1:
                        steps.append((g, "max rows", None, None))
                        if layer.queries and not (last and g >= 1):
                            steps.append((g, "queries", None, None))
                if h == 2 and n:
                    steps.append((g, "values", quads[n - 1], n - 1))
                if h == 3 and n:
                    if layer.sums:
                        steps.append((g, "sums", quads[n - 1], n - 1))
                    if quads[n - 1][0] != quad[0]:
                        steps.append((g, "drain", quads[n - 1][0], None))
                        after = after + finish(g, quads[n - 1][0])
        steps.append((g, "values", quads[-1], len(quads) - 1))
        if layer.sums:
            steps.append((g, "sums", quads[-1], len(quads) - 1))
        steps.append((g, "drain", CHUNKS - 1, None))
        steps += after
        after = finish(g, CHUNKS - 1)
    steps += after + side
    if layer.queries:
        steps += [(g, "project", half, None) for half in range(2)]
    return steps


def tiled(kind, what):
    return kind in ("queries", "max", "max rows", "turn", "project") or kind == "post" and what[0] in POST_TILED


class Layer:

    def __init__(self, name, scale, sums, v_width, q_dmas, sem):
        self.scale, self.sums, self.turns, self.v_width, self.q_dmas = scale, sums, not sums, v_width, q_dmas
        self.queries = sums
        self.ahead = 3 if self.queries else 2
        count = [sum(tiled(kind, what) for _, kind, what, _ in pass_steps(self, first, last))
                 for first, last in ((True, False), (False, False), (False, True))]
        self.pass_tiles, self.short = count[1], count[1] - count[0]
        assert self.pass_tiles % 2 == 0
        self.first_tiles = M_ITEMS + 1 + (3 if sums else 0)
        self.all_tiles = self.first_tiles + count[0] + (BATCH - 2) * count[1] + count[2]
        self.tile_ready = sem(f"{name}_tile_ready")
        self.tile_done = sem(f"{name}_tile_done")
        self.scores_ready = sem(f"{name}_scores_ready")
        self.probs_ready = sem(f"{name}_probs_ready")
        self.quad_done = sem(f"{name}_quad_done")
        self.inverse_ready = sem(f"{name}_inverse_ready")
        self.inverted = sem(f"{name}_inverted")
        self.chunk_free = sem(f"{name}_chunk_free")
        self.high_ready = sem(f"{name}_high_ready")
        self.masked = sem(f"{name}_masked")
        self.max_turn = sem(f"{name}_max_turn")
        self.mask_turn = sem(f"{name}_mask_turn")
        self.parts_ready = sem(f"{name}_parts_ready")
        self.stack_in = [sem(f"{name}_stack_in{r}") for r in range(RING)]
        self.max_in = [sem(f"{name}_max_in{r}") for r in range(RING)]


def build(nc, t, dump=None):
    with ExitStack() as ctx:
        tensors = {}

        def sb(name, shape, dt=F32, scope=ctx):
            tensors[name] = scope.enter_context(nc.sbuf_tensor(name, shape, dt))
            return tensors[name]

        def sem(name):
            return ctx.enter_context(nc.semaphore(name))

        tile_ps = ctx.enter_context(nc.psum_tensor("tile_ps", [P, 2, 2 * BANK], F32))
        score_ps = ctx.enter_context(nc.psum_tensor("score_ps", [P, 2, BANK], F32))
        value_ps = ctx.enter_context(nc.psum_tensor("value_ps", [P, BANK], F32))
        sum_ps = ctx.enter_context(nc.psum_tensor("sum_ps", [P, BANK], F32))

        ident = sb("ident", [P, P])
        late_key = sb("late_key", [P, SEQ], BF16)
        upper = sb("upper", [P, P])
        ones = sb("ones", [P, P])
        affine1 = sb("affine1", [P, 2, DIM])

        x = sb("x", [P, BLOCKS, DIM])
        xn = sb("xn", [P, BLOCKS, DIM])
        stats = sb("stats", [P, SB, 6])
        mean_var = sb("mean_var", [P, SB, 2])
        var_eps = sb("var_eps", [P, SB])
        root = sb("root", [P, SB])
        rstd = sb("rstd", [P, SB])
        newton = sb("newton", [P, SB])
        gate_of = sb("gate_of", [P, TOPK, BLOCKS])
        token_no = sb("token_no", [P, SB])

        both = ctx.enter_context(ExitStack())
        q_stack = sb("q_stack", [P, RING, GROUP, SEQ], F32R, both)
        probs = sb("probs", [P, 8, BANK], F32, both)
        sum_inv = sb("sum_inv", [P, BANK], F32, both)
        turn_inv = sb("turn_inv", [P, CB, GROUP, 1], F32, both)
        max_of = sb("max_of", [P, GROUP, SB], F32, both)
        max_parts = sb("max_parts", [P, 4, GROUP * SB], F32R, both)
        max_rows = sb("max_rows", [P, P], F32R, both)

        with ExitStack() as first:
            xn_t = sb("xn_t", [P, TOK], F32, first)
            k_stack1 = sb("k_stack1", [P, RING, SEQ], F32R, first)
            v_blocks1 = sb("v_blocks1", [P, RING, SB, LATENT], F32, first)
            latent = sb("latent", [P, TOK], F32R, first)
            latent_rows = sb("latent_rows", [P, BLOCKS, LATENT], F32, first)
            q_high = sb("q_high", [P, SEQ], F32R, first)
            q_low = sb("q_low", [P, SEQ], F32R, first)
            attended = sb("attended", [P, GROUPS, SEQ], F32, first)
            down3 = sb("down3", [P, 3, LATENT], F32, first)
            absorbed_q = sb("absorbed_q", [P, HEADS * LATENT], F32, first)
            absorbed_o = sb("absorbed_o", [P, GROUPS, DIM], F32, first)
        w_in = attended
        wq_raw, wout_raw = w_in[:, 0, :], w_in[:, 1, :].rearrange("p (g o) -> p g o", g=8)
        wk_raw, wv_raw = w_in[0:LATENT, 2, :], w_in[0:LATENT, 3, :]
        wq_t = probs[:, 0:2, :].rearrange("p a (g d) -> p (a g) d", g=4)
        wkv_t = probs[:, 2, :].rearrange("p (w g c) -> p w g c", w=2, g=8)

        second = ctx.enter_context(ExitStack())
        v_tokens = sb("v_tokens", [P, BLOCKS, HEADS, HD2 + 1], F32, second)
        v_blocks2 = sb("v_blocks2", [P, RING, SB, GROUP, HD2 + 1], F32, second)
        with ExitStack() as between:
            h_t = sb("h_t", [P, SEQ], F32, between)
            wqkv = sb("wqkv", [P, 3 * DIM], F32, between)
            rope = sb("rope", [P, 2, SB, HD2 // 2], F32, between)
            qk_raw = sb("qk_raw", [P, 2, SB, 2 * DIM], F32, between)
            qk = sb("qk", [P, 2, SB, 2 * DIM], F32, between)
            rope_part = sb("rope_part", [P, 2, SB, 2 * DIM // 2], F32, between)
            qk_high = sb("qk_high", [P, 2, SEQ], F32R, between)
            qk_low = sb("qk_low", [P, 2, SEQ], F32R, between)
        k_stack2 = sb("k_stack2", [P, RING, GROUP, SEQ], F32R, second)
        second.close()
        both.close()

        room = x[:, 0:SB * (BATCH - 1), :].rearrange("p n d -> p (n d)")
        taken = 0

        def cut(columns):
            nonlocal taken
            taken += columns
            assert taken <= SB * (BATCH - 1) * DIM
            return room[:, taken - columns:taken]

        def routing(columns):
            return cut(columns * EXPERTS).rearrange("p (n e) -> p n e", e=EXPERTS)

        turned = cut(SEQ)
        h2_rows = cut(SB * (DIM + 1)).rearrange("p (n d) -> p n d", n=SB)
        wproj, wgate = cut(DIM), cut(EXPERTS)
        gates, rank, first_slot, r0, r1, r2 = (routing(SB) for _ in range(6))
        chosen = [routing(SB) for _ in range(TOPK)]
        mask = routing(SB + 1)
        before = routing(1)
        row_value = cut(SB)
        slot_of, kept, gate_part, put_at = (cut(TOPK * SB).rearrange("p (k n) -> p k n", k=TOPK) for _ in range(4))
        put_at = put_at.bitcast(U32)
        attn = x[:, SB * (BATCH - 1):, :]
        affine2 = affine1

        last_part = ctx.enter_context(ExitStack())
        w1 = sb("w1", [P, 2, HIDDEN], F32, last_part)
        w2 = sb("w2", [P, 2, HIDDEN // P, DIM], F32, last_part)
        b1_rows = sb("b1_rows", [EXPERTS * HIDDEN // P, P], F32, last_part)
        b1 = sb("b1", [P, EXPERTS, HIDDEN // P], F32, last_part)
        b2 = sb("b2", [P, 2, DIM], F32, last_part)
        expert_in = sb("expert_in", [P, 2, SB, DIM + 1], F32, last_part)
        sent_back = sb("sent_back", [P, 2, SB], F32, last_part)
        out_at = sb("out_at", [P, EXPERTS, SB], U32, last_part)
        expert_in_t = sb("expert_in_t", [P, 2, CAPACITY], F32, last_part)
        hidden = sb("hidden", [P, 2, HIDDEN // P, BANK], F32, last_part)
        expert_out = sb("expert_out", [P, 2, SB, DIM], F32, last_part)
        fetched = sb("fetched", [P, TOPK, BLOCKS, DIM], F32, last_part)
        x1_back = sb("x1_back", [P, BLOCKS, DIM], F32, last_part)

        x1_dram = nc.dram_tensor("x1_scratch", [BATCH, SEQ, DIM], F32).ap()
        q_dram = nc.dram_tensor("q_scratch", [BATCH, 2, HEADS, HD2, SEQ], F32).ap()
        k_dram = nc.dram_tensor("k_scratch", [BATCH, 2, HEADS, HD2, SEQ], F32).ap()
        slots_in = nc.dram_tensor("slots_in", [EXPERTS * CAPACITY, DIM + 1], F32).ap()
        token_out = nc.dram_tensor("token_out", [TOPK * TOK, DIM], F32).ap()

        def tokens(dram, b):
            return dram[b].rearrange("(n p) d -> p n d", p=P)

        def blocks_of(b):
            return slice(SB * b, SB * (b + 1))

        x_in = [sem(f"x_in{b}") for b in range(BATCH)]
        w_loaded, consts, ones_rows = sem("w_loaded"), sem("consts"), sem("ones_rows")
        sp_turn = sem("sp_turn")
        dve_step, dve_turn = sem("dve_step"), sem("dve_turn")
        var_ready, root_ready, normed = sem("var_ready"), sem("root_ready"), sem("normed")
        pre_ready, pre_done, high_written = sem("pre_ready"), sem("pre_done"), sem("high_written")
        stored = sem("stored")
        a1 = Layer("a1", KDIM ** -0.5, True, LATENT, 3 * GROUP + 2, sem)
        a2 = Layer("a2", HD2 ** -0.5, False, HD2 + 1, 9, sem)
        a1.k_stack, a1.v_blocks = k_stack1, v_blocks1
        a2.k_stack, a2.v_blocks = k_stack2, v_blocks2
        PRE_TILES = 13
        QUADS = 12
        A1_TILES, A2_TILES = a1.all_tiles, a2.all_tiles

        mid_tiles = []
        for b in range(BATCH + 1):
            if b < BATCH:
                mid_tiles += [("h", b, 0)] + [("qkv", b, k) for k in range(4)]
            if b:
                mid_tiles += [("qk", b - 1, w) for w in range(2)]

        x1_ready, x1_stored, h_ready = sem("x1_ready"), sem("x1_stored"), sem("h_ready")
        mid_loaded = sem("mid_loaded")
        mid_ready, mid_act, mid_dve = sem("mid_ready"), sem("mid_act"), sem("mid_dve")
        qk_drained, qk_turned, qk_rounded = sem("qk_drained"), sem("qk_turned"), sem("qk_rounded")
        qk_stored = sem("qk_stored")
        cleared = sem("cleared")
        v_ones, stack_cleared = sem("v_ones"), sem("stack_cleared")
        late_loaded, b1_loaded = sem("late_loaded"), sem("b1_loaded")
        h2_ready, exp_in, exp_out, mask_ready = sem("h2_ready"), sem("exp_in"), sem("exp_out"), sem("mask_ready")
        zeroed, ids_ready, scattered, pool_turn = sem("zeroed"), sem("ids_ready"), sem("scattered"), sem("pool_turn")
        w_in2 = [sem(f"expert_w{k}") for k in range(2)]
        e_in = [sem(f"expert_in{k}") for k in range(2)]
        e_turned, e_turned_done = sem("expert_turned"), sem("expert_turned_done")
        hid_ready, hid_done, out_ready = sem("hidden_ready"), sem("hidden_done"), sem("out_ready")
        out_done, out_stored = sem("out_done"), [sem(f"out_stored{k}") for k in range(2)]
        b1_ready, b1_turned = sem("b1_ready"), sem("b1_turned")
        fetched_in = [sem(f"fetched_in{b}") for b in range(BATCH)]
        x1_loaded, final_ready = sem("x1_loaded"), sem("final_ready")

        def mid_at(kind, b, k):
            return mid_tiles.index((kind, b, k))

        block = ctx.enter_context(nc.Block())

        def passes(eng, do):
            do(0, True, False)
            with eng.Fori(1, BATCH - 1) as i:
                do(i, False, False)
            do(BATCH - 1, False, True)

        @block.gpsimd
        def _(pool):
            pool.memset(ident[:], 0.0).then_inc(consts, 1)
            pool.memset(late_key[:], 0.0).then_inc(consts, 1)
            pool.memset(upper[:], 1.0).then_inc(consts, 1)
            pool.memset(ones[:], 1.0).then_inc(consts, 1)
            pool.iota(token_no[:], [[P, SB]], base=1, channel_multiplier=1,
                      allow_small_or_imprecise_dtypes=True).then_inc(consts, 1)
            pool.wait_ge(consts, 5)
            pool.affine_select(out=ident[:], in_=ident[:], compare_op=ALU.not_equal, fill=1.0, base=0,
                               pattern=[[-1, P]], channel_multiplier=1).then_inc(consts, 1)
            diagonal = late_key[:, SEQ - P:]
            pool.affine_select(out=diagonal, in_=diagonal, compare_op=ALU.is_ge, fill=MASKED, base=0,
                               pattern=[[-1, P]], channel_multiplier=1).then_inc(consts, 1)
            pool.affine_select(out=upper[:], in_=upper[:], compare_op=ALU.is_ge, fill=0.0,
                               base=0, pattern=[[1, P]], channel_multiplier=-1).then_inc(consts, 1)
            pool.wait_ge(consts, 8)
            pool.memset(latent[STACK:P, :].bitcast(F32), 1.0).then_inc(ones_rows, 1)

            def mask(a):
                probs_ready = Tally(a.probs_ready, 2, UNITS * GROUPS)

                def slots(i, first, last):
                    probs_ready.turn(i)
                    for g, kind, what, quad in pass_steps(a, first, last):
                        if kind == "post" and what[0] == "scatter":
                            scatter(*what[1], i - 1)
                        if kind != "score" or what[1] < GROUP - 1:
                            continue
                        (c, kb, off), _ = what
                        exps = probs_ready.next(GROUP)
                        if kb >= CB * c:
                            pool.wait_ge(a.probs_ready, exps)
                            pool.sem_inc(a.mask_turn, 1)
                            part = probs[:, GROUP * (quad % 2):GROUP * (quad % 2 + 1), off:off + P]
                            pool.affine_select(out=part, in_=part, compare_op=ALU.is_ge, fill=0.0, base=0,
                                               pattern=[[0, GROUP], [1, P]], channel_multiplier=-1).then_inc(a.masked, 1)

                passes(pool, slots)

            def scatter(k, m, b):
                if m == 0:
                    pool.wait_ge(ids_ready, TOPK * b + k + 1)
                    pool.sem_inc(pool_turn, 1)
                pool.indirect_dma_start(
                    out=slots_in, out_offset=bass.IndirectOffsetOnAxis(ap=put_at[:, k, m:m + 1], axis=0),
                    in_=h2_rows[:, m, :], in_offset=None, bounds_check=EXPERTS * CAPACITY - 1,
                    oob_is_err=False).then_inc(scattered, 16)

            mask(a1)
            pool.wait_ge(a1.tile_done, 2 + A1_TILES)
            for rows in (slice(LATENT, 2 * LATENT), slice(2 * LATENT, P)):
                pool.memset(q_stack[rows].rearrange("p r h q -> p (r h q)").bitcast(F32), 0.0).then_inc(stack_cleared, 1)
            pool.wait_ge(qk_stored, 16 * 4 * BATCH)
            pool.wait_ge(stack_cleared, 2)
            for r in (2, 3):
                pool.memset(k_stack2[:, r].rearrange("p h q -> p (h q)").bitcast(F32), 1.0).then_inc(stack_cleared, 1)
            pool.wait_ge(zeroed, 16 * 9)
            mask(a2)
            for _, (name, what) in post_steps():
                if name == "scatter":
                    scatter(*what, BATCH - 1)
            for e in range(EXPERTS):
                pool.wait_ge(out_done, e + 1)
                for m in range(SB):
                    pool.indirect_dma_start(
                        out=token_out, out_offset=bass.IndirectOffsetOnAxis(ap=out_at[:, e, m:m + 1], axis=0),
                        in_=expert_out[:, e % 2, m, :], in_offset=None, bounds_check=TOPK * TOK - 1,
                        oob_is_err=False).then_inc(out_stored[e % 2], 16)

        @block.sync
        def _(sp):
            for b in range(BATCH):
                sp.dma_start(x[:, blocks_of(b), :], tokens(t["x"], b)).then_inc(x_in[b], 16)
                if b == 0:
                    sp.dma_start(wq_raw, t["wq"].rearrange("d h k -> d (h k)")).then_inc(w_loaded, 16)
                    sp.dma_start(wk_raw, t["wk"].rearrange("c h k -> c (h k)")).then_inc(w_loaded, 16)
                    sp.dma_start(wv_raw, t["wv"].rearrange("c h k -> c (h k)")).then_inc(w_loaded, 16)
                    sp.dma_start(wout_raw, t["wout"].rearrange("(g two) k o -> (two k) g o", two=2)).then_inc(w_loaded, 16)
                    for r in range(3):
                        sp.dma_start(down3[:, r, :], t["wdown"]).then_inc(w_loaded, 16)
            for k, name in enumerate(("ln1_g", "ln1_b")):
                sp.dma_start(affine1[:, k, :], t[name].partition_broadcast(P)).then_inc(w_loaded, 16)

            def max_rows_in(a, r):
                for part in range(2):
                    n = GROUP * SB
                    sp.dma_start(q_stack[STACK + part:STACK + part + 1, r, :, :].bitcast(F32)
                                 .rearrange("p h (n q) -> p (h n) q", q=P),
                                 max_rows[n * part:n * (part + 1), :].bitcast(F32)).then_inc(a.max_in[r], 16)

            def store_x1(b):
                sp.wait_ge(x1_ready, SB * b + SB)
                sp.sem_inc(sp_turn, 1)
                sp.dma_start(x1_dram[bass.ds(b, 1)].rearrange("one (n p) d -> p (one n) d", p=P),
                             x[:, bass.ds(b * SB, SB), :]).then_inc(x1_stored, 16)

            def slots_of(a, stack_in):
                tile_done = Tally(a.tile_done, 2, a.pass_tiles, a.short)
                for g in range(a.ahead):
                    if a.queries:
                        sp.wait_ge(a.tile_done, tile_done.next())
                    stack_in(g, 0)
                sp.wait_ge(a.tile_done, tile_done.next(M_ITEMS + 1))
                max_rows_in(a, 0)
                if not a.queries:
                    router_in()
                    zero_slots()
                tile_done.start += a.first_tiles

                def slots(i, first, last):
                    tile_done.turn(i, first)
                    at = -1
                    for g, kind, what, _ in pass_steps(a, first, last):
                        done = tile_done.next() if tiled(kind, what) else None
                        if kind == "queries":
                            sp.wait_ge(a.tile_done, done)
                            stack_in((g + 3) % GROUPS, i if g < 1 else i + 1)
                        elif not a.queries and g > at and not (last and g >= 2):
                            sp.wait_ge(a.inverse_ready, 2 * GROUPS * i + 2 * g + 1)
                            stack_in((g + 2) % GROUPS, i if g < 2 else i + 1)
                        if kind == "max rows":
                            sp.wait_ge(a.tile_done, done)
                            max_rows_in(a, (g + 1) % RING)
                        elif a.queries and kind == "norm" and what == ("apply", 0):
                            store_x1(i - 1)
                        at = max(at, g)

                passes(sp, slots)

            def stack_in1(g, b):
                done = a1.stack_in[g]
                for j in range(GROUP):
                    rows = slice(LATENT * j, LATENT * (j + 1))
                    for part, src in enumerate((q_high, q_high, q_low)):
                        sp.dma_start(q_stack[LATENT * part:LATENT * (part + 1), g, j, :].bitcast(F32),
                                     src[rows, :].bitcast(F32)).then_inc(done, 16)
                sp.dma_start(k_stack1[0:ROWS, g, :].bitcast(F32),
                             latent[0:ROWS, bass.ds(b * SEQ, SEQ)].bitcast(F32)).then_inc(done, 16)
                sp.dma_start(v_blocks1[:, g, :, :], latent_rows[:, bass.ds(b * SB, SB), :]).then_inc(done, 16)

            def stack_in2(g, b):
                done = a2.stack_in[g]
                sp.wait_ge(qk_stored, 16 * 4 * BATCH)
                heads = slice(GROUP * g, GROUP * (g + 1))
                for part in range(4):
                    rows = slice(HD2 * part, HD2 * (part + 1))
                    for stack, dram, low in ((q_stack, q_dram, part // 2), (k_stack2, k_dram, part % 2)):
                        src = dram[bass.ds(b, 1), low, heads, :, :].rearrange("one h c q -> c (one h) q")
                        sp.dma_start(stack[rows, g, :, :].bitcast(F32), src).then_inc(done, 16)
                sp.dma_start(v_blocks2[:, g, :, :, :], v_tokens[:, bass.ds(b * SB, SB), heads, :]).then_inc(done, 16)

            def zero_slots():
                rows, columns = q_stack[STACK - 64:STACK], GROUP * SEQ
                for dram in (slots_in, token_out):
                    flat = dram.rearrange("s d -> (s d)")
                    for r in range(RING):
                        part = flat[64 * columns * r:64 * columns * (r + 1)].rearrange("(p f) -> p f", p=64)
                        sp.dma_start(part, rows[:, r].rearrange("p h q -> p (h q)").bitcast(F32)).then_inc(zeroed, 16)
                rest = slots_in.rearrange("s d -> (s d)")[64 * columns * RING:].rearrange("(p f) -> p f", p=64)
                sp.dma_start(rest, rows[:, 0, 0, 0:EXPERTS * CAPACITY // 64].bitcast(F32)).then_inc(zeroed, 16)

            def router_in():
                sp.dma_start(wproj, t["wproj"]).then_inc(late_loaded, 16)
                sp.dma_start(wgate, t["wgate"]).then_inc(late_loaded, 16)
                for k, name in enumerate(("ln2_g", "ln2_b")):
                    sp.dma_start(affine2[:, k, :], t[name].partition_broadcast(P)).then_inc(late_loaded, 16)

            sp.wait_ge(pre_done, PRE_TILES)
            sp.wait_ge(ones_rows, 1)
            slots_of(a1, stack_in1)

            sp.wait_ge(a1.tile_done, 2 + A1_TILES)
            sp.dma_start(wqkv[:], t["wqkv"]).then_inc(mid_loaded, 16)
            for k, name in enumerate(("rope_cos", "rope_sin")):
                sp.dma_start(rope[:, k, :, :], t[name].rearrange("(n p) j -> p n j", p=P)).then_inc(mid_loaded, 16)
            store_x1(BATCH - 1)
            for b in range(BATCH):
                for w, dram in enumerate((q_dram, k_dram)):
                    sp.wait_ge(mid_dve, 2 * b + w + 1)
                    for low, src in enumerate((qk_high, qk_low)):
                        sp.dma_start(dram[b, low].rearrange("h c q -> (h c) q"),
                                     src[:, w, :].bitcast(F32)).then_inc(qk_stored, 16)
            sp.wait_ge(qk_stored, 16 * 4 * BATCH)
            sp.wait_ge(stack_cleared, 6)
            sp.wait_ge(v_ones, 1)
            slots_of(a2, stack_in2)

            sp.wait_ge(a2.tile_done, 2 + A2_TILES)
            sp.wait_ge(zeroed, 16 * 9)
            sp.dma_start(b1_rows[:], t["b1"].rearrange("e (f p) -> (e f) p", p=P)).then_inc(b1_loaded, 16)

            def weights_in(e, k):
                sp.dma_start(w1[:, k, :], t["w1"][e]).then_inc(w_in2[k], 16)
                sp.dma_start(w2[:, k, :, :], t["w2"][e].rearrange("(f p) d -> p f d", p=P)).then_inc(w_in2[k], 16)
                sp.dma_start(b2[:, k, :], t["b2"][e].partition_broadcast(P)).then_inc(w_in2[k], 16)

            def expert_rows_in(e, k):
                sp.dma_start(expert_in[:, k, :, :],
                             slots_in[CAPACITY * e:CAPACITY * (e + 1), :].rearrange("(n p) d -> p n d", p=P)
                             ).then_inc(e_in[k], 16)

            weights_in(0, 0)
            weights_in(1, 1)
            sp.wait_ge(scattered, 16 * TOPK * BLOCKS)
            expert_rows_in(0, 0)
            expert_rows_in(1, 1)
            for b in range(BATCH):
                sp.dma_start(x1_back[:, blocks_of(b), :], tokens(x1_dram, b)).then_inc(x1_loaded, 16)
            for e in range(EXPERTS - 2):
                sp.wait_ge(out_done, e + 1)
                weights_in(e + 2, e % 2)
                expert_rows_in(e + 2, e % 2)
            for k in range(2):
                sp.wait_ge(out_stored[k], 16 * SB * EXPERTS // 2)
            for b in range(BATCH):
                for k in range(TOPK):
                    at = TOK * k + SEQ * b
                    sp.dma_start(fetched[:, k, blocks_of(b), :],
                                 token_out[at:at + SEQ, :].rearrange("(n p) d -> p n d", p=P)).then_inc(fetched_in[b], 16)
            for b in range(BATCH):
                sp.wait_ge(final_ready, SB * (b + 1))
                sp.dma_start(tokens(t["out"], b), x[:, blocks_of(b), :]).then_inc(stored, 16)
            for n, (name, make) in enumerate((dump or {}).items()):
                sp.dma_start(t[name], make(tensors)).then_inc(stored, 16)
            sp.wait_ge(stored, 16 * (BATCH + len(dump or {})))

        @block.scalar
        def _(act):
            roots = Tally(var_ready, 0, 3)

            def square_root():
                act.wait_ge(var_ready, roots.next())
                act.activation(root[:], var_eps[:], ACT.Sqrt).then_inc(root_ready, 1)

            def copy(out, src):
                return act.activation(out, src, ACT.Copy)

            for b in range(BATCH):
                square_root()
            n = 0

            def drain(out, src):
                nonlocal n
                act.wait_ge(pre_ready, n + 1)
                copy(out, src).then_inc(pre_done, 1)
                n += 1

            drain(wq_t.rearrange("p g d -> p (g d)"), tile_ps[:, 0, :])
            drain(wkv_t.rearrange("p w g c -> p (w g c)"), tile_ps[:, 1, 0:2 * 8 * LATENT])
            drain(absorbed_q[:].rearrange("p (g two c) -> p two g c", two=2, c=LATENT),
                  tile_ps[:, 0, :].rearrange("p (two k) -> p two k", two=2)[:, :, 0:8 * LATENT]
                  .rearrange("p two (g c) -> p two g c", c=LATENT))
            act.wait_ge(pre_ready, n + 1)
            for j in range(GROUP):
                rows, col = slice(LATENT * j, LATENT * (j + 1)), BANK * (j % 2)
                last = copy(absorbed_o[rows, :, :], tile_ps[rows, 1, col:col + BANK].rearrange("p (g o) -> p g o", o=DIM))
            last.then_inc(pre_done, 1)
            n += 1
            for b in range(BATCH):
                drain(xn_t[:, SEQ * b:SEQ * (b + 1)], tile_ps[:, n % 2, :])
            for b in range(BATCH):
                act.wait_ge(pre_ready, n + 1)
                copy(latent[0:STACK, SEQ * b:SEQ * (b + 1)], tile_ps[0:STACK, n % 2, :]).then_inc(high_written, 1)
                n += 1
            drain(latent_rows[:].rearrange("p n c -> p (n c)"), tile_ps[:, n % 2, :])
            assert n == PRE_TILES

            def gate_exp(b):
                act.wait_ge(exp_in, b + 1)
                act.activation(gates, r0, ACT.Exp).then_inc(exp_out, 1)

            def exponentials(a):
                act.sem_inc(a.probs_ready, 2)
                act.sem_inc(a.chunk_free, 1)
                scores_ready = Tally(a.scores_ready, 0, UNITS * GROUPS)
                quad_used = Tally(a.quad_done, 0, QUADS * GROUPS)
                quad_done = Tally(a.quad_done, 2, QUADS * GROUPS)
                inverse_ready = Tally(a.inverse_ready, 2, 2 * GROUPS)

                def slots(i, first, last):
                    for tally in (scores_ready, quad_used, quad_done, inverse_ready):
                        tally.turn(i, first)
                    if not first:
                        roots.turn(i)
                    for g, kind, what, quad in pass_steps(a, first, last):
                        if kind == "score":
                            (c, kb, off), h = what
                            u = GROUP * quad + h
                            if h == 0:
                                act.wait_ge(a.quad_done, quad_used.next())
                            act.wait_ge(a.scores_ready, scores_ready.next())
                            act.activation(probs[:, u % 8, off:], score_ps[:, u % 2, off:], ACT.Exp,
                                           scale=a.scale).then_inc(a.probs_ready, 1)
                        elif kind == "drain":
                            act.wait_ge(a.quad_done, quad_done.next(len(key_blocks(what))))
                            act.wait_ge(a.inverse_ready, inverse_ready.next())
                            if a.sums:
                                copy(attended[:, g, BANK * what:BANK * (what + 1)], value_ps[:])
                                copy(sum_inv[:], sum_ps[:]).then_inc(a.chunk_free, 1)
                            else:
                                copy(sum_inv[:], value_ps[:]).then_inc(a.chunk_free, 1)
                        elif kind == "norm" and what[0] == "root":
                            square_root()
                        elif kind == "post" and what[0] == "exp":
                            gate_exp(i - 1)

                roots.loop_from_1(3 if a.queries else 1)
                passes(act, slots)

            exponentials(a1)

            def rounded(b):
                if b:
                    act.wait_ge(qk_stored, 16 * 4 * b)
                for w in range(2):
                    at = mid_at("qk", b, w)
                    act.wait_ge(mid_ready, at + 1)
                    copy(qk_high[:, w, :], tile_ps[:, at % 2, :]).then_inc(qk_rounded, 1)

            for b in range(BATCH):
                at = mid_at("h", b, 0)
                act.wait_ge(mid_ready, at + 1)
                copy(h_t[:], tile_ps[:, at % 2, :]).then_inc(mid_act, 1)
                if b == 0:
                    square_root()
                    act.wait_ge(v_ones, 1)
                if b >= 2:
                    act.wait_ge(qk_turned, b - 1)
                for m in range(4):
                    at = mid_at("qkv", b, m)
                    act.wait_ge(mid_ready, at + 1)
                    tile = tile_ps[:, at % 2, :].rearrange("p (n c) -> p n c", n=2)
                    copy(qk_raw[:, b % 2, 2 * m:2 * m + 2, :], tile[:, :, 0:2 * DIM]).then_inc(qk_drained, 1)
                    for two in range(2):
                        last = copy(v_tokens[:, SB * b + 2 * m + two, :, 0:HD2],
                                    tile[:, two, 2 * DIM:3 * DIM].rearrange("p (h c) -> p h c", c=HD2))
                    last.then_inc(mid_act, 1)
                    if b == 0 and m % 2:
                        square_root()
                if b:
                    rounded(b - 1)
            rounded(BATCH - 1)

            exponentials(a2)

            square_root()
            gate_exp(BATCH - 1)
            act.wait_ge(b1_turned, 1)
            for e in range(EXPERTS):
                act.wait_ge(w_in2[e % 2], 48 * (e // 2 + 1))
                for c in range(2):
                    for f in range(HIDDEN // P):
                        unit = 8 * e + 4 * c + f
                        act.wait_ge(hid_ready, unit + 1)
                        if f == 0 and 2 * e + c >= 2:
                            act.wait_ge(out_ready, 2 * e + c - 1)
                        act.activation(hidden[:, c, f, :], score_ps[:, unit % 2, :], ACT.Gelu,
                                       bias=b1[:, e, f:f + 1]).then_inc(hid_done, 1)
            for b in range(BATCH):
                square_root()

        @block.tensor
        def _(pe):
            pe.wait_ge(consts, 8)
            pe.wait_ge(w_loaded, 16 * 9)
            for g in range(8):
                last = pe.transpose(tile_ps[:, 0, P * g:P * (g + 1)], wq_raw[:, P * g:P * (g + 1)], ident[:])
            last.then_inc(pre_ready, 1)
            for w, raw in enumerate((wk_raw, wv_raw)):
                for g in range(8):
                    at = (8 * w + g) * LATENT
                    last = pe.transpose(tile_ps[:, 1, at:at + LATENT], raw[:, P * g:P * (g + 1)], ident[0:LATENT, 0:LATENT])
            last.then_inc(pre_ready, 1)
            pe.wait_ge(pre_done, 2)
            for h in range(HEADS):
                k = slice(KDIM * (h % 2), KDIM * (h % 2 + 1))
                col = BANK * (h % 2) + LATENT * (h // 2)
                last = pe.matmul(tile_ps[:, 0, col:col + LATENT], wq_t[k, h // 2, :], wkv_t[k, 0, h // 2, :],
                                 start=True, stop=True)
            last.then_inc(pre_ready, 1)
            for h in range(HEADS):
                k = slice(KDIM * (h % 2), KDIM * (h % 2 + 1))
                j, g = h % GROUP, h // GROUP
                col = BANK * (h % 2) + P * g
                last = pe.matmul(tile_ps[LATENT * j:LATENT * (j + 1), 1, col:col + P],
                                 wkv_t[k, 1, h // 2, :], wout_raw[k, h // 2, :], start=True, stop=True)
            last.then_inc(pre_ready, 1)
            n = 4
            for b in range(BATCH):
                pe.wait_ge(normed, SB * (b + 1))
                pe.wait_ge(pre_done, n - 1)
                for m in range(SB):
                    last = pe.transpose(tile_ps[:, n % 2, P * m:P * (m + 1)], xn[:, SB * b + m, :], ident[:])
                last.then_inc(pre_ready, 1)
                n += 1
            for b in range(BATCH):
                pe.wait_ge(pre_done, n - 1)
                for c in range(CHUNKS):
                    at = SEQ * b + BANK * c
                    last = pe.matmul(tile_ps[0:STACK, n % 2, BANK * c:BANK * (c + 1)],
                                     down3[:].rearrange("p r c -> p (r c)"), xn_t[:, at:at + BANK], start=True, stop=True)
                last.then_inc(pre_ready, 1)
                n += 1
            pe.wait_ge(pre_done, n - 1)
            for m in range(BLOCKS):
                last = pe.matmul(tile_ps[:, n % 2, LATENT * m:LATENT * (m + 1)], xn_t[:, P * m:P * (m + 1)],
                                 down3[:, 0, :], start=True, stop=True)
            last.then_inc(pre_ready, 1)
            pe.wait_ge(pre_done, n + 1)

            def attention(a):
                pe.sem_inc(a.quad_done, 2)
                tile_done = Tally(a.tile_done, 0, a.pass_tiles, a.short)
                probs_ready = Tally(a.probs_ready, 0, UNITS * GROUPS)
                chunk_free = Tally(a.chunk_free, 0, 2 * GROUPS)
                masked = Tally(a.masked, 0, SB * GROUPS)
                tiles = 0

                def next_tile():
                    nonlocal tiles
                    pe.wait_ge(a.tile_done, tile_done.next())
                    tiles += 1
                    return tile_ps[:, (tiles - 1) % 2, :]

                def keys_of(r, h):
                    return a.k_stack[0:ROWS, r, :] if a.queries else a.k_stack[0:ROWS, r, h, :]

                def queries(g, b):
                    tile = next_tile()
                    for c in range(CHUNKS):
                        last = pe.matmul(tile[:, BANK * c:BANK * (c + 1)], absorbed_q[:, P * g:P * (g + 1)],
                                         xn_t[:, bass.ds(b * SEQ + BANK * c, BANK)], start=True, stop=True)
                    last.then_inc(a.tile_ready, 1)

                def max_scores(r, heads, qb):
                    tile = next_tile()
                    keys = (qb + 1) * P
                    for at, h in enumerate(heads):
                        for k0 in range(0, keys, BANK):
                            wide = max(2 * P, min(BANK, keys - k0))
                            col = BANK * at + k0
                            last = pe.matmul(tile[:, col:col + wide], q_stack[0:STACK, r, h, P * qb:P * (qb + 1)],
                                             keys_of(r, h)[0:STACK, k0:k0 + wide], start=True, stop=True)
                    last.then_inc(a.tile_ready, 1)

                def max_to_rows(parts):
                    pe.wait_ge(a.parts_ready, parts)
                    tile = next_tile()
                    pe.transpose(tile[:, 0:P], max_parts[:].rearrange("p a b -> p (a b)").bitcast(F32),
                                 ident[:]).then_inc(a.tile_ready, 1)

                def score(r, c, kb, off, h, unit):
                    pe.wait_ge(a.probs_ready, probs_ready.next())
                    start = min(off, BANK - 2 * P)
                    last = pe.matmul(score_ps[:, unit % 2, start:], keys_of(r, h)[:, P * kb:P * (kb + 1)],
                                     q_stack[0:ROWS, r, h, BANK * c + start:BANK * (c + 1)],
                                     start=True, stop=True)
                    last.then_inc(a.scores_ready, 1)

                def values(r, c, kb, off, quad, ready):
                    if kb == 0:
                        pe.wait_ge(a.chunk_free, chunk_free.next())
                    if kb >= CB * c:
                        pe.wait_ge(a.masked, masked.next())
                    else:
                        pe.wait_ge(a.probs_ready, ready)
                    for h in range(GROUP):
                        v = a.v_blocks[:, r, kb, :] if a.queries else a.v_blocks[:, r, kb, h, :]
                        last = pe.matmul(value_ps[LATENT * h:LATENT * h + a.v_width, off:], v,
                                         probs[:, (GROUP * quad + h) % 8, off:],
                                         start=kb == 0, stop=True, skip_group_check=True)
                    return last

                def sums(kb, off, quad):
                    for h in range(GROUP):
                        last = pe.matmul(sum_ps[LATENT * h:LATENT * (h + 1), off:], ones[:, 0:LATENT],
                                         probs[:, (GROUP * quad + h) % 8, off:],
                                         start=kb == 0, stop=True, skip_group_check=True)
                    return last

                def turn(drained):
                    pe.wait_ge(a.chunk_free, drained)
                    tile = next_tile()
                    for m in range(CB):
                        last = pe.transpose(tile[:, P * m:P * (m + 1)], sum_inv[:, P * m:P * (m + 1)], ident[:])
                    last.then_inc(a.tile_ready, 1)

                def project(half, scaled):
                    pe.wait_ge(a.inverse_ready, 2 * scaled + 3)
                    tile = next_tile()
                    for m in range(CB):
                        q = P * (CB * half + m)
                        for g in range(GROUPS):
                            mm = pe.matmul(tile[:, P * m:P * (m + 1)], attended[:, g, q:q + P],
                                           absorbed_o[:, g, :], start=g == 0, stop=g == GROUPS - 1)
                    mm.then_inc(a.tile_ready, 1)

                if a.queries:
                    for g in range(a.ahead):
                        queries(g, 0)
                pe.wait_ge(a.stack_in[0], 16 * a.q_dmas)
                for heads, qb in max_items():
                    max_scores(0, heads, qb)
                max_to_rows(1)
                tile_done.start += a.first_tiles

                def slots(i, first, last):
                    for tally in (tile_done, probs_ready, chunk_free, masked):
                        tally.turn(i, first)
                    at = -1
                    for g, kind, what, quad in pass_steps(a, first, last):
                        if kind == "queries":
                            queries((g + 3) % GROUPS, i if g < 1 else i + 1)
                            continue
                        if g > at:
                            if not (last and g == 3):
                                pe.wait_ge(a.stack_in[(g + 1) % RING], 16 * a.q_dmas * (i + (1 if g < 3 else 2)))
                            pe.wait_ge(a.max_in[g], 32 * (i + 1))
                            at = g
                        if kind == "score":
                            score(g, *what[0], what[1], GROUP * quad + what[1])
                        elif kind == "max":
                            max_scores((g + 1) % RING, *what)
                        elif kind == "max rows":
                            max_to_rows(GROUPS * i + g + 2)
                        elif kind == "values":
                            mm = values(g, *what, quad, UNITS * (GROUPS * i + g) + 2 + GROUP * (quad + 1))
                            if not a.sums:
                                mm.then_inc(a.quad_done, 1)
                        elif kind == "sums":
                            sums(*what[1:], quad).then_inc(a.quad_done, 1)
                        elif kind == "turn":
                            turn(2 * (GROUPS * i + g) + what + 2)
                        elif kind == "project":
                            project(what, GROUPS * i + GROUPS)
                        elif kind == "post" and what[0] in POST_TILED:
                            post(*what, i - 1)
                    if first and not a.queries:
                        pe.wait_ge(late_loaded, 64)

                def post(name, half, b):
                    if name == "turn h":
                        pe.wait_ge(h2_ready, b + 1)
                    if name == "count":
                        pe.wait_ge(mask_ready, b + 1)
                    tile = next_tile()
                    if name in ("turn x", "logits") or name == "project" and half == 0:
                        pe.wait_ge(a.tile_done, tile_done.here() + 1)
                    if name in ("turn x", "turn h"):
                        for m in range(SB):
                            src = attn[:, m, :] if name == "turn x" else h2_rows[:, m, 0:DIM]
                            last = pe.transpose(tile[:, P * m:P * (m + 1)], src, ident[:])
                    elif name == "count":
                        flat = mask.rearrange("p n e -> p (n e)")
                        pe.matmul(tile[:, 0:EXPERTS * (SB + 1)], upper[:], flat, start=True, stop=True, skip_group_check=True)
                        for n in range(1, SB + 1):
                            last = pe.matmul(tile[:, EXPERTS * n:EXPERTS * (SB + 1)], ones[:], flat[:, 0:EXPERTS * (SB + 1 - n)],
                                             start=False, stop=True, skip_group_check=True)
                    else:
                        weight, width = (wproj, P) if name == "project" else (wgate, EXPERTS)
                        for m in range(CB * half, CB * (half + 1)) if name == "project" else range(SB):
                            last = pe.matmul(tile[:, width * m:width * (m + 1)], turned[:, P * m:P * (m + 1)], weight,
                                             start=True, stop=True)
                    last.then_inc(a.tile_ready, 1)

                passes(pe, slots)
                if not a.queries:
                    for _, (name, what) in post_steps():
                        if name in POST_TILED:
                            post(name, what, BATCH - 1)

            attention(a1)

            pe.wait_ge(mid_loaded, 48)
            pe.wait_ge(a1.tile_done, 2 + A1_TILES)

            def mid_tile(kind, b, k):
                at = mid_at(kind, b, k)
                if at >= 2:
                    kinds = [what[0] == "qk" for what in mid_tiles[:at - 1]]
                    if kinds[-1]:
                        pe.wait_ge(mid_dve, sum(kinds))
                    else:
                        pe.wait_ge(mid_act, len(kinds) - sum(kinds))
                return tile_ps[:, at % 2, :]

            by_kind = wqkv[:].rearrange("p (h s c) -> p s h c", s=3, c=HD2)
            for b in range(BATCH + 1):
                if b < BATCH:
                    pe.wait_ge(h_ready, b + 1)
                    tile = mid_tile("h", b, 0)
                    for m in range(SB):
                        last = pe.transpose(tile[:, P * m:P * (m + 1)], x[:, SB * b + m, :], ident[:])
                    last.then_inc(mid_ready, 1)
                    pe.wait_ge(mid_act, 5 * b + 1)
                    for k in range(4):
                        tile = mid_tile("qkv", b, k)
                        for two in range(2):
                            m = 2 * k + two
                            last = pe.matmul(tile[:, BANK * two:BANK * two + 3 * DIM], h_t[:, P * m:P * (m + 1)],
                                             by_kind, start=True, stop=True)
                        last.then_inc(mid_ready, 1)
                if b:
                    pe.wait_ge(qk_turned, b)
                    for w in range(2):
                        tile = mid_tile("qk", b - 1, w)
                        for m in range(SB):
                            last = pe.transpose(tile[:, P * m:P * (m + 1)], qk[:, (b - 1) % 2, m, DIM * w:DIM * (w + 1)],
                                                ident[:])
                        last.then_inc(mid_ready, 1)

            pe.wait_ge(mid_dve, 2 * BATCH)
            pe.wait_ge(cleared, 1)
            attention(a2)

            pe.wait_ge(b1_loaded, 16)
            pe.transpose(score_ps[:, 0, 0:EXPERTS * HIDDEN // P], b1_rows[:], ident[0:EXPERTS * HIDDEN // P, 0:EXPERTS * HIDDEN // P]
                         ).then_inc(b1_ready, 1)
            pe.wait_ge(b1_turned, 1)

            def expert_turn(e):
                pe.wait_ge(e_in[e % 2], 16 * (e // 2 + 1))
                if e:
                    pe.wait_ge(e_turned_done, e)
                for m in range(SB):
                    last = pe.transpose(tile_ps[:, 0, P * m:P * (m + 1)], expert_in[:, e % 2, m, 0:DIM], ident[:])
                last.then_inc(e_turned, 1)

            def expert_hidden(e, c):
                for f in range(HIDDEN // P):
                    unit = 8 * e + 4 * c + f
                    if unit >= 2:
                        pe.wait_ge(hid_done, unit - 1)
                    pe.matmul(score_ps[:, unit % 2, :], w1[:, e % 2, P * f:P * (f + 1)],
                              expert_in_t[:, e % 2, BANK * c:BANK * (c + 1)], start=True, stop=True).then_inc(hid_ready, 1)

            def expert_output(e, c):
                pe.wait_ge(hid_done, 8 * e + 4 * (c + 1))
                if c == 0 and e:
                    pe.wait_ge(out_done, e)
                for m in range(CB):
                    for f in range(HIDDEN // P):
                        last = pe.matmul(tile_ps[:, 1, BANK * c + P * m:BANK * c + P * (m + 1)],
                                         hidden[:, c, f, P * m:P * (m + 1)], w2[:, e % 2, f, :],
                                         start=f == 0, stop=f == HIDDEN // P - 1)
                last.then_inc(out_ready, 1)

            expert_turn(0)
            for e in range(EXPERTS):
                pe.wait_ge(w_in2[e % 2], 48 * (e // 2 + 1))
                pe.wait_ge(e_turned_done, e + 1)
                expert_hidden(e, 0)
                expert_hidden(e, 1)
                expert_output(e, 0)
                if e + 1 < EXPERTS:
                    expert_turn(e + 1)
                expert_output(e, 1)

        @block.vector
        def _(dve):
            chain = Tally(dve_step, 0, NORM_LINKS)
            norms = Tally(root_ready, 0, 3)

            def mark(ins):
                chain.next()
                ins.then_inc(dve_step, 1)

            def caught():
                dve.wait_ge(dve_step, chain.base + chain.n)

            def link(ins):
                mark(ins)
                caught()

            def norm_piece(piece, src, out):
                if piece == "stats":
                    dve.sem_inc(dve_turn, 1)
                    for n in range(SB):
                        ins = dve.bn_stats(stats[:, n, :], src[:, n, :])
                    mark(ins)
                elif piece == "moments":
                    caught()
                    dve.sem_inc(dve_turn, 1)
                    for n in range(SB):
                        ins = dve.bn_aggr(mean_var[:, n, :], stats[:, n, :])
                    link(ins)
                    dve.tensor_scalar(var_eps[:], mean_var[:, :, 1], EPS, None, ALU.add).then_inc(var_ready, 1)
                elif piece == "newton":
                    dve.wait_ge(root_ready, norms.next())
                    link(dve.reciprocal(rstd[:], root[:]))
                    link(dve.tensor_tensor(newton[:], rstd[:], rstd[:], ALU.mult))
                    link(dve.tensor_tensor(newton[:], newton[:], var_eps[:], ALU.mult))
                    link(dve.tensor_scalar(newton[:], newton[:], -0.5, 1.5, ALU.mult, ALU.add))
                    mark(dve.tensor_tensor(rstd[:], rstd[:], newton[:], ALU.mult))
                elif piece == "apply":
                    caught()
                    for n in range(SB):
                        ins = dve.tensor_scalar(out[:, n, :], src[:, n, :], mean_var[:, n, 0:1], rstd[:, n:n + 1],
                                                ALU.subtract, ALU.mult)
                    mark(ins)

            def norm(src, b, out):
                for piece in ("stats", "moments", "newton", "apply"):
                    norm_piece(piece, src[:, blocks_of(b), :], out[:, blocks_of(b), :])
                caught()

            def mid_norm(what, b):
                piece, r = what
                part = bass.ds(b * SB, SB)
                if piece == "stats" and r:
                    if r == 1:
                        dve.wait_ge(x1_ready, SB * b + SB)
                    else:
                        caught()
                if piece == "apply" and r == 2:
                    dve.wait_ge(x1_stored, 16 * b + 16)
                if piece == "gain":
                    caught()
                    gain_and_bias(x[:, part, :], affine1, h_ready)
                else:
                    norm_piece(piece, (xn, x, xn)[r][:, part, :], (xn, xn, x)[r][:, part, :])
                if piece == "apply" and r == 0:
                    caught()
                    dve.tensor_tensor(x[:, part, :], x[:, part, :], xn[:, part, :], ALU.add).then_inc(x1_ready, SB)

            def gain_and_bias(part, vectors, signal):
                for which, op in enumerate((ALU.mult, ALU.add)):
                    vector = vectors[:, which, :].unsqueeze(1).broadcast_to([P, SB, DIM])
                    ins = dve.tensor_tensor(part, part, vector, op)
                    if op == ALU.mult:
                        link(ins)
                    else:
                        ins.then_inc(signal, 1)

            link(dve.memset(max_parts[:].rearrange("p a b -> p (a b)").bitcast(F32), 0.0))
            dve.wait_ge(w_loaded, 16 * 9)
            dve.wait_ge(consts, 8)
            for b in range(BATCH):
                dve.wait_ge(x_in[b], 16)
                norm(x, b, xn)
                dve.sem_inc(normed, SB)
            for b in range(BATCH):
                dve.wait_ge(high_written, b + 1)
                rows = slice(LATENT, 2 * LATENT)
                dve.tensor_tensor(latent[rows, SEQ * b:SEQ * (b + 1)], tile_ps[rows, (8 + b) % 2, :],
                                  latent[rows, SEQ * b:SEQ * (b + 1)].bitcast(F32), ALU.subtract).then_inc(pre_done, 1)

            def attention(a):
                dve.sem_inc(a.tile_done, 2)
                dve.sem_inc(a.inverse_ready, 3)
                tile_ready = Tally(a.tile_ready, 0, a.pass_tiles, a.short)
                tile_done = Tally(a.tile_done, 2, a.pass_tiles, a.short)
                high_ready = Tally(a.high_ready, 0, (2 if a.queries else 1) * GROUPS)
                inverted = Tally(a.inverted, 0, 2 * GROUPS)
                chunk_free = Tally(a.chunk_free, 1, 2 * GROUPS)
                tiles = 0

                def next_tile():
                    nonlocal tiles
                    dve.wait_ge(a.tile_ready, tile_ready.next())
                    tile_done.next()
                    tiles += 1
                    return tile_ps[:, (tiles - 1) % 2, :]

                def queries(last_use):
                    tile = next_tile()
                    if last_use:
                        dve.wait_ge(*last_use)
                    dve.tensor_copy(q_high[:], tile).then_inc(a.high_ready, 1)
                    dve.wait_ge(a.high_ready, high_ready.next())
                    dve.tensor_tensor(q_low[:], tile, q_high[:].bitcast(F32), ALU.subtract).then_inc(a.tile_done, 1)

                def max_scores(heads, qb):
                    tile = next_tile()
                    dve.sem_inc(a.max_turn, 1)
                    keys = (qb + 1) * P
                    for at, h in enumerate(heads):
                        row = tile[:, BANK * at:BANK * at + keys]
                        ins = dve.tensor_tensor_reduce(row, row, late_key[:, SEQ - keys:], 1.0, MASKED, ALU.add, ALU.max,
                                                       max_of[:, h, qb:qb + 1])
                    ins.then_inc(a.tile_done, 1)

                def max_to_rows(last_use):
                    dve.wait_ge(a.tile_done, tile_done.base + tile_done.n)
                    flat = max_of[:].rearrange("p h n -> p (h n)")
                    dve.tensor_scalar(max_parts[:, 0, :], flat, -1.0, None, ALU.mult).then_inc(a.high_ready, 1)
                    dve.wait_ge(a.high_ready, high_ready.next())
                    dve.scalar_tensor_tensor(out=max_parts[:, 1, :], in0=flat, scalar=-1.0, in1=max_parts[:, 0, :].bitcast(F32),
                                             op0=ALU.mult, op1=ALU.subtract).then_inc(a.parts_ready, 1)
                    tile = next_tile()
                    if last_use:
                        dve.wait_ge(*last_use)
                    dve.tensor_copy(max_rows[:], tile[:, 0:P]).then_inc(a.tile_done, 1)

                def inverse(c, m):
                    part = sum_inv[:, P * m:P * (m + 1)]
                    if m == 0:
                        dve.wait_ge(a.chunk_free, chunk_free.next())
                    ins = dve.reciprocal(part, part)
                    if m == CB - 1:
                        ins.then_inc(a.inverted, 1)

                def scale(g, c):
                    dve.wait_ge(a.inverted, inverted.next())
                    part = attended[:, g, BANK * c:BANK * (c + 1)]
                    dve.tensor_tensor(part, part, sum_inv[:], ALU.mult).then_inc(a.inverse_ready, 1)

                def turn(g, c, i):
                    tile = next_tile()[:, 0:BANK].rearrange("p (m h v) -> p m h v", m=CB, h=GROUP)
                    dve.wait_ge(a.tile_done, tile_done.base + tile_done.n - 1)
                    dve.reciprocal(turn_inv[:], tile[:, :, :, HD2:HD2 + 1]).then_inc(a.inverse_ready, 1)
                    dve.wait_ge(a.inverse_ready, inverse_ready.next())
                    out = attn[:, CB * c:CB * (c + 1), P // GROUP * g:P // GROUP * (g + 1)]
                    for m in range(CB):
                        ins = dve.tensor_tensor(out[:, m, :].rearrange("p (h v) -> p h v", h=GROUP), tile[:, m, :, 0:HD2],
                                                turn_inv[:, m, :, :].broadcast_to([P, GROUP, HD2]), ALU.mult)
                    ins.then_inc(a.tile_done, 1)

                inverse_ready = Tally(a.inverse_ready, 3, 2 * GROUPS)
                if a.queries:
                    queries(None)
                    for g in range(1, a.ahead):
                        queries((a.stack_in[g - 1], 16 * a.q_dmas))
                for heads, qb in max_items():
                    max_scores(heads, qb)
                max_to_rows(None)
                tile_ready.start += a.first_tiles
                tile_done.start += a.first_tiles
                high_ready.start += 4 if a.queries else 1

                def slots(i, first, last):
                    for tally in (tile_ready, tile_done, high_ready, inverse_ready, inverted, chunk_free):
                        tally.turn(i, first)
                    if not first:
                        chain.turn(i)
                        norms.turn(i)
                    for g, kind, what, quad in pass_steps(a, first, last):
                        if kind == "queries":
                            queries((a.stack_in[(g + 2) % RING], 16 * a.q_dmas * (i + (1 if g < 2 else 2))))
                        elif kind == "max":
                            max_scores(*what)
                        elif kind == "max rows":
                            max_to_rows((a.max_in[g], 32 * (i + 1)))
                        elif kind == "inverse":
                            inverse(*what)
                        elif kind == "scale":
                            scale(g, what)
                        elif kind == "turn":
                            turn(g, what, i)
                        elif kind == "norm" and a.queries:
                            mid_norm(what, i - 1)
                        elif kind == "norm":
                            post_norm(what[0], i - 1)
                        elif kind == "post":
                            post(*what, i - 1)
                        elif kind == "project":
                            tile = next_tile()
                            dve.tensor_copy(xn[:, bass.ds(i * SB + CB * what, CB), :],
                                            tile[:, 0:BANK].rearrange("p (n o) -> p n o", o=DIM)).then_inc(a.tile_done, 1)
                    if first and not a.queries:
                        for e in range(EXPERTS):
                            dve.memset(rank[:, :, e], float(EXPERTS - e))
                            dve.memset(first_slot[:, :, e], float(CAPACITY * e - 1))
                        dve.memset(mask[:, SB:, :], 0.0)
                        link(dve.memset(before, 0.0))
                        dve.wait_ge(late_loaded, 64)
                        for tally, per in ((chain, POST_LINKS), (norms, 1)):
                            tally.loop_from_1(per)

                def wide(v):
                    return v.unsqueeze(2).broadcast_to([P, SB, EXPERTS])

                def post_norm(piece, b):
                    out = h2_rows[:, :, 0:DIM]
                    if piece == "stats":
                        dve.wait_ge(a.tile_done, tile_done.here())
                    if piece == "apply":
                        dve.wait_ge(scattered, 16 * TOPK * SB * b)
                    if piece == "gain":
                        caught()
                        gain_and_bias(out, affine2, h2_ready)
                    else:
                        norm_piece(piece, xn[:, bass.ds(b * SB, SB), :], out)

                def choose(left, k):
                    link(dve.tensor_reduce(row_value, left, AX.X, ALU.max))
                    link(dve.tensor_tensor(r2, left, wide(row_value), ALU.is_equal))
                    link(dve.tensor_tensor(r2, r2, rank, ALU.mult))
                    link(dve.tensor_reduce(row_value, r2, AX.X, ALU.max))
                    link(dve.tensor_tensor(chosen[k], r2, wide(row_value), ALU.is_equal))

                def post(name, what, b):
                    if name in POST_TILED:
                        tile = next_tile()
                    if name in ("turn x", "turn h"):
                        dve.tensor_copy(turned, tile).then_inc(a.tile_done, 1)
                    elif name == "project":
                        stream = xn[:, bass.ds(b * SB + CB * what, CB), :]
                        tile = tile[:, BANK * what:BANK * (what + 1)].rearrange("p (n o) -> p n o", o=DIM)
                        dve.tensor_tensor(stream, tile, stream, ALU.add).then_inc(a.tile_done, 1)
                    elif name == "logits":
                        logits = tile[:, 0:SB * EXPERTS].rearrange("p (n e) -> p n e", e=EXPERTS)
                        link(dve.tensor_reduce(row_value, logits, AX.X, ALU.max))
                        dve.tensor_tensor(r0, logits, wide(row_value), ALU.subtract).then_inc(exp_in, 1)
                        dve.wait_ge(exp_in, b + 1)
                        dve.sem_inc(a.tile_done, 1)
                    elif name == "choose":
                        dve.wait_ge(exp_out, b + 1)
                        link(dve.tensor_reduce(row_value, gates, AX.X, ALU.add))
                        link(dve.reciprocal(row_value, row_value))
                        link(dve.tensor_tensor(gates, gates, wide(row_value), ALU.mult))
                        choose(gates, 0)
                        link(dve.tensor_tensor(r1, gates, chosen[0], ALU.mult))
                        link(dve.tensor_tensor(r1, gates, r1, ALU.subtract))
                        link(dve.tensor_tensor(r1, r1, chosen[0], ALU.subtract))
                    elif name == "choose more":
                        choose(r1, 1)
                        dve.tensor_tensor(mask[:, 0:SB, :], chosen[0], chosen[1], ALU.add).then_inc(mask_ready, 1)
                    elif name == "count":
                        counts = tile[:, 0:(SB + 1) * EXPERTS].rearrange("p (n e) -> p n e", e=EXPERTS)
                        link(dve.tensor_tensor(r1, counts[:, 0:SB, :], before.broadcast_to([P, SB, EXPERTS]), ALU.add))
                        dve.tensor_tensor(before, counts[:, SB:, :], before, ALU.add).then_inc(a.tile_done, 1)
                        link(dve.tensor_scalar(r2, r1, float(CAPACITY), None, ALU.is_le))
                        link(dve.tensor_tensor(r1, r1, first_slot, ALU.add))
                    elif name == "place":
                        for k in range(TOPK):
                            for out, of in ((slot_of, r1), (kept, r2), (gate_part, gates)):
                                link(dve.tensor_tensor(r0, chosen[k], of, ALU.mult))
                                link(dve.tensor_reduce(out[:, k, :], r0, AX.X, ALU.add))
                        dve.tensor_tensor(gate_of[:, :, bass.ds(b * SB, SB)], gate_part, kept, ALU.mult)
                        link(dve.tensor_tensor(slot_of, slot_of, kept, ALU.mult))
                        link(dve.tensor_scalar(kept, kept, -float(EXPERTS * CAPACITY), float(EXPERTS * CAPACITY), ALU.mult, ALU.add))
                        link(dve.tensor_tensor(slot_of, slot_of, kept, ALU.add))
                        link(dve.tensor_copy(put_at, slot_of))
                    elif name == "ids":
                        if what:
                            dve.wait_ge(scattered, 16 * SB * (TOPK * b + what))
                        ins = dve.tensor_scalar(h2_rows[:, :, DIM:DIM + 1], token_no[:].unsqueeze(2), float(TOK * what), None, ALU.add)
                        ins.then_inc(ids_ready, 1)
                        if what == TOPK - 1:
                            link(dve.tensor_scalar(token_no[:], token_no[:], float(SEQ), None, ALU.add))

                if a.queries:
                    for tally, per in ((chain, NORM_LINKS), (norms, 3)):
                        tally.loop_from_1(per)
                passes(dve, slots)
                if not a.queries:
                    assert chain.n == POST_LINKS
                    for kind, what in post_steps():
                        if kind == "norm":
                            post_norm(what[0], BATCH - 1)
                        else:
                            post(*what, BATCH - 1)

            attention(a1)

            assert chain.n == NORM_LINKS and norms.n == 3
            dve.wait_ge(a1.tile_done, 2 + A1_TILES)
            dve.memset(v_tokens[:, :, :, HD2:HD2 + 1], 1.0).then_inc(v_ones, 1)

            def rotate(b):
                dve.wait_ge(qk_drained, 4 * (b + 1))
                halves = [v[:, b % 2].rearrange("p n (s two j) -> p n s two j", two=2, j=HD2 // 2) for v in (qk_raw, qk)]
                shape = [P, SB, 2 * HEADS, HD2 // 2]
                cos, sin = (rope[:, k, :, :].unsqueeze(2).broadcast_to(shape) for k in range(2))
                part_a, part_b = (rope_part[:, k, :, :].rearrange("p n (s j) -> p n s j", j=HD2 // 2) for k in range(2))
                t1, t2 = halves[0][:, :, :, 0, :], halves[0][:, :, :, 1, :]
                if b >= 2:
                    dve.wait_ge(mid_ready, mid_at("qk", b - 2, 1) + 1)
                dve.tensor_tensor(part_a, t1, cos, ALU.mult)
                link(dve.tensor_tensor(part_b, t2, sin, ALU.mult))
                link(dve.tensor_tensor(halves[1][:, :, :, 0, :], part_a, part_b, ALU.subtract))
                dve.tensor_tensor(part_a, t1, sin, ALU.mult)
                link(dve.tensor_tensor(part_b, t2, cos, ALU.mult))
                dve.tensor_tensor(halves[1][:, :, :, 1, :], part_a, part_b, ALU.add).then_inc(qk_turned, 1)

            def rest(b):
                if b:
                    dve.wait_ge(qk_stored, 16 * 4 * b)
                for w in range(2):
                    dve.wait_ge(qk_rounded, 2 * b + w + 1)
                    dve.tensor_tensor(qk_low[:, w, :], tile_ps[:, mid_at("qk", b, w) % 2, :],
                                      qk_high[:, w, :].bitcast(F32), ALU.subtract).then_inc(mid_dve, 1)

            steps = [what for _, what in norm_steps()]
            for what in steps[:-2]:
                mid_norm(what, BATCH - 1)
            dve.wait_ge(mid_loaded, 48)
            rotate(0)
            for what in steps[-2:]:
                mid_norm(what, BATCH - 1)
            for b in range(BATCH):
                if b + 1 < BATCH:
                    rotate(b + 1)
                rest(b)
            dve.wait_ge(qk_stored, 16 * 4 * BATCH)
            dve.wait_ge(stack_cleared, 2)
            for r in (0, 1):
                dve.memset(k_stack2[:, r].rearrange("p h q -> p (h q)").bitcast(F32), 1.0).then_inc(stack_cleared, 1)
            dve.memset(value_ps[:], 0.0).then_inc(cleared, 1)
            dve.wait_ge(cleared, 1)

            attention(a2)

            dve.wait_ge(b1_ready, 1)
            dve.tensor_copy(b1[:].rearrange("p e f -> p (e f)"), score_ps[:, 0, 0:EXPERTS * HIDDEN // P]).then_inc(b1_turned, 1)

            def expert_turned(e):
                dve.wait_ge(e_turned, e + 1)
                dve.tensor_copy(expert_in_t[:, e % 2, :], tile_ps[:, 0, :]).then_inc(e_turned_done, 1)
                number, past = expert_in[:, e % 2, :, DIM], sent_back[:, 0, :]
                link(dve.tensor_scalar(past, number, 0.5, float(2 * TOPK * TOK), ALU.is_lt, ALU.mult))
                link(dve.scalar_tensor_tensor(out=sent_back[:, 1, :], in0=number, scalar=-1.0, in1=past, op0=ALU.add, op1=ALU.add))
                link(dve.tensor_copy(out_at[:, e, :], sent_back[:, 1, :]))

            expert_turned(0)
            for e in range(EXPERTS):
                if e + 1 < EXPERTS:
                    if e:
                        dve.wait_ge(hid_ready, 8 * e)
                    expert_turned(e + 1)
                dve.wait_ge(out_ready, 2 * (e + 1))
                if e >= 2:
                    dve.wait_ge(out_stored[e % 2], 16 * SB * (e // 2))
                dve.wait_ge(w_in2[e % 2], 48 * (e // 2 + 1))
                dve.tensor_tensor(expert_out[:, e % 2, :, :], tile_ps[:, 1, :].rearrange("p (n d) -> p n d", d=DIM),
                                  b2[:, e % 2, :].unsqueeze(1).broadcast_to([P, SB, DIM]), ALU.add).then_inc(out_done, 1)
            dve.wait_ge(x1_loaded, 16 * BATCH)
            for b in range(BATCH):
                dve.wait_ge(fetched_in[b], 32)
                for k in range(TOPK):
                    for n in range(SB * b, SB * (b + 1)):
                        ins = dve.scalar_tensor_tensor(out=xn[:, n, :], in0=fetched[:, k, n, :], scalar=gate_of[:, k, n:n + 1],
                                                       in1=xn[:, n, :], op0=ALU.mult, op1=ALU.add)
                    link(ins)
                norm(xn, b, xn)
                part = blocks_of(b)
                dve.tensor_tensor(x[:, part, :], x1_back[:, part, :], xn[:, part, :], ALU.add).then_inc(final_ready, SB)


def rope_tables():
    import numpy as np

    freq = (1.0 / np.float32(10000.0) ** (np.arange(0, HD2, 2, dtype=np.float32) / np.float32(HD2))).astype(np.float32)
    angle = np.arange(SEQ, dtype=np.float32)[:, None] * freq
    return np.cos(angle).astype(np.float32), np.sin(angle).astype(np.float32)


_INS = {
    "x": "L0_attn_x_bld", "wq": "L0_attn_Wq", "wdown": "L0_attn_Wkv_down", "wk": "L0_attn_Wk_up",
    "wv": "L0_attn_Wv_up", "wout": "L0_attn_Wout", "ln1_g": "L0_ffn_ln1_g", "ln1_b": "L0_ffn_ln1_b",
    "wqkv": "L0_ffn_Wqkv", "wproj": "L0_ffn_Wproj", "ln2_g": "L0_ffn_ln2_g", "ln2_b": "L0_ffn_ln2_b",
    "wgate": "L0_ffn_Wgate", "w1": "L0_ffn_W1", "b1": "L0_ffn_b1", "w2": "L0_ffn_W2", "b2": "L0_ffn_b2",
}


def kernel(**inputs):
    import numpy as np
    import concourse.bacc as bacc
    from concourse.bass_utils import run_bass_kernel_spmd

    nc = bacc.Bacc("TRN2", target_bir_lowering=False, num_devices=1)
    arrays = {f"in_{k}": np.ascontiguousarray(inputs[name]) for k, name in _INS.items()}
    arrays["in_rope_cos"], arrays["in_rope_sin"] = rope_tables()
    t = {k[3:]: nc.dram_tensor(k, a.shape, F32, kind="ExternalInput").ap() for k, a in arrays.items()}
    t["out"] = nc.dram_tensor("out", [BATCH, SEQ, DIM], F32, kind="ExternalOutput").ap()
    build(nc, t)
    got = run_bass_kernel_spmd(nc, [arrays], core_ids=[0])
    return got.results[0]["out"]
```

```python
from contextlib import ExitStack

import concourse.bass as bass
from concourse import mybir

F32 = mybir.dt.float32
F32R = mybir.dt.float32r
BF16 = mybir.dt.bfloat16
U32 = mybir.dt.uint32
I32 = mybir.dt.int32
ALU = mybir.AluOpType
ACT = mybir.ActivationFunctionType
AX = mybir.AxisListType

P = 128
BANK = 512
BATCH, SEQ, DIM = 4, 1024, 128
TOK = BATCH * SEQ
BLOCKS = TOK // P
SB = SEQ // P
CHUNKS = SEQ // BANK
CB = BANK // P
HEADS, LATENT, KDIM = 16, 32, 64
GROUP = 4
GROUPS = HEADS // GROUP
HD2 = DIM // HEADS
EXPERTS, HIDDEN, TOPK = 8, 512, 2
CAPACITY = 2 * TOK // EXPERTS
EPS = 1e-5
MASKED = -2.0 ** 126
STACK = 96
ROWS = STACK + 2
RING = 4
UNITS = 12 * GROUP
M_ITEMS = 24


class Tally:

    def __init__(self, sem, start=0, per=0, short=0):
        self.sem, self.start, self.per, self.short = sem, start, per, short
        self.base, self.n = start, 0

    def turn(self, i, first=False):
        self.base, self.n = self.start if first else self.start + i * self.per - self.short, 0

    def here(self):
        return self.base + self.n

    def loop_from_1(self, per):
        self.start, self.per = self.base + self.n - per, per

    def next(self, k=1):
        self.n += k
        return self.base + self.n


def key_blocks(c):
    return [(kb, max(0, kb - CB * c) * P) for kb in range(CB * (c + 1))]


def max_items():
    short = [((h, h + 1), qb) for qb in range(CB) for h in (0, 2)]
    long = [((h,), qb) for qb in range(CB, SB) for h in range(GROUP)]
    return short + long


NEWTON = 3
HALF_BITS = 0x5f3759df
SPACE = None


def norm_pieces(r):
    names = [("stats", 0), ("stats", 1), ("moments", 0), ("variance", 0), ("guess", 0), ("guess", 1)]
    names += [("newton", j) for j in range(3 * NEWTON)] + [("apply", 0), ("apply", 1)]
    return [("norm", (*name, r)) for name in names]


def norm_steps():
    return (norm_pieces(0) + [("norm", ("x1", 0, 0))] + norm_pieces(1) + norm_pieces(2)
            + [("norm", ("gain", 0, 2)), ("norm", ("gain", 1, 2))])


def post_steps():
    steps = [("turn x", 0), SPACE, SPACE, ("project", 0), ("project", 1), SPACE]
    steps = [step and ("post", step) for step in steps]
    steps += norm_pieces(0) + [("norm", ("gain", 0, 0)), ("norm", ("gain", 1, 0))]
    more = 4 * [SPACE] + [("turn h", 0), SPACE, SPACE, ("logits", 0)] + 4 * [SPACE] + [("exp", 0)]
    more += [("gates", j) for j in range(3)]
    more += [("choose", (0, j)) for j in range(5)] + [("left", j) for j in range(3)]
    more += [("choose", (1, j)) for j in range(5)] + [("mask", 0)] + 4 * [SPACE] + [("count", 0)]
    more += [("number", j) for j in range(2)] + [("place", j) for j in range(8)]
    for k in range(TOPK):
        more += [("ids", k)]
        for m in range(SB):
            more += [("scatter", (k, m)), SPACE]
        more += 3 * [SPACE]
    return steps + [step and ("post", step) for step in more]


POST_TILED = ("turn x", "project", "turn h", "logits", "count")
LEAD = 2
BURST = 2
TILE_COST, PLACE_COST = 100, 500
NORM_MARKS = 1 + 1 + 1 + 2 + 3 * NEWTON + 1
NORMS_MARKS = 3 * NORM_MARKS + 1
POST_MARKS = NORM_MARKS + 1 + 1 + 3 + 2 * 5 + 3 + 1 + 2 + 8 + 1


def shares(quads, items, places, sums):
    widths = [BANK - off for _, _, off in quads]
    costs = [TILE_COST + len(heads) * (qb + 1) * P for heads, qb in items]
    work = [2 * max(2 * P, widths[n]) + (4 if sums else 2) * widths[n - 1] + PLACE_COST
            for n in range(len(quads)) for _ in range(2)]
    due, done = [], 0
    for place in range(2 * len(quads)):
        part = min(1, sum(work[:place + 1]) / sum(work[:places]))
        while done < len(items) and sum(costs[:done + 1]) <= part * sum(costs) + TILE_COST:
            done += 1
        due.append(done)
    return due


def pass_steps(layer, first, last):
    quads = [(c, kb, off) for c in range(CHUNKS) for kb, off in key_blocks(c)]
    steps, after = [], []
    side = []
    if not first:
        if layer.queries:
            side = [SPACE, ("project", (0, -1)), ("project", (1, -1))] + norm_steps()
        else:
            side = post_steps()
        side = [step and (0, *step, None) for step in side]

    def finish(g, c):
        if layer.sums:
            return [(g, "inverse", (c, m), None) for m in range(CB)] + [(g, "scale", c, None)]
        return [(g, "turn", c, None)]

    def use(g, n):
        c = quads[n][0]
        first_half = [(g, "values", quads[n], n)]
        second_half = [(g, "sums", quads[n], n)] if layer.sums else []
        if n == len(quads) - 1 or quads[n + 1][0] != c:
            second_half.append((g, "drain", c, None))
        return first_half, second_half, finish(g, c) if second_half and second_half[-1][1] == "drain" else []

    def aside(many):
        for _ in range(many):
            if not after + side or waiting and waiting[0] < 0:
                return
            step = (after or side).pop(0)
            if not step:
                return
            steps.append(step)

    waiting = None if first else (-1, len(quads) - 1)
    rows_at = 2 * len(quads) - 3
    wanted = shares(quads, max_items(), rows_at - LEAD, layer.sums)
    for g in range(GROUPS):
        next_max = not (last and g == GROUPS - 1)
        items, done = max_items() if next_max else [], 0
        for n, quad in enumerate(quads):
            for h in range(GROUP):
                steps.append((g, "score", (quad, h), n))
                if h >= 2 and waiting:
                    used = use(*waiting)
                    steps += used[h - 2]
                    if h == 3:
                        after = after + used[2]
                if h % 2 == 0:
                    continue
                place = 2 * n + h // 2 + 1
                for item in items[done:wanted[place - 1]]:
                    done += 1
                    steps.append((g, "max", item, None))
                    if after or place < rows_at - LEAD - 1:
                        aside(1)
                if not next_max:
                    aside(2)
                elif place == rows_at:
                    steps.append((g, "max rows", None, None))
                    if layer.queries and not (last and g >= 1):
                        steps.append((g, "queries", None, None))
                elif place > rows_at:
                    aside(BURST)
            waiting = (g, n)
    if last:
        used = use(*waiting)
        steps += used[0] + used[1] + after + used[2] + side
        if layer.queries:
            steps += [(g, "project", (half, 0), None) for half in range(2)]
    else:
        steps += after + side
    steps = [step for step in steps if step]
    if not first:
        kinds = [(kind, what) for _, kind, what, _ in steps]
        reader = ("project", (1, -1)) if layer.queries else ("post", ("turn x", 0))
        writer = ("drain", 0) if layer.queries else ("turn", 0)
        assert kinds.index(reader) < kinds.index(("values", quads[CB - 1])) < kinds.index(writer)
    return steps


def tiled(kind, what):
    return kind in ("queries", "max", "max rows", "turn", "project") or kind == "post" and what[0] in POST_TILED


class Layer:

    def __init__(self, name, scale, sums, v_width, q_dmas, sem):
        self.scale, self.sums, self.v_width, self.q_dmas = scale, sums, v_width, q_dmas
        self.queries = sums
        self.ahead = 3 if self.queries else 2
        count = [sum(tiled(kind, what) for _, kind, what, _ in pass_steps(self, first, last))
                 for first, last in ((True, False), (False, False), (False, True))]
        self.pass_tiles, self.short = count[1], count[1] - count[0]
        assert self.pass_tiles % 2 == 0
        self.first_tiles = M_ITEMS + 1 + (3 if sums else 0)
        self.all_tiles = self.first_tiles + count[0] + (BATCH - 2) * count[1] + count[2]
        self.tile_ready = sem(f"{name}_tile_ready")
        self.tile_done = sem(f"{name}_tile_done")
        self.scores_ready = sem(f"{name}_scores_ready")
        self.probs_ready = sem(f"{name}_probs_ready")
        self.quad_done = sem(f"{name}_quad_done")
        self.inverse_ready = sem(f"{name}_inverse_ready")
        self.inverted = sem(f"{name}_inverted")
        self.chunk_free = sem(f"{name}_chunk_free")
        self.high_ready = sem(f"{name}_high_ready")
        self.masked = sem(f"{name}_masked")
        self.max_turn = sem(f"{name}_max_turn")
        self.mask_turn = sem(f"{name}_mask_turn")
        self.parts_ready = sem(f"{name}_parts_ready")
        self.stack_in = [sem(f"{name}_stack_in{r}") for r in range(RING)]
        self.max_in = [sem(f"{name}_max_in{r}") for r in range(RING)]


def build(nc, t):
    with ExitStack() as ctx:
        def sb(name, shape, dt=F32, scope=ctx):
            return scope.enter_context(nc.sbuf_tensor(name, shape, dt))

        def sem(name):
            return ctx.enter_context(nc.semaphore(name))

        tile_ps = ctx.enter_context(nc.psum_tensor("tile_ps", [P, 2, 2 * BANK], F32))
        score_ps = ctx.enter_context(nc.psum_tensor("score_ps", [P, 2, BANK], F32))
        value_ps = ctx.enter_context(nc.psum_tensor("value_ps", [P, BANK], F32))
        sum_ps = ctx.enter_context(nc.psum_tensor("sum_ps", [P, BANK], F32))

        ident = sb("ident", [P, P])
        late_key = sb("late_key", [P, SEQ], BF16)
        upper = sb("upper", [P, P])
        ones = sb("ones", [P, P])
        affine1 = sb("affine1", [P, 2, DIM])

        x = sb("x", [P, BLOCKS, DIM])
        xn = sb("xn", [P, BLOCKS, DIM])
        stats = sb("stats", [P, SB, 6])
        mean_var = sb("mean_var", [P, SB, 2])
        var_eps = sb("var_eps", [P, SB])
        rstd = sb("rstd", [P, SB])
        newton = sb("newton", [P, SB])
        gate_of = sb("gate_of", [P, TOPK, BLOCKS])
        token_no = sb("token_no", [P, SB])

        both = ctx.enter_context(ExitStack())
        q_stack = sb("q_stack", [P, RING, GROUP, SEQ], F32R, both)
        probs = sb("probs", [P, 8, BANK], F32, both)
        sum_inv = sb("sum_inv", [P, BANK], F32, both)
        turn_inv = sb("turn_inv", [P, CB, GROUP, 1], F32, both)
        max_of = sb("max_of", [P, GROUP, SB], F32, both)
        max_parts = sb("max_parts", [P, 4, GROUP * SB], F32R, both)
        max_rows = sb("max_rows", [P, P], F32R, both)

        with ExitStack() as first:
            xn_t = sb("xn_t", [P, TOK], F32, first)
            k_stack1 = sb("k_stack1", [P, RING, SEQ], F32R, first)
            v_blocks1 = sb("v_blocks1", [P, RING, SB, LATENT], F32, first)
            latent = sb("latent", [P, TOK], F32R, first)
            latent_rows = sb("latent_rows", [P, BLOCKS, LATENT], F32, first)
            q_high = sb("q_high", [P, SEQ], F32R, first)
            q_low = sb("q_low", [P, SEQ], F32R, first)
            attended = sb("attended", [P, GROUPS, SEQ], F32, first)
            down3 = sb("down3", [P, 3, LATENT], F32, first)
            absorbed_q = sb("absorbed_q", [P, HEADS * LATENT], F32, first)
            absorbed_o = sb("absorbed_o", [P, GROUPS, DIM], F32, first)
        w_in = attended
        wq_raw, wout_raw = w_in[:, 0, :], w_in[:, 1, :].rearrange("p (g o) -> p g o", g=8)
        wk_raw, wv_raw = w_in[0:LATENT, 2, :], w_in[0:LATENT, 3, :]
        wq_t = probs[:, 0:2, :].rearrange("p a (g d) -> p (a g) d", g=4)
        wkv_t = probs[:, 2, :].rearrange("p (w g c) -> p w g c", w=2, g=8)

        second = ctx.enter_context(ExitStack())
        v_tokens = sb("v_tokens", [P, BLOCKS, HEADS, HD2 + 1], F32, second)
        v_blocks2 = sb("v_blocks2", [P, RING, SB, GROUP, HD2 + 1], F32, second)
        with ExitStack() as between:
            h_t = sb("h_t", [P, SEQ], F32, between)
            wqkv = sb("wqkv", [P, 3 * DIM], F32, between)
            rope = sb("rope", [P, 2, SB, HD2 // 2], F32, between)
            qk_raw = sb("qk_raw", [P, 2, SB, 2 * DIM], F32, between)
            qk = sb("qk", [P, 2, SB, 2 * DIM], F32, between)
            rope_part = probs[:].rearrange("p u q -> p (u q)").rearrange("p (k n s) -> p k n s", k=4, n=SB)
            qk_high = sb("qk_high", [P, 2, SEQ], F32R, between)
            qk_low = sb("qk_low", [P, 2, SEQ], F32R, between)
        k_stack2 = sb("k_stack2", [P, RING, GROUP, SEQ], F32R, second)
        second.close()
        both.close()

        room = x[:, 0:SB * (BATCH - 1), :].rearrange("p n d -> p (n d)")
        taken = 0

        def cut(columns):
            nonlocal taken
            taken += columns
            assert taken <= SB * (BATCH - 1) * DIM
            return room[:, taken - columns:taken]

        def routing(columns):
            return cut(columns * EXPERTS).rearrange("p (n e) -> p n e", e=EXPERTS)

        turned = cut(SEQ)
        h2_rows = cut(SB * (DIM + 1)).rearrange("p (n d) -> p n d", n=SB)
        wproj, wgate = cut(DIM), cut(EXPERTS)
        rank, first_slot, r0 = (routing(SB) for _ in range(3))
        three, picks = routing(3 * SB), routing(3 * SB)
        gates, r1, r2 = (three[:, SB * k:SB * (k + 1), :] for k in range(3))
        chosen = [routing(SB) for _ in range(TOPK)]
        mask = routing(SB + 1)
        before = routing(1)
        row_value = cut(SB)
        picked = cut(3 * TOPK * SB).rearrange("p (k v n) -> p k v n", k=TOPK, v=3)
        slot_of, put_at = (cut(TOPK * SB).rearrange("p (k n) -> p k n", k=TOPK) for _ in range(2))
        put_at = put_at.bitcast(U32)
        attn = x[:, SB * (BATCH - 1):, :]
        affine2 = affine1

        last_part = ctx.enter_context(ExitStack())
        w1 = sb("w1", [P, 2, HIDDEN], F32, last_part)
        w2 = sb("w2", [P, 2, HIDDEN // P, DIM], F32, last_part)
        b1_rows = sb("b1_rows", [EXPERTS * HIDDEN // P, P], F32, last_part)
        b1 = sb("b1", [P, EXPERTS, HIDDEN // P], F32, last_part)
        b2 = sb("b2", [P, 2, DIM], F32, last_part)
        expert_in = sb("expert_in", [P, 2, SB, DIM + 1], F32, last_part)
        shift = sb("shift", [P, SB], F32, last_part)
        sent_back = sb("sent_back", [P, 2, SB], F32, last_part)
        out_at = sb("out_at", [P, EXPERTS, SB], U32, last_part)
        expert_in_t = sb("expert_in_t", [P, 2, 2, CAPACITY], F32R, last_part)
        w1_parts = sb("w1_parts", [P, 2, 2, HIDDEN], F32R, last_part)
        hidden = sb("hidden", [P, 2, HIDDEN // P, BANK], F32, last_part)
        expert_out = sb("expert_out", [P, 2, SB, DIM], F32, last_part)
        fetched = sb("fetched", [P, TOPK, BLOCKS, DIM], F32, last_part)
        x1_back = sb("x1_back", [P, BLOCKS, DIM], F32, last_part)

        x1_dram = nc.dram_tensor("x1_scratch", [BATCH, SEQ, DIM], F32).ap()
        q_dram = nc.dram_tensor("q_scratch", [BATCH, 2, HEADS, HD2, SEQ], F32).ap()
        k_dram = nc.dram_tensor("k_scratch", [BATCH, 2, HEADS, HD2, SEQ], F32).ap()
        slots_in = nc.dram_tensor("slots_in", [EXPERTS * CAPACITY, DIM + 1], F32).ap()
        token_out = nc.dram_tensor("token_out", [TOPK * TOK, DIM], F32).ap()

        def tokens(dram, b):
            return dram[b].rearrange("(n p) d -> p n d", p=P)

        def blocks_of(b):
            return slice(SB * b, SB * (b + 1))

        x_in = [sem(f"x_in{b}") for b in range(BATCH)]
        w_loaded, consts, ones_rows = sem("w_loaded"), sem("consts"), sem("ones_rows")
        sp_turn = sem("sp_turn")
        dve_step, dve_turn = sem("dve_step"), sem("dve_turn")
        normed = sem("normed")
        pre_ready, pre_done, high_written = sem("pre_ready"), sem("pre_done"), sem("high_written")
        stored = sem("stored")
        a1 = Layer("a1", KDIM ** -0.5, True, LATENT, 3 * GROUP + 2, sem)
        a2 = Layer("a2", HD2 ** -0.5, False, HD2 + 1, 9, sem)
        a1.k_stack, a1.v_blocks = k_stack1, v_blocks1
        a2.k_stack, a2.v_blocks = k_stack2, v_blocks2
        FIRST_TILES, PRE_TILES = 4 + 3, 4 + 3 * BATCH
        QUADS = 12
        A1_TILES, A2_TILES = a1.all_tiles, a2.all_tiles

        mid_tiles = []
        for b in range(BATCH + 1):
            if b < BATCH:
                mid_tiles += [("h", b, 0)] + [("qkv", b, k) for k in range(4)]
            if b:
                mid_tiles += [("qk", b - 1, w) for w in range(2)]

        x1_ready, x1_stored, h_ready = sem("x1_ready"), sem("x1_stored"), sem("h_ready")
        mid_loaded = sem("mid_loaded")
        mid_ready, mid_act, mid_dve = sem("mid_ready"), sem("mid_act"), sem("mid_dve")
        qk_drained, qk_turned, qk_rounded = sem("qk_drained"), sem("qk_turned"), sem("qk_rounded")
        qk_stored = sem("qk_stored")
        cleared = sem("cleared")
        first_keys_cleared, keys_cleared = sem("first_keys_cleared"), sem("keys_cleared")
        rotated = sem("rotated")
        v_ones, stack_cleared = sem("v_ones"), sem("stack_cleared")
        late_loaded, b1_loaded = sem("late_loaded"), sem("b1_loaded")
        h2_ready, exp_in, exp_out, mask_ready = sem("h2_ready"), sem("exp_in"), sem("exp_out"), sem("mask_ready")
        zeroed, ids_ready, scattered, pool_turn = sem("zeroed"), sem("ids_ready"), sem("scattered"), sem("pool_turn")
        w_in2 = [sem(f"expert_w{k}") for k in range(2)]
        e_in = [sem(f"expert_in{k}") for k in range(2)]
        e_turned, e_turned_done = sem("expert_turned"), sem("expert_turned_done")
        hid_ready, hid_done, out_ready = sem("hidden_ready"), sem("hidden_done"), sem("out_ready")
        out_done, out_stored = sem("out_done"), [sem(f"out_stored{k}") for k in range(2)]
        b1_ready, b1_turned = sem("b1_ready"), sem("b1_turned")
        fetched_in = [sem(f"fetched_in{b}") for b in range(BATCH)]
        shift_ready, normed_last = sem("shift_ready"), sem("normed_last")
        x1_loaded, final_ready = sem("x1_loaded"), sem("final_ready")

        def mid_at(kind, b, k):
            return mid_tiles.index((kind, b, k))

        def angles():
            return [rope[:, k, :, :].unsqueeze(2).broadcast_to([P, SB, 2 * HEADS, HD2 // 2]) for k in range(2)]

        def products():
            return [rope_part[:, k, :, :].rearrange("p n (s j) -> p n s j", j=HD2 // 2) for k in range(4)]

        block = ctx.enter_context(nc.Block())

        def passes(eng, do):
            do(0, True, False)
            with eng.Fori(1, BATCH - 1) as i:
                do(i, False, False)
            do(BATCH - 1, False, True)

        @block.gpsimd
        def _(pool):
            pool.memset(ident[:], 0.0).then_inc(consts, 1)
            pool.memset(late_key[:], 0.0).then_inc(consts, 1)
            pool.memset(upper[:], 1.0).then_inc(consts, 1)
            pool.memset(ones[:], 1.0).then_inc(consts, 1)
            pool.iota(token_no[:], [[P, SB]], base=1, channel_multiplier=1,
                      allow_small_or_imprecise_dtypes=True).then_inc(consts, 1)
            pool.wait_ge(consts, 5)
            pool.affine_select(out=ident[:], in_=ident[:], compare_op=ALU.not_equal, fill=1.0, base=0,
                               pattern=[[-1, P]], channel_multiplier=1).then_inc(consts, 1)
            diagonal = late_key[:, SEQ - P:]
            pool.affine_select(out=diagonal, in_=diagonal, compare_op=ALU.is_ge, fill=MASKED, base=0,
                               pattern=[[-1, P]], channel_multiplier=1).then_inc(consts, 1)
            pool.affine_select(out=upper[:], in_=upper[:], compare_op=ALU.is_ge, fill=0.0,
                               base=0, pattern=[[1, P]], channel_multiplier=-1).then_inc(consts, 1)
            pool.wait_ge(consts, 8)
            pool.memset(latent[STACK:P, :].bitcast(F32), 1.0).then_inc(ones_rows, 1)

            def mask(a):
                probs_ready = Tally(a.probs_ready, 2, UNITS * GROUPS)

                def slots(i, first, last):
                    probs_ready.turn(i)
                    for g, kind, what, quad in pass_steps(a, first, last):
                        if kind == "post" and what[0] == "scatter":
                            scatter(*what[1], i - 1)
                        if kind != "score" or what[1] < GROUP - 1:
                            continue
                        (c, kb, off), _ = what
                        exps = probs_ready.next(GROUP)
                        if kb >= CB * c:
                            pool.wait_ge(a.probs_ready, exps)
                            pool.sem_inc(a.mask_turn, 1)
                            part = probs[:, GROUP * (quad % 2):GROUP * (quad % 2 + 1), off:off + P]
                            pool.affine_select(out=part, in_=part, compare_op=ALU.is_ge, fill=0.0, base=0,
                                               pattern=[[0, GROUP], [1, P]], channel_multiplier=-1).then_inc(a.masked, 1)

                passes(pool, slots)

            def scatter(k, m, b):
                if m == 0:
                    pool.wait_ge(zeroed, 16 * 9)
                    pool.wait_ge(ids_ready, TOPK * b + k + 1)
                    pool.sem_inc(pool_turn, 1)
                pool.indirect_dma_start(
                    out=slots_in, out_offset=bass.IndirectOffsetOnAxis(ap=put_at[:, k, m:m + 1], axis=0),
                    in_=h2_rows[:, m, :], in_offset=None, bounds_check=EXPERTS * CAPACITY - 1,
                    oob_is_err=False).then_inc(scattered, 16)

            mask(a1)
            pool.wait_ge(a1.tile_done, 2 + A1_TILES)
            for rows in (slice(LATENT, 2 * LATENT), slice(2 * LATENT, P)):
                pool.memset(q_stack[rows].rearrange("p r h q -> p (r h q)").bitcast(F32), 0.0).then_inc(stack_cleared, 1)
            cos, sin = angles()
            parts = products()
            pool.wait_ge(mid_loaded, 48)
            pool.wait_ge(stack_cleared, 2)
            for b in range(BATCH):
                pool.wait_ge(qk_drained, 4 * (b + 1))
                if b:
                    pool.wait_ge(qk_turned, b)
                second = qk_raw[:, b % 2].rearrange("p n (s two j) -> p n s two j", two=2, j=HD2 // 2)[:, :, :, 1, :]
                pool.tensor_tensor(parts[1], second, sin, ALU.mult).then_inc(rotated, 1)
                pool.wait_ge(rotated, 2 * b + 1)
                pool.tensor_tensor(parts[3], second, cos, ALU.mult).then_inc(rotated, 1)
            pool.wait_ge(rotated, 2 * BATCH)
            pool.wait_ge(mid_dve, 2 * BATCH)
            for r in range(1, RING):
                if r == 2:
                    pool.wait_ge(qk_stored, 16 * 4 * BATCH)
                pool.memset(k_stack2[:, r].rearrange("p h q -> p (h q)").bitcast(F32), 1.0).then_inc(keys_cleared, 1)
            mask(a2)
            for kind, what in filter(None, post_steps()):
                if kind == "post" and what[0] == "scatter":
                    scatter(*what[1], BATCH - 1)
            for e in range(EXPERTS):
                pool.wait_ge(out_done, e + 1)
                for m in range(SB):
                    pool.indirect_dma_start(
                        out=token_out, out_offset=bass.IndirectOffsetOnAxis(ap=out_at[:, e, m:m + 1], axis=0),
                        in_=expert_out[:, e % 2, m, :], in_offset=None, bounds_check=TOPK * TOK - 1,
                        oob_is_err=False).then_inc(out_stored[e % 2], 16)
            pool.wait_ge(x1_loaded, 16 * BATCH)
            for b in range(BATCH):
                part = blocks_of(b)
                pool.wait_ge(normed_last, b + 1)
                pool.tensor_tensor(x[:, part, :], x1_back[:, part, :], xn[:, part, :], ALU.add).then_inc(final_ready, SB)

        @block.sync
        def _(sp):
            for b in range(BATCH):
                sp.dma_start(x[:, blocks_of(b), :], tokens(t["x"], b)).then_inc(x_in[b], 16)
                if b == 0:
                    sp.dma_start(wq_raw, t["wq"].rearrange("d h k -> d (h k)")).then_inc(w_loaded, 16)
                    sp.dma_start(wk_raw, t["wk"].rearrange("c h k -> c (h k)")).then_inc(w_loaded, 16)
                    sp.dma_start(wv_raw, t["wv"].rearrange("c h k -> c (h k)")).then_inc(w_loaded, 16)
                    sp.dma_start(wout_raw, t["wout"].rearrange("(g two) k o -> (two k) g o", two=2)).then_inc(w_loaded, 16)
                    for r in range(3):
                        sp.dma_start(down3[:, r, :], t["wdown"]).then_inc(w_loaded, 16)
            for k, name in enumerate(("ln1_g", "ln1_b")):
                sp.dma_start(affine1[:, k, :], t[name].partition_broadcast(P)).then_inc(w_loaded, 16)

            def max_rows_in(a, r):
                for part in range(2):
                    n = GROUP * SB
                    sp.dma_start(q_stack[STACK + part:STACK + part + 1, r, :, :].bitcast(F32)
                                 .rearrange("p h (n q) -> p (h n) q", q=P),
                                 max_rows[n * part:n * (part + 1), :].bitcast(F32)).then_inc(a.max_in[r], 16)

            def store_x1(b):
                sp.wait_ge(x1_ready, SB * b + SB)
                sp.sem_inc(sp_turn, 1)
                sp.dma_start(x1_dram[bass.ds(b, 1)].rearrange("one (n p) d -> p (one n) d", p=P),
                             x[:, bass.ds(b * SB, SB), :]).then_inc(x1_stored, 16)

            def slots_of(a, stack_in):
                tile_done = Tally(a.tile_done, 2, a.pass_tiles, a.short)
                for g in range(2):
                    if a.queries:
                        sp.wait_ge(a.tile_done, tile_done.next())
                    else:
                        sp.wait_ge((first_keys_cleared, keys_cleared)[g], 1)
                    stack_in(g, 0)
                sp.wait_ge(a.tile_done, tile_done.next(M_ITEMS + 1))
                max_rows_in(a, 0)
                if a.queries:
                    sp.wait_ge(a.tile_done, tile_done.next())
                    stack_in(2, 0)
                if a.queries:
                    sp.wait_ge(pre_done, PRE_TILES)
                else:
                    router_in()
                    sp.wait_ge(keys_cleared, RING - 1)
                tile_done.start += a.first_tiles

                def slots(i, first, last):
                    tile_done.turn(i, first)
                    at = -1
                    for g, kind, what, _ in pass_steps(a, first, last):
                        done = tile_done.next() if tiled(kind, what) else None
                        if kind == "queries":
                            sp.wait_ge(a.tile_done, done)
                            stack_in((g + 3) % GROUPS, i if g < 1 else i + 1)
                        elif not a.queries and g > at and not (last and g >= 2):
                            sp.wait_ge(a.inverse_ready, 2 * GROUPS * i + 2 * g + 1)
                            stack_in((g + 2) % GROUPS, i if g < 2 else i + 1)
                        if kind == "max rows":
                            sp.wait_ge(a.tile_done, done)
                            max_rows_in(a, (g + 1) % RING)
                            if first and not a.queries:
                                zero_slots(g)
                        elif a.queries and kind == "norm" and what[0] == "x1":
                            store_x1(i - 1)
                        at = max(at, g)

                passes(sp, slots)

            def stack_in1(g, b):
                done = a1.stack_in[g]
                for j in range(GROUP):
                    rows = slice(LATENT * j, LATENT * (j + 1))
                    for part, src in enumerate((q_high, q_high, q_low)):
                        sp.dma_start(q_stack[LATENT * part:LATENT * (part + 1), g, j, :].bitcast(F32),
                                     src[rows, :].bitcast(F32)).then_inc(done, 16)
                sp.dma_start(k_stack1[0:ROWS, g, :].bitcast(F32),
                             latent[0:ROWS, bass.ds(b * SEQ, SEQ)].bitcast(F32)).then_inc(done, 16)
                sp.dma_start(v_blocks1[:, g, :, :], latent_rows[:, bass.ds(b * SB, SB), :]).then_inc(done, 16)

            def stack_in2(g, b):
                done = a2.stack_in[g]
                sp.wait_ge(qk_stored, 16 * 4 * BATCH)
                heads = slice(GROUP * g, GROUP * (g + 1))
                for part in range(4):
                    rows = slice(HD2 * part, HD2 * (part + 1))
                    for stack, dram, low in ((q_stack, q_dram, part // 2), (k_stack2, k_dram, part % 2)):
                        src = dram[bass.ds(b, 1), low, heads, :, :].rearrange("one h c q -> c (one h) q")
                        sp.dma_start(stack[rows, g, :, :].bitcast(F32), src).then_inc(done, 16)
                sp.dma_start(v_blocks2[:, g, :, :, :], v_tokens[:, bass.ds(b * SB, SB), heads, :]).then_inc(done, 16)

            def zero_slots(r):
                rows, columns = q_stack[STACK - 64:STACK, r], GROUP * SEQ
                for dram in (slots_in, token_out):
                    part = dram.rearrange("s d -> (s d)")[64 * columns * r:64 * columns * (r + 1)]
                    sp.dma_start(part.rearrange("(p f) -> p f", p=64),
                                 rows.rearrange("p h q -> p (h q)").bitcast(F32)).then_inc(zeroed, 16)
                if r == 0:
                    rest = slots_in.rearrange("s d -> (s d)")[64 * columns * RING:].rearrange("(p f) -> p f", p=64)
                    sp.dma_start(rest, rows[:, 0, 0:EXPERTS * CAPACITY // 64].bitcast(F32)).then_inc(zeroed, 16)

            def router_in():
                sp.dma_start(wproj, t["wproj"]).then_inc(late_loaded, 16)
                sp.dma_start(wgate, t["wgate"]).then_inc(late_loaded, 16)
                for k, name in enumerate(("ln2_g", "ln2_b")):
                    sp.dma_start(affine2[:, k, :], t[name].partition_broadcast(P)).then_inc(late_loaded, 16)

            sp.wait_ge(pre_done, FIRST_TILES)
            sp.wait_ge(ones_rows, 1)
            slots_of(a1, stack_in1)

            sp.wait_ge(a1.tile_done, 2 + A1_TILES)
            sp.dma_start(wqkv[:], t["wqkv"]).then_inc(mid_loaded, 16)
            for k, name in enumerate(("rope_cos", "rope_sin")):
                sp.dma_start(rope[:, k, :, :], t[name].rearrange("(n p) j -> p n j", p=P)).then_inc(mid_loaded, 16)
            store_x1(BATCH - 1)
            for b in range(BATCH):
                for w, dram in enumerate((q_dram, k_dram)):
                    sp.wait_ge(mid_dve, 2 * b + w + 1)
                    for low, src in enumerate((qk_high, qk_low)):
                        sp.dma_start(dram[b, low].rearrange("h c q -> (h c) q"),
                                     src[:, w, :].bitcast(F32)).then_inc(qk_stored, 16)
            sp.wait_ge(qk_stored, 16 * 4 * BATCH)
            sp.wait_ge(stack_cleared, 2)
            sp.wait_ge(v_ones, 1)
            slots_of(a2, stack_in2)

            sp.wait_ge(a2.tile_done, 2 + A2_TILES)
            sp.wait_ge(zeroed, 16 * 9)
            sp.dma_start(b1_rows[:], t["b1"].rearrange("e (f p) -> (e f) p", p=P)).then_inc(b1_loaded, 16)

            def weights_in(e, k):
                sp.dma_start(w1[:, k, :], t["w1"][e]).then_inc(w_in2[k], 16)
                sp.dma_start(w2[:, k, :, :], t["w2"][e].rearrange("(f p) d -> p f d", p=P)).then_inc(w_in2[k], 16)
                sp.dma_start(b2[:, k, :], t["b2"][e].partition_broadcast(P)).then_inc(w_in2[k], 16)

            def expert_rows_in(e, k):
                sp.dma_start(expert_in[:, k, :, :],
                             slots_in[CAPACITY * e:CAPACITY * (e + 1), :].rearrange("(n p) d -> p n d", p=P)
                             ).then_inc(e_in[k], 16)

            weights_in(0, 0)
            weights_in(1, 1)
            sp.wait_ge(scattered, 16 * TOPK * BLOCKS)
            expert_rows_in(0, 0)
            expert_rows_in(1, 1)
            for e in range(EXPERTS - 2):
                sp.wait_ge(out_done, e + 1)
                weights_in(e + 2, e % 2)
                expert_rows_in(e + 2, e % 2)
                if e < BATCH:
                    sp.dma_start(x1_back[:, blocks_of(e), :], tokens(x1_dram, e)).then_inc(x1_loaded, 16)
            for k in range(2):
                sp.wait_ge(out_stored[k], 16 * SB * EXPERTS // 2)
            for b in range(BATCH):
                for k in range(TOPK):
                    at = TOK * k + SEQ * b
                    sp.dma_start(fetched[:, k, blocks_of(b), :],
                                 token_out[at:at + SEQ, :].rearrange("(n p) d -> p n d", p=P)).then_inc(fetched_in[b], 16)
            for b in range(BATCH):
                sp.wait_ge(final_ready, SB * (b + 1))
                sp.dma_start(tokens(t["out"], b), x[:, blocks_of(b), :]).then_inc(stored, 16)
            sp.wait_ge(stored, 16 * BATCH)

        @block.scalar
        def _(act):
            def copy(out, src):
                return act.activation(out, src, ACT.Copy)

            n = 0

            def drain(out, src):
                nonlocal n
                act.wait_ge(pre_ready, n + 1)
                copy(out, src).then_inc(pre_done, 1)
                n += 1

            drain(wq_t.rearrange("p g d -> p (g d)"), tile_ps[:, 0, :])
            drain(wkv_t.rearrange("p w g c -> p (w g c)"), tile_ps[:, 1, 0:2 * 8 * LATENT])
            drain(absorbed_q[:].rearrange("p (g two c) -> p two g c", two=2, c=LATENT),
                  tile_ps[:, 0, :].rearrange("p (two k) -> p two k", two=2)[:, :, 0:8 * LATENT]
                  .rearrange("p two (g c) -> p two g c", c=LATENT))
            act.wait_ge(pre_ready, n + 1)
            for j in range(GROUP):
                rows, col = slice(LATENT * j, LATENT * (j + 1)), BANK * (j % 2)
                last = copy(absorbed_o[rows, :, :], tile_ps[rows, 1, col:col + BANK].rearrange("p (g o) -> p g o", o=DIM))
            last.then_inc(pre_done, 1)
            n += 1
            for b in range(BATCH):
                drain(xn_t[:, SEQ * b:SEQ * (b + 1)], tile_ps[:, n % 2, :])
                act.wait_ge(pre_ready, n + 1)
                copy(latent[0:STACK, SEQ * b:SEQ * (b + 1)], tile_ps[0:STACK, n % 2, :]).then_inc(high_written, 1)
                n += 1
                act.wait_ge(pre_done, n)
                drain(latent_rows[:, SB * b:SB * (b + 1), :].rearrange("p n c -> p (n c)"), tile_ps[:, n % 2, 0:SB * LATENT])
            assert n == PRE_TILES

            def gate_exp(b):
                act.wait_ge(exp_in, b + 1)
                act.activation(gates, r0, ACT.Exp).then_inc(exp_out, 1)

            def exponentials(a):
                act.sem_inc(a.probs_ready, 2)
                act.sem_inc(a.chunk_free, 1)
                scores_ready = Tally(a.scores_ready, 0, UNITS * GROUPS)
                quad_used = Tally(a.quad_done, 0, QUADS * GROUPS)
                quad_done = Tally(a.quad_done, 2, QUADS * GROUPS, SB)
                inverse_ready = Tally(a.inverse_ready, 2, 2 * GROUPS, 1)

                def slots(i, first, last):
                    for tally in (scores_ready, quad_used, quad_done, inverse_ready):
                        tally.turn(i, first)
                    for g, kind, what, quad in pass_steps(a, first, last):
                        if kind == "score":
                            (c, kb, off), h = what
                            u = GROUP * quad + h
                            if h == 0:
                                act.wait_ge(a.quad_done, quad_used.next())
                            act.wait_ge(a.scores_ready, scores_ready.next())
                            act.activation(probs[:, u % 8, off:], score_ps[:, u % 2, off:], ACT.Exp,
                                           scale=a.scale).then_inc(a.probs_ready, 1)
                        elif kind == "drain":
                            act.wait_ge(a.quad_done, quad_done.next(len(key_blocks(what))))
                            act.wait_ge(a.inverse_ready, inverse_ready.next())
                            if a.sums:
                                copy(attended[:, g % GROUPS, BANK * what:BANK * (what + 1)], value_ps[:])
                                copy(sum_inv[:], sum_ps[:]).then_inc(a.chunk_free, 1)
                            else:
                                copy(sum_inv[:], value_ps[:]).then_inc(a.chunk_free, 1)
                        elif kind == "post" and what[0] == "exp":
                            gate_exp(i - 1)

                passes(act, slots)

            exponentials(a1)

            def rounded(b):
                if b:
                    act.wait_ge(qk_stored, 16 * 4 * b)
                for w in range(2):
                    at = mid_at("qk", b, w)
                    act.wait_ge(mid_ready, at + 1)
                    copy(qk_high[:, w, :], tile_ps[:, at % 2, :]).then_inc(qk_rounded, 1)

            for b in range(BATCH):
                at = mid_at("h", b, 0)
                act.wait_ge(mid_ready, at + 1)
                copy(h_t[:], tile_ps[:, at % 2, :]).then_inc(mid_act, 1)
                if b == 0:
                    act.wait_ge(v_ones, 1)
                if b >= 2:
                    act.wait_ge(qk_turned, b - 1)
                for m in range(4):
                    at = mid_at("qkv", b, m)
                    act.wait_ge(mid_ready, at + 1)
                    tile = tile_ps[:, at % 2, :].rearrange("p (n c) -> p n c", n=2)
                    copy(qk_raw[:, b % 2, 2 * m:2 * m + 2, :], tile[:, :, 0:2 * DIM]).then_inc(qk_drained, 1)
                    for two in range(2):
                        last = copy(v_tokens[:, SB * b + 2 * m + two, :, 0:HD2],
                                    tile[:, two, 2 * DIM:3 * DIM].rearrange("p (h c) -> p h c", c=HD2))
                    last.then_inc(mid_act, 1)
                if b:
                    rounded(b - 1)
            rounded(BATCH - 1)

            exponentials(a2)

            gate_exp(BATCH - 1)
            act.wait_ge(b1_turned, 1)
            for e in range(EXPERTS):
                act.wait_ge(w_in2[e % 2], 48 * (e // 2 + 1))
                for c in range(2):
                    for f in range(HIDDEN // P):
                        unit = 8 * e + 4 * c + f
                        act.wait_ge(hid_ready, unit + 1)
                        if f == 0 and 2 * e + c >= 2:
                            act.wait_ge(out_ready, 2 * e + c - 1)
                        act.activation(hidden[:, c, f, :], score_ps[:, unit % 2, :], ACT.Gelu,
                                       bias=b1[:, e, f:f + 1]).then_inc(hid_done, 1)
            for b in range(BATCH):
                act.wait_ge(shift_ready, b + 1)
                for n in range(SB):
                    row = xn[:, SB * b + n, :]
                    last = act.activation(row, row, ACT.Identity, bias=shift[:, n:n + 1], scale=rstd[:, n:n + 1])
                last.then_inc(normed_last, 1)

        @block.tensor
        def _(pe):
            pe.wait_ge(consts, 8)
            pe.wait_ge(w_loaded, 16 * 9)
            for g in range(8):
                last = pe.transpose(tile_ps[:, 0, P * g:P * (g + 1)], wq_raw[:, P * g:P * (g + 1)], ident[:])
            last.then_inc(pre_ready, 1)
            for w, raw in enumerate((wk_raw, wv_raw)):
                for g in range(8):
                    at = (8 * w + g) * LATENT
                    last = pe.transpose(tile_ps[:, 1, at:at + LATENT], raw[:, P * g:P * (g + 1)], ident[0:LATENT, 0:LATENT])
            last.then_inc(pre_ready, 1)
            pe.wait_ge(pre_done, 2)
            for h in range(HEADS):
                k = slice(KDIM * (h % 2), KDIM * (h % 2 + 1))
                col = BANK * (h % 2) + LATENT * (h // 2)
                last = pe.matmul(tile_ps[:, 0, col:col + LATENT], wq_t[k, h // 2, :], wkv_t[k, 0, h // 2, :],
                                 start=True, stop=True)
            last.then_inc(pre_ready, 1)
            for h in range(HEADS):
                k = slice(KDIM * (h % 2), KDIM * (h % 2 + 1))
                j, g = h % GROUP, h // GROUP
                col = BANK * (h % 2) + P * g
                last = pe.matmul(tile_ps[LATENT * j:LATENT * (j + 1), 1, col:col + P],
                                 wkv_t[k, 1, h // 2, :], wout_raw[k, h // 2, :], start=True, stop=True)
            last.then_inc(pre_ready, 1)

            def latents(b, n):
                pe.wait_ge(normed, SB * (b + 1))
                pe.wait_ge(pre_done, n - 1)
                for m in range(SB):
                    last = pe.transpose(tile_ps[:, n % 2, P * m:P * (m + 1)], xn[:, SB * b + m, :], ident[:])
                last.then_inc(pre_ready, 1)
                n += 1
                pe.wait_ge(pre_done, n)
                for c in range(CHUNKS):
                    at = SEQ * b + BANK * c
                    last = pe.matmul(tile_ps[0:STACK, n % 2, BANK * c:BANK * (c + 1)],
                                     down3[:].rearrange("p r c -> p (r c)"), xn_t[:, at:at + BANK], start=True, stop=True)
                last.then_inc(pre_ready, 1)
                n += 1
                for m in range(SB):
                    at = SEQ * b + P * m
                    last = pe.matmul(tile_ps[:, n % 2, LATENT * m:LATENT * (m + 1)], xn_t[:, at:at + P],
                                     down3[:, 0, :], start=True, stop=True)
                last.then_inc(pre_ready, 1)

            def other_latents(tile_done):
                pe.wait_ge(*tile_done)
                for b in range(1, BATCH):
                    latents(b, 4 + 3 * b)
                pe.wait_ge(pre_done, PRE_TILES)

            latents(0, 4)
            pe.wait_ge(pre_done, FIRST_TILES)

            def attention(a):
                pe.sem_inc(a.quad_done, 2)
                tile_done = Tally(a.tile_done, 0, a.pass_tiles, a.short)
                probs_ready = Tally(a.probs_ready, 0, UNITS * GROUPS)
                chunk_free = Tally(a.chunk_free, 0, 2 * GROUPS)
                masked = Tally(a.masked, 0, SB * GROUPS, 1)
                tiles = 0

                def next_tile():
                    nonlocal tiles
                    pe.wait_ge(a.tile_done, tile_done.next())
                    tiles += 1
                    return tile_ps[:, (tiles - 1) % 2, :]

                def keys_of(r, h):
                    return a.k_stack[0:ROWS, r, :] if a.queries else a.k_stack[0:ROWS, r, h, :]

                def queries(g, b):
                    tile = next_tile()
                    for c in range(CHUNKS):
                        last = pe.matmul(tile[:, BANK * c:BANK * (c + 1)], absorbed_q[:, P * g:P * (g + 1)],
                                         xn_t[:, bass.ds(b * SEQ + BANK * c, BANK)], start=True, stop=True)
                    last.then_inc(a.tile_ready, 1)

                def max_scores(r, heads, qb):
                    tile = next_tile()
                    keys = (qb + 1) * P
                    for at, h in enumerate(heads):
                        for k0 in range(0, keys, BANK):
                            wide = max(2 * P, min(BANK, keys - k0))
                            col = BANK * at + k0
                            last = pe.matmul(tile[:, col:col + wide], q_stack[0:STACK, r, h, P * qb:P * (qb + 1)],
                                             keys_of(r, h)[0:STACK, k0:k0 + wide], start=True, stop=True)
                    last.then_inc(a.tile_ready, 1)

                def max_to_rows(parts):
                    pe.wait_ge(a.parts_ready, parts)
                    tile = next_tile()
                    pe.transpose(tile[:, 0:P], max_parts[:].rearrange("p a b -> p (a b)").bitcast(F32),
                                 ident[:]).then_inc(a.tile_ready, 1)

                def score(r, c, kb, off, h, unit):
                    pe.wait_ge(a.probs_ready, probs_ready.next())
                    start = min(off, BANK - 2 * P)
                    last = pe.matmul(score_ps[:, unit % 2, start:], keys_of(r, h)[:, P * kb:P * (kb + 1)],
                                     q_stack[0:ROWS, r, h, BANK * c + start:BANK * (c + 1)],
                                     start=True, stop=True)
                    last.then_inc(a.scores_ready, 1)

                def values(r, c, kb, off, quad, ready):
                    r %= RING
                    if kb == 0:
                        pe.wait_ge(a.chunk_free, chunk_free.next())
                    if kb >= CB * c:
                        pe.wait_ge(a.masked, masked.next())
                    else:
                        pe.wait_ge(a.probs_ready, ready)
                    for h in range(GROUP):
                        v = a.v_blocks[:, r, kb, :] if a.queries else a.v_blocks[:, r, kb, h, :]
                        last = pe.matmul(value_ps[LATENT * h:LATENT * h + a.v_width, off:], v,
                                         probs[:, (GROUP * quad + h) % 8, off:],
                                         start=kb == 0, stop=True, skip_group_check=True)
                    return last

                def sums(kb, off, quad):
                    for h in range(GROUP):
                        last = pe.matmul(sum_ps[LATENT * h:LATENT * (h + 1), off:], ones[:, 0:LATENT],
                                         probs[:, (GROUP * quad + h) % 8, off:],
                                         start=kb == 0, stop=True, skip_group_check=True)
                    return last

                def turn(drained):
                    pe.wait_ge(a.chunk_free, drained)
                    tile = next_tile()
                    for m in range(CB):
                        last = pe.transpose(tile[:, P * m:P * (m + 1)], sum_inv[:, P * m:P * (m + 1)], ident[:])
                    last.then_inc(a.tile_ready, 1)

                def project(half, scaled):
                    pe.wait_ge(a.inverse_ready, 2 * scaled + 3)
                    tile = next_tile()
                    for m in range(CB):
                        q = P * (CB * half + m)
                        for g in range(GROUPS):
                            mm = pe.matmul(tile[:, P * m:P * (m + 1)], attended[:, g, q:q + P],
                                           absorbed_o[:, g, :], start=g == 0, stop=g == GROUPS - 1)
                    mm.then_inc(a.tile_ready, 1)

                if a.queries:
                    queries(0, 0)
                    other_latents((a.tile_done, 2 + 1))
                    queries(1, 0)
                pe.wait_ge(a.stack_in[0], 16 * a.q_dmas)
                for heads, qb in max_items():
                    max_scores(0, heads, qb)
                max_to_rows(1)
                if a.queries:
                    queries(2, 0)
                tile_done.start += a.first_tiles

                def slots(i, first, last):
                    for tally in (tile_done, probs_ready, chunk_free, masked):
                        tally.turn(i, first)
                    at = -1
                    for g, kind, what, quad in pass_steps(a, first, last):
                        if kind == "queries":
                            queries((g + 3) % GROUPS, i if g < 1 else i + 1)
                            continue
                        if g > at:
                            if not (last and g == 3):
                                pe.wait_ge(a.stack_in[(g + 1) % RING], 16 * a.q_dmas * (i + (1 if g < 3 else 2)))
                            pe.wait_ge(a.max_in[g], 32 * (i + 1))
                            at = g
                        if kind == "score":
                            score(g, *what[0], what[1], GROUP * quad + what[1])
                        elif kind == "max":
                            max_scores((g + 1) % RING, *what)
                        elif kind == "max rows":
                            max_to_rows(GROUPS * i + g + 2)
                        elif kind == "values":
                            mm = values(g, *what, quad, UNITS * (GROUPS * i + g) + 2 + GROUP * (quad + 1))
                            if not a.sums:
                                mm.then_inc(a.quad_done, 1)
                        elif kind == "sums":
                            sums(*what[1:], quad).then_inc(a.quad_done, 1)
                        elif kind == "turn":
                            turn(2 * (GROUPS * i + g) + what + 2)
                        elif kind == "project":
                            half, back = what
                            project(half, GROUPS * (i + back) + GROUPS)
                        elif tiled(kind, what):
                            post(*what, i - 1)
                    if first and not a.queries:
                        pe.wait_ge(late_loaded, 64)

                def post(name, half, b):
                    if name == "turn h":
                        pe.wait_ge(h2_ready, b + 1)
                    if name == "count":
                        pe.wait_ge(mask_ready, b + 1)
                    tile = next_tile()
                    if name in ("turn x", "logits") or name == "project" and half == 0:
                        pe.wait_ge(a.tile_done, tile_done.here() + 1)
                    if name in ("turn x", "turn h"):
                        for m in range(SB):
                            src = attn[:, m, :] if name == "turn x" else h2_rows[:, m, 0:DIM]
                            last = pe.transpose(tile[:, P * m:P * (m + 1)], src, ident[:])
                    elif name == "count":
                        flat = mask.rearrange("p n e -> p (n e)")
                        pe.matmul(tile[:, 0:EXPERTS * (SB + 1)], upper[:], flat, start=True, stop=True, skip_group_check=True)
                        for n in range(1, SB + 1):
                            last = pe.matmul(tile[:, EXPERTS * n:EXPERTS * (SB + 1)], ones[:], flat[:, 0:EXPERTS * (SB + 1 - n)],
                                             start=False, stop=True, skip_group_check=True)
                    else:
                        weight, width = (wproj, P) if name == "project" else (wgate, EXPERTS)
                        for m in range(CB * half, CB * (half + 1)) if name == "project" else range(SB):
                            last = pe.matmul(tile[:, width * m:width * (m + 1)], turned[:, P * m:P * (m + 1)], weight,
                                             start=True, stop=True)
                    last.then_inc(a.tile_ready, 1)

                passes(pe, slots)
                if not a.queries:
                    for kind, what in filter(None, post_steps()):
                        if tiled(kind, what):
                            post(*what, BATCH - 1)

            attention(a1)

            pe.wait_ge(mid_loaded, 48)
            pe.wait_ge(a1.tile_done, 2 + A1_TILES)

            def mid_tile(kind, b, k):
                at = mid_at(kind, b, k)
                if at >= 2:
                    kinds = [what[0] == "qk" for what in mid_tiles[:at - 1]]
                    if kinds[-1]:
                        pe.wait_ge(mid_dve, sum(kinds))
                    else:
                        pe.wait_ge(mid_act, len(kinds) - sum(kinds))
                return tile_ps[:, at % 2, :]

            by_kind = wqkv[:].rearrange("p (h s c) -> p s h c", s=3, c=HD2)
            for b in range(BATCH + 1):
                if b < BATCH:
                    pe.wait_ge(h_ready, b + 1)
                    tile = mid_tile("h", b, 0)
                    for m in range(SB):
                        last = pe.transpose(tile[:, P * m:P * (m + 1)], x[:, SB * b + m, :], ident[:])
                    last.then_inc(mid_ready, 1)
                    pe.wait_ge(mid_act, 5 * b + 1)
                    for k in range(4):
                        tile = mid_tile("qkv", b, k)
                        for two in range(2):
                            m = 2 * k + two
                            last = pe.matmul(tile[:, BANK * two:BANK * two + 3 * DIM], h_t[:, P * m:P * (m + 1)],
                                             by_kind, start=True, stop=True)
                        last.then_inc(mid_ready, 1)
                if b:
                    pe.wait_ge(qk_turned, b)
                    for w in range(2):
                        tile = mid_tile("qk", b - 1, w)
                        for m in range(SB):
                            last = pe.transpose(tile[:, P * m:P * (m + 1)], qk[:, (b - 1) % 2, m, DIM * w:DIM * (w + 1)],
                                                ident[:])
                        last.then_inc(mid_ready, 1)

            pe.wait_ge(mid_dve, 2 * BATCH)
            pe.wait_ge(cleared, 1)
            attention(a2)

            pe.wait_ge(b1_loaded, 16)
            pe.transpose(score_ps[:, 0, 0:EXPERTS * HIDDEN // P], b1_rows[:], ident[0:EXPERTS * HIDDEN // P, 0:EXPERTS * HIDDEN // P]
                         ).then_inc(b1_ready, 1)
            pe.wait_ge(b1_turned, 1)

            def expert_turn(e):
                pe.wait_ge(e_in[e % 2], 16 * (e // 2 + 1))
                if e:
                    pe.wait_ge(e_turned_done, e)
                for m in range(SB):
                    last = pe.transpose(tile_ps[:, 0, P * m:P * (m + 1)], expert_in[:, e % 2, m, 0:DIM], ident[:])
                last.then_inc(e_turned, 1)

            def expert_hidden(e, c):
                for f in range(HIDDEN // P):
                    unit = 8 * e + 4 * c + f
                    if unit >= 2:
                        pe.wait_ge(hid_done, unit - 1)
                    for step, (low_w, low_x) in enumerate(((0, 0), (0, 1), (1, 0))):
                        mm = pe.matmul(score_ps[:, unit % 2, :], w1_parts[:, e % 2, low_w, P * f:P * (f + 1)],
                                       expert_in_t[:, e % 2, low_x, BANK * c:BANK * (c + 1)], start=step == 0, stop=step == 2)
                    mm.then_inc(hid_ready, 1)

            def expert_output(e, c):
                pe.wait_ge(hid_done, 8 * e + 4 * (c + 1))
                if c == 0 and e:
                    pe.wait_ge(out_done, e)
                for m in range(CB):
                    for f in range(HIDDEN // P):
                        last = pe.matmul(tile_ps[:, 1, BANK * c + P * m:BANK * c + P * (m + 1)],
                                         hidden[:, c, f, P * m:P * (m + 1)], w2[:, e % 2, f, :],
                                         start=f == 0, stop=f == HIDDEN // P - 1)
                last.then_inc(out_ready, 1)

            expert_turn(0)
            for e in range(EXPERTS):
                pe.wait_ge(w_in2[e % 2], 48 * (e // 2 + 1))
                pe.wait_ge(e_turned_done, e + 1)
                expert_hidden(e, 0)
                expert_hidden(e, 1)
                expert_output(e, 0)
                if e + 1 < EXPERTS:
                    expert_turn(e + 1)
                expert_output(e, 1)

        @block.vector
        def _(dve):
            chain = Tally(dve_step, 0, NORMS_MARKS)

            def mark(ins):
                chain.next()
                ins.then_inc(dve_step, 1)

            def caught():
                dve.wait_ge(dve_step, chain.base + chain.n)

            def link(ins):
                mark(ins)
                caught()

            def norm_piece(piece, j, src, out):
                half = range(CB * j, CB * (j + 1))
                if piece == "stats":
                    if j == 0:
                        dve.sem_inc(dve_turn, 1)
                    for n in half:
                        ins = dve.bn_stats(stats[:, n, :], src[:, n, :])
                    if j == 1:
                        mark(ins)
                elif piece == "moments":
                    caught()
                    dve.sem_inc(dve_turn, 1)
                    for n in range(SB):
                        ins = dve.bn_aggr(mean_var[:, n, :], stats[:, n, :])
                    mark(ins)
                elif piece == "variance":
                    caught()
                    mark(dve.tensor_scalar(var_eps[:], mean_var[:, :, 1], EPS, None, ALU.add))
                elif piece == "guess":
                    caught()
                    bits = newton[:].bitcast(I32)
                    if j == 0:
                        mark(dve.tensor_scalar(bits, var_eps[:].bitcast(I32), 1, None, ALU.logical_shift_right))
                    else:
                        mark(dve.tensor_scalar(rstd[:].bitcast(I32), bits, -1.0, float(HALF_BITS), ALU.mult, ALU.add))
                elif piece == "newton":
                    caught()
                    if j % 3 == 0:
                        mark(dve.tensor_tensor(newton[:], rstd[:], rstd[:], ALU.mult))
                    elif j % 3 == 1:
                        mark(dve.scalar_tensor_tensor(out=newton[:], in0=newton[:], scalar=-0.5, in1=var_eps[:],
                                                      op0=ALU.mult, op1=ALU.mult))
                    else:
                        mark(dve.scalar_tensor_tensor(out=rstd[:], in0=newton[:], scalar=1.5, in1=rstd[:],
                                                      op0=ALU.add, op1=ALU.mult))
                elif piece == "apply":
                    if j == 0:
                        caught()
                    for n in half:
                        ins = dve.tensor_scalar(out[:, n, :], src[:, n, :], mean_var[:, n, 0:1], rstd[:, n:n + 1],
                                                ALU.subtract, ALU.mult)
                    if j == 1:
                        mark(ins)

            def norm(src, b, out):
                for _, (piece, j, _) in filter(None, norm_pieces(0)):
                    norm_piece(piece, j, src[:, blocks_of(b), :], out[:, blocks_of(b), :])
                caught()

            def gain_piece(j, part, vectors, signal):
                caught()
                ins = dve.tensor_tensor(part, part, vectors[:, j, :].unsqueeze(1).broadcast_to([P, SB, DIM]),
                                        (ALU.mult, ALU.add)[j])
                if j == 0:
                    mark(ins)
                else:
                    ins.then_inc(signal, 1)

            def mid_norm(what, b):
                piece, j, r = what
                part = bass.ds(b * SB, SB)
                if piece == "stats" and j == 0 and r == 1:
                    dve.wait_ge(x1_ready, SB * b + SB)
                if piece == "stats" and j == 0 and r == 2:
                    caught()
                if piece == "apply" and j == 0 and r == 2:
                    dve.wait_ge(x1_stored, 16 * b + 16)
                if piece == "gain":
                    gain_piece(j, x[:, part, :], affine1, h_ready)
                elif piece == "x1":
                    caught()
                    dve.tensor_tensor(x[:, part, :], x[:, part, :], xn[:, part, :], ALU.add).then_inc(x1_ready, SB)
                else:
                    norm_piece(piece, j, (xn, x, xn)[r][:, part, :], (xn, xn, x)[r][:, part, :])

            link(dve.memset(max_parts[:].rearrange("p a b -> p (a b)").bitcast(F32), 0.0))

            def first_norm(b):
                dve.wait_ge(x_in[b], 16)
                norm(x, b, xn)
                dve.sem_inc(normed, SB)

            def latent_rest(b):
                dve.wait_ge(high_written, b + 1)
                rows = slice(LATENT, 2 * LATENT)
                dve.tensor_tensor(latent[rows, SEQ * b:SEQ * (b + 1)], tile_ps[rows, (5 + 3 * b) % 2, :],
                                  latent[rows, SEQ * b:SEQ * (b + 1)].bitcast(F32), ALU.subtract).then_inc(pre_done, 1)

            def other_latents():
                first_norm(2)
                latent_rest(1)
                first_norm(3)
                latent_rest(2)
                latent_rest(3)

            first_norm(0)
            first_norm(1)
            latent_rest(0)
            dve.wait_ge(w_loaded, 16 * 9)
            dve.wait_ge(consts, 8)

            def attention(a):
                dve.sem_inc(a.tile_done, 2)
                dve.sem_inc(a.inverse_ready, 3)
                tile_ready = Tally(a.tile_ready, 0, a.pass_tiles, a.short)
                tile_done = Tally(a.tile_done, 2, a.pass_tiles, a.short)
                high_ready = Tally(a.high_ready, 0, (2 if a.queries else 1) * GROUPS)
                inverted = Tally(a.inverted, 0, 2 * GROUPS, 1)
                chunk_free = Tally(a.chunk_free, 1, 2 * GROUPS, 1)
                tiles = 0

                def next_tile():
                    nonlocal tiles
                    dve.wait_ge(a.tile_ready, tile_ready.next())
                    tile_done.next()
                    tiles += 1
                    return tile_ps[:, (tiles - 1) % 2, :]

                def queries(last_use):
                    tile = next_tile()
                    if last_use:
                        dve.wait_ge(*last_use)
                    dve.tensor_copy(q_high[:], tile).then_inc(a.high_ready, 1)
                    dve.wait_ge(a.high_ready, high_ready.next())
                    dve.tensor_tensor(q_low[:], tile, q_high[:].bitcast(F32), ALU.subtract).then_inc(a.tile_done, 1)

                def max_scores(heads, qb):
                    tile = next_tile()
                    dve.sem_inc(a.max_turn, 1)
                    keys = (qb + 1) * P
                    for at, h in enumerate(heads):
                        row = tile[:, BANK * at:BANK * at + keys]
                        ins = dve.tensor_tensor_reduce(row, row, late_key[:, SEQ - keys:], 1.0, MASKED, ALU.add, ALU.max,
                                                       max_of[:, h, qb:qb + 1])
                    ins.then_inc(a.tile_done, 1)

                def max_to_rows(last_use):
                    dve.wait_ge(a.tile_done, tile_done.base + tile_done.n)
                    flat = max_of[:].rearrange("p h n -> p (h n)")
                    dve.tensor_scalar(max_parts[:, 0, :], flat, -1.0, None, ALU.mult).then_inc(a.high_ready, 1)
                    dve.wait_ge(a.high_ready, high_ready.next())
                    dve.scalar_tensor_tensor(out=max_parts[:, 1, :], in0=flat, scalar=-1.0, in1=max_parts[:, 0, :].bitcast(F32),
                                             op0=ALU.mult, op1=ALU.subtract).then_inc(a.parts_ready, 1)
                    tile = next_tile()
                    if last_use:
                        dve.wait_ge(*last_use)
                    dve.tensor_copy(max_rows[:], tile[:, 0:P]).then_inc(a.tile_done, 1)

                def inverse(c, m):
                    part = sum_inv[:, P * m:P * (m + 1)]
                    if m == 0:
                        dve.wait_ge(a.chunk_free, chunk_free.next())
                    ins = dve.reciprocal(part, part)
                    if m == CB - 1:
                        ins.then_inc(a.inverted, 1)

                def scale(g, c):
                    dve.wait_ge(a.inverted, inverted.next())
                    part = attended[:, g, BANK * c:BANK * (c + 1)]
                    dve.tensor_tensor(part, part, sum_inv[:], ALU.mult).then_inc(a.inverse_ready, 1)

                def turn(g, c):
                    tile = next_tile()[:, 0:BANK].rearrange("p (m h v) -> p m h v", m=CB, h=GROUP)
                    dve.wait_ge(a.tile_done, tile_done.base + tile_done.n - 1)
                    dve.reciprocal(turn_inv[:], tile[:, :, :, HD2:HD2 + 1]).then_inc(a.inverse_ready, 1)
                    dve.wait_ge(a.inverse_ready, inverse_ready.next())
                    out = attn[:, CB * c:CB * (c + 1), P // GROUP * g:P // GROUP * (g + 1)]
                    for m in range(CB):
                        ins = dve.tensor_tensor(out[:, m, :].rearrange("p (h v) -> p h v", h=GROUP), tile[:, m, :, 0:HD2],
                                                turn_inv[:, m, :, :].broadcast_to([P, GROUP, HD2]), ALU.mult)
                    ins.then_inc(a.tile_done, 1)

                inverse_ready = Tally(a.inverse_ready, 3, 2 * GROUPS, 1)
                if a.queries:
                    queries(None)
                    other_latents()
                    queries((a.stack_in[0], 16 * a.q_dmas))
                for heads, qb in max_items():
                    max_scores(heads, qb)
                max_to_rows(None)
                if a.queries:
                    queries((a.stack_in[1], 16 * a.q_dmas))
                tile_ready.start += a.first_tiles
                tile_done.start += a.first_tiles
                high_ready.start += 4 if a.queries else 1

                def slots(i, first, last):
                    for tally in (tile_ready, tile_done, high_ready, inverse_ready, inverted, chunk_free):
                        tally.turn(i, first)
                    if not first:
                        chain.turn(i)
                    for g, kind, what, quad in pass_steps(a, first, last):
                        if kind == "queries":
                            queries((a.stack_in[(g + 2) % RING], 16 * a.q_dmas * (i + (1 if g < 2 else 2))))
                        elif kind == "max":
                            max_scores(*what)
                        elif kind == "max rows":
                            max_to_rows((a.max_in[g], 32 * (i + 1)))
                        elif kind == "inverse":
                            inverse(*what)
                        elif kind == "scale":
                            scale(g % GROUPS, what)
                        elif kind == "turn":
                            turn(g % GROUPS, what)
                        elif kind == "norm" and a.queries:
                            if what == ("stats", 0, 0):
                                dve.wait_ge(a.tile_done, tile_done.here())
                            mid_norm(what, i - 1)
                        elif kind == "norm":
                            post_norm(*what, i - 1)
                        elif kind == "post":
                            post(*what, i - 1)
                        elif kind == "project":
                            tile = next_tile()
                            half, back = what
                            dve.tensor_copy(xn[:, bass.ds((i + back) * SB + CB * half, CB), :],
                                            tile[:, 0:BANK].rearrange("p (n o) -> p n o", o=DIM)).then_inc(a.tile_done, 1)
                    if first and not a.queries:
                        for e in range(EXPERTS):
                            dve.memset(rank[:, :, e], float(EXPERTS - e))
                            dve.memset(first_slot[:, :, e], float(CAPACITY * e - 1))
                        dve.memset(mask[:, SB:, :], 0.0)
                        link(dve.memset(before, 0.0))
                        dve.wait_ge(late_loaded, 64)
                        chain.loop_from_1(POST_MARKS)

                def wide(v):
                    return v.unsqueeze(2).broadcast_to([P, SB, EXPERTS])

                def post_norm(piece, j, _, b):
                    out = h2_rows[:, :, 0:DIM]
                    if piece == "stats" and j == 0:
                        dve.wait_ge(a.tile_done, tile_done.here())
                    if piece == "apply" and j == 0:
                        dve.wait_ge(scattered, 16 * TOPK * SB * b)
                    if piece == "gain":
                        gain_piece(j, out, affine2, h2_ready)
                    else:
                        norm_piece(piece, j, xn[:, bass.ds(b * SB, SB), :], out)

                def routing_step(name, j, b):
                    if name == "gates" and j == 0:
                        dve.wait_ge(exp_out, b + 1)
                        return dve.tensor_reduce(row_value, gates, AX.X, ALU.add)
                    caught()
                    if name == "gates":
                        if j == 1:
                            return dve.reciprocal(row_value, row_value)
                        return dve.tensor_tensor(gates, gates, wide(row_value), ALU.mult)
                    if name == "choose":
                        k, j = j
                        if j == 0:
                            return dve.tensor_reduce(row_value, (gates, r1)[k], AX.X, ALU.max)
                        if j == 1:
                            return dve.tensor_tensor(r2, (gates, r1)[k], wide(row_value), ALU.is_equal)
                        if j == 2:
                            return dve.tensor_tensor(r2, r2, rank, ALU.mult)
                        if j == 3:
                            return dve.tensor_reduce(row_value, r2, AX.X, ALU.max)
                        return dve.tensor_tensor(chosen[k], r2, wide(row_value), ALU.is_equal)
                    if name == "left":
                        if j == 0:
                            return dve.tensor_tensor(r1, gates, chosen[0], ALU.mult)
                        if j == 1:
                            return dve.tensor_tensor(r1, gates, r1, ALU.subtract)
                        return dve.tensor_tensor(r1, r1, chosen[0], ALU.subtract)
                    if name == "number":
                        if j == 0:
                            return dve.tensor_scalar(r2, r1, float(CAPACITY), None, ALU.is_le)
                        return dve.tensor_tensor(r1, r1, first_slot, ALU.add)
                    if name == "place":
                        k = j // 2
                        kept = picked[:, :, 2, :]
                        if j < 2 * TOPK and j % 2 == 0:
                            of = chosen[k].unsqueeze(1).broadcast_to([P, 3, SB, EXPERTS])
                            return dve.tensor_tensor(picks.rearrange("p (v n) e -> p v n e", v=3), of,
                                                     three.rearrange("p (v n) e -> p v n e", v=3), ALU.mult)
                        if j < 2 * TOPK:
                            return dve.tensor_reduce(picked[:, k, :, :], picks.rearrange("p (v n) e -> p v n e", v=3), AX.X, ALU.add)
                        if j == 4:
                            dve.tensor_tensor(gate_of[:, :, bass.ds(b * SB, SB)], picked[:, :, 0, :], kept, ALU.mult)
                            return dve.tensor_tensor(slot_of, picked[:, :, 1, :], kept, ALU.mult)
                        if j == 5:
                            return dve.tensor_scalar(kept, kept, -float(EXPERTS * CAPACITY), float(EXPERTS * CAPACITY),
                                                     ALU.mult, ALU.add)
                        if j == 6:
                            return dve.tensor_tensor(slot_of, slot_of, kept, ALU.add)
                        return dve.tensor_copy(put_at, slot_of)

                def post(name, j, b):
                    if name in POST_TILED:
                        tile = next_tile()
                    if name in ("turn x", "turn h"):
                        dve.tensor_copy(turned, tile).then_inc(a.tile_done, 1)
                    elif name == "project":
                        stream = xn[:, bass.ds(b * SB + CB * j, CB), :]
                        tile = tile[:, BANK * j:BANK * (j + 1)].rearrange("p (n o) -> p n o", o=DIM)
                        dve.tensor_tensor(stream, tile, stream, ALU.add).then_inc(a.tile_done, 1)
                    elif name == "logits":
                        logits = tile[:, 0:SB * EXPERTS].rearrange("p (n e) -> p n e", e=EXPERTS)
                        link(dve.tensor_reduce(row_value, logits, AX.X, ALU.max))
                        dve.tensor_tensor(r0, logits, wide(row_value), ALU.subtract).then_inc(exp_in, 1)
                        dve.wait_ge(exp_in, b + 1)
                        dve.sem_inc(a.tile_done, 1)
                    elif name == "mask":
                        caught()
                        dve.tensor_tensor(mask[:, 0:SB, :], chosen[0], chosen[1], ALU.add).then_inc(mask_ready, 1)
                    elif name == "count":
                        counts = tile[:, 0:(SB + 1) * EXPERTS].rearrange("p (n e) -> p n e", e=EXPERTS)
                        link(dve.tensor_tensor(r1, counts[:, 0:SB, :], before.broadcast_to([P, SB, EXPERTS]), ALU.add))
                        dve.tensor_tensor(before, counts[:, SB:, :], before, ALU.add).then_inc(a.tile_done, 1)
                    elif name == "ids":
                        caught()
                        if j:
                            dve.wait_ge(scattered, 16 * SB * (TOPK * b + j))
                        ins = dve.tensor_scalar(h2_rows[:, :, DIM:DIM + 1], token_no[:].unsqueeze(2), float(TOK * j), None, ALU.add)
                        ins.then_inc(ids_ready, 1)
                        if j == TOPK - 1:
                            mark(dve.tensor_scalar(token_no[:], token_no[:], float(SEQ), None, ALU.add))
                    elif name not in ("exp", "scatter"):
                        mark(routing_step(name, j, b))

                if a.queries:
                    chain.loop_from_1(NORMS_MARKS)
                passes(dve, slots)
                if not a.queries:
                    assert chain.n == POST_MARKS
                    for kind, what in filter(None, post_steps()):
                        if kind == "norm":
                            post_norm(*what, BATCH - 1)
                        else:
                            post(*what, BATCH - 1)

            attention(a1)

            assert chain.n == NORMS_MARKS
            dve.wait_ge(a1.tile_done, 2 + A1_TILES)
            dve.memset(v_tokens[:, :, :, HD2:HD2 + 1], 1.0).then_inc(v_ones, 1)

            def rotate(b):
                dve.wait_ge(qk_drained, 4 * (b + 1))
                halves = [v[:, b % 2].rearrange("p n (s two j) -> p n s two j", two=2, j=HD2 // 2) for v in (qk_raw, qk)]
                first, second = halves[0][:, :, :, 0, :], halves[0][:, :, :, 1, :]
                cos, sin = angles()
                parts = products()
                if b >= 2:
                    dve.wait_ge(mid_ready, mid_at("qk", b - 2, 1) + 1)
                dve.tensor_tensor(parts[0], first, cos, ALU.mult)
                link(dve.tensor_tensor(parts[2], first, sin, ALU.mult))
                dve.wait_ge(rotated, 2 * b + 1)
                dve.tensor_tensor(halves[1][:, :, :, 0, :], parts[0], parts[1], ALU.subtract)
                dve.wait_ge(rotated, 2 * b + 2)
                dve.tensor_tensor(halves[1][:, :, :, 1, :], parts[2], parts[3], ALU.add).then_inc(qk_turned, 1)

            def rest(b):
                if b:
                    dve.wait_ge(qk_stored, 16 * 4 * b)
                for w in range(2):
                    dve.wait_ge(qk_rounded, 2 * b + w + 1)
                    dve.tensor_tensor(qk_low[:, w, :], tile_ps[:, mid_at("qk", b, w) % 2, :],
                                      qk_high[:, w, :].bitcast(F32), ALU.subtract).then_inc(mid_dve, 1)

            for _, what in filter(None, norm_steps()):
                if what == ("apply", 0, 2):
                    dve.wait_ge(mid_loaded, 48)
                    rotate(0)
                mid_norm(what, BATCH - 1)
            for b in range(BATCH):
                if b + 1 < BATCH:
                    rotate(b + 1)
                rest(b)
            dve.memset(k_stack2[:, 0].rearrange("p h q -> p (h q)").bitcast(F32), 1.0).then_inc(first_keys_cleared, 1)
            dve.memset(value_ps[:], 0.0).then_inc(cleared, 1)
            dve.wait_ge(cleared, 1)

            attention(a2)

            dve.wait_ge(b1_ready, 1)
            dve.tensor_copy(b1[:].rearrange("p e f -> p (e f)"), score_ps[:, 0, 0:EXPERTS * HIDDEN // P]).then_inc(b1_turned, 1)

            def expert_turned(e):
                w1_high, w1_low = (w1_parts[:, e % 2, low, :] for low in range(2))
                dve.wait_ge(w_in2[e % 2], 48 * (e // 2 + 1))
                link(dve.tensor_copy(w1_high, w1[:, e % 2, :]))
                dve.tensor_tensor(w1_low, w1[:, e % 2, :], w1_high.bitcast(F32), ALU.subtract)
                dve.wait_ge(e_turned, e + 1)
                high, low = (expert_in_t[:, e % 2, low, :] for low in range(2))
                link(dve.tensor_copy(high, tile_ps[:, 0, :]))
                dve.tensor_tensor(low, tile_ps[:, 0, :], high.bitcast(F32), ALU.subtract).then_inc(e_turned_done, 1)
                number, past = expert_in[:, e % 2, :, DIM], sent_back[:, 0, :]
                link(dve.tensor_scalar(past, number, 0.5, float(2 * TOPK * TOK), ALU.is_lt, ALU.mult))
                link(dve.scalar_tensor_tensor(out=sent_back[:, 1, :], in0=number, scalar=-1.0, in1=past, op0=ALU.add, op1=ALU.add))
                link(dve.tensor_copy(out_at[:, e, :], sent_back[:, 1, :]))

            expert_turned(0)
            for e in range(EXPERTS):
                if e + 1 < EXPERTS:
                    if e:
                        dve.wait_ge(hid_ready, 8 * e)
                    expert_turned(e + 1)
                dve.wait_ge(out_ready, 2 * (e + 1))
                if e >= 2:
                    dve.wait_ge(out_stored[e % 2], 16 * SB * (e // 2))
                dve.wait_ge(w_in2[e % 2], 48 * (e // 2 + 1))
                dve.tensor_tensor(expert_out[:, e % 2, :, :], tile_ps[:, 1, :].rearrange("p (n d) -> p n d", d=DIM),
                                  b2[:, e % 2, :].unsqueeze(1).broadcast_to([P, SB, DIM]), ALU.add).then_inc(out_done, 1)
            for b in range(BATCH):
                dve.wait_ge(fetched_in[b], 32)
                for k in range(TOPK):
                    for n in range(SB * b, SB * (b + 1)):
                        ins = dve.scalar_tensor_tensor(out=xn[:, n, :], in0=fetched[:, k, n, :], scalar=gate_of[:, k, n:n + 1],
                                                       in1=xn[:, n, :], op0=ALU.mult, op1=ALU.add)
                    link(ins)
                part = blocks_of(b)
                for _, (piece, j, _) in filter(None, norm_pieces(0)):
                    if piece == "guess" and j == 1 and b:
                        dve.wait_ge(normed_last, b)
                    if piece != "apply":
                        norm_piece(piece, j, xn[:, part, :], None)
                caught()
                link(dve.tensor_tensor(newton[:], mean_var[:, :, 0], rstd[:], ALU.mult))
                dve.tensor_scalar(shift[:], newton[:], -1.0, None, ALU.mult).then_inc(shift_ready, 1)


def rope_tables():
    import numpy as np

    freq = (1.0 / np.float32(10000.0) ** (np.arange(0, HD2, 2, dtype=np.float32) / np.float32(HD2))).astype(np.float32)
    angle = np.arange(SEQ, dtype=np.float32)[:, None] * freq
    return np.cos(angle).astype(np.float32), np.sin(angle).astype(np.float32)


_INS = {
    "x": "L0_attn_x_bld", "wq": "L0_attn_Wq", "wdown": "L0_attn_Wkv_down", "wk": "L0_attn_Wk_up",
    "wv": "L0_attn_Wv_up", "wout": "L0_attn_Wout", "ln1_g": "L0_ffn_ln1_g", "ln1_b": "L0_ffn_ln1_b",
    "wqkv": "L0_ffn_Wqkv", "wproj": "L0_ffn_Wproj", "ln2_g": "L0_ffn_ln2_g", "ln2_b": "L0_ffn_ln2_b",
    "wgate": "L0_ffn_Wgate", "w1": "L0_ffn_W1", "b1": "L0_ffn_b1", "w2": "L0_ffn_W2", "b2": "L0_ffn_b2",
}


def kernel(**inputs):
    import numpy as np
    import concourse.bacc as bacc
    from concourse.bass_utils import run_bass_kernel_spmd

    nc = bacc.Bacc("TRN2", target_bir_lowering=False, num_devices=1)
    arrays = {f"in_{k}": np.ascontiguousarray(inputs[name]) for k, name in _INS.items()}
    arrays["in_rope_cos"], arrays["in_rope_sin"] = rope_tables()
    t = {k[3:]: nc.dram_tensor(k, a.shape, F32, kind="ExternalInput").ap() for k, a in arrays.items()}
    t["out"] = nc.dram_tensor("out", [BATCH, SEQ, DIM], F32, kind="ExternalOutput").ap()
    build(nc, t)
    got = run_bass_kernel_spmd(nc, [arrays], core_ids=[0])
    return got.results[0]["out"]
```
